# Optimizing a Trainium2 kernel written in Bass

```python
import numpy as np
import jax
import jax.numpy as jnp

def _softmax(x, axis=-1):
    return jax.nn.softmax(x, axis=axis)

def _gelu(x):
    return jax.nn.gelu(x, approximate=True)

def _silu(x):
    return jax.nn.silu(x)

def _sigmoid(x):
    return jax.nn.sigmoid(x)

def _layernorm(x, axis=-1, eps=1e-05):
    m = jnp.mean(x, axis=axis, keepdims=True)
    v = jnp.var(x, axis=axis, keepdims=True)
    return (x - m) / jnp.sqrt(v + eps)

def _scatter_add(tgt, idx, src, axis=0):
    return tgt.at[idx].add(src)

def _segment_sum(src, seg, n):
    return jax.ops.segment_sum(src, seg, n)
kernel_name = 'mk_gps_d2_gnn_r32_3f1f0d'

def setup_inputs(seed: int=0):
    np.random.seed(seed)
    _w = jnp.asarray

    def _rec_inputs():
        import jax
        import jax.numpy as jnp
        _gk = jax.random.key(seed)
        x = -0.0003713 + 1 * jax.random.normal(jax.random.fold_in(_gk, 1), (3125, 256), jnp.float32)
        src = jax.random.randint(jax.random.fold_in(_gk, 2), (50000,), 0, 3125, jnp.int32)
        dst = jnp.minimum((3125 * jax.random.uniform(jax.random.fold_in(_gk, 3), (50000,)) ** 2.0).astype(jnp.int32), 99999)
        _o = jnp.argsort(dst, stable=True)
        src = src[_o]
        dst = dst[_o]
        edge_attr_64 = -9.77346e-05 + 0.999888 * jax.random.normal(jax.random.fold_in(_gk, 12), (50000, 64), jnp.float32)
        edge_weight = jax.random.uniform(jax.random.fold_in(_gk, 13), (50000,), jnp.float32, 0.0, 0.03125)
        return (x, src, dst, edge_attr_64, edge_weight)
    x, src, dst, edge_attr_64, edge_weight = _rec_inputs()

    def _L0_gnn_setup():
        import jax, jax.numpy as jnp
        import numpy as np
        N_NODES = 50000
        key = jax.random.key(seed)
        k1, k2, k3, k4, k5 = jax.random.split(key, 5)
        N, E, F_IN, F_E, F_OUT = (N_NODES, 25000, 256, 64, 256)
        feat = jax.random.normal(k1, (N, F_IN), dtype=jnp.float32)
        edge_feat = jax.random.normal(k2, (E, F_E), dtype=jnp.float32)
        limit = float(np.sqrt(6.0 / (F_IN + F_E + F_OUT)))
        weight = jax.random.uniform(k3, (F_IN + F_E, F_OUT), minval=-limit, maxval=limit, dtype=jnp.float32)
        bias = jnp.zeros((F_OUT,), dtype=jnp.float32)
        src = jax.random.randint(k4, (E,), 0, N, dtype=jnp.int32)
        dst = jax.random.randint(k5, (E,), 0, N, dtype=jnp.int32)
        return {'feat': feat, 'edge_feat': edge_feat, 'weight': weight, 'bias': bias, 'src': src, 'dst': dst}
    _L0_gnn_all = _L0_gnn_setup()
    _L0_gnn_in = {k: v for k, v in _L0_gnn_all.items() if k in ('weight', 'bias')}
    del _L0_gnn_all

    def _L0_mix_setup():
        import jax, jax.numpy as jnp
        import numpy as np
        C_CURV = 1.0
        MIN_NORM = 1e-15
        BALL_EPS = 1e-05
        ATT_EPS = 1e-15
        DIM = 32

        def _norm(x):
            return jnp.clip(jnp.linalg.norm(x, axis=-1, keepdims=True), MIN_NORM)

        def proj(x, c):
            maxnorm = (1.0 - BALL_EPS) / jnp.sqrt(c)
            n = _norm(x)
            return jnp.where(n > maxnorm, x / n * maxnorm, x)

        def expmap0(u, c):
            sc = jnp.sqrt(c)
            n = _norm(u)
            return jnp.tanh(sc * n) * u / (sc * n)

        def logmap0(p, c):
            sc = jnp.sqrt(c)
            n = _norm(p)
            return jnp.arctanh(jnp.clip(sc * n, -1.0 + 1e-07, 1.0 - 1e-07)) * p / (sc * n)

        def mobius_add(x, y, c):
            x2 = jnp.sum(x * x, -1, keepdims=True)
            y2 = jnp.sum(y * y, -1, keepdims=True)
            xy = jnp.sum(x * y, -1, keepdims=True)
            num = (1 + 2 * c * xy + c * y2) * x + (1 - c * x2) * y
            den = 1 + 2 * c * xy + c * c * x2 * y2
            return num / jnp.clip(den, MIN_NORM)

        def conv1d(x, w, pad, groups=1):
            return jax.lax.conv_general_dilated(x, w, (1,), [(pad, pad)], dimension_numbers=('NCH', 'OIH', 'NCH'), feature_group_count=groups)

        def batchnorm(x, gamma, beta):
            mean = jnp.mean(x, axis=(0, 2), keepdims=True)
            var = jnp.var(x, axis=(0, 2), keepdims=True)
            xn = (x - mean) * jax.lax.rsqrt(var + 1e-05)
            return gamma[None, :, None] * xn + beta[None, :, None]

        def _reference_tuple_inner(x, w_qkv, bn_gamma, bn_beta, w_dw, w_pw, w_res, b_res):
            c = C_CURV
            h = logmap0(proj(x, c), c)
            h = jnp.transpose(h, (1, 2, 0))
            h = conv1d(h, w_qkv, pad=2)
            h = batchnorm(h, bn_gamma, bn_beta)
            h = jax.nn.relu(jnp.transpose(h, (2, 0, 1)))
            qkv = proj(expmap0(h, c), c)
            t = jnp.transpose(logmap0(proj(qkv, c), c), (1, 2, 0))
            s = conv1d(t, w_dw, pad=2, groups=t.shape[1])
            s = conv1d(s, w_pw, pad=0, groups=t.shape[1] // DIM)
            cat = jnp.concatenate([t, s], axis=1)
            ai = proj(expmap0(jnp.transpose(cat, (2, 0, 1)), c), c)
            t2 = logmap0(proj(ai, c), c)
            L, N, C2 = t2.shape
            g = C2 // (3 * DIM)
            qkv3 = jnp.transpose(t2, (1, 2, 0)).reshape(N, g, 3 * DIM, L)
            q, k, v = jnp.split(qkv3, 3, axis=2)
            q = jax.nn.relu(q)
            k = jax.nn.relu(k)
            vk = jnp.einsum('ngdl,ngel->ngde', v, k)
            out = jnp.einsum('ngde,ngdl->ngdl', vk, q)
            out = out / (jnp.sum(v, -1, keepdims=True) + ATT_EPS)
            out = jnp.transpose(out.reshape(N, g * DIM, L), (2, 0, 1))
            fx_h = proj(expmap0(out, c), c)
            ft = jnp.transpose(logmap0(proj(fx_h, c), c), (1, 2, 0))
            ft = conv1d(ft, w_res, pad=0) + b_res[None, :, None]
            fx = proj(expmap0(jnp.transpose(ft, (2, 0, 1)), c), c)
            residual = mobius_add(fx, x, c)
            return (fx, residual)
        key = jax.random.key(seed)
        ks = jax.random.split(key, 6)
        L, N, C, TD = (64, 16, 256, 256)
        x = jax.random.normal(ks[0], (L, N, C), jnp.float32) * 0.05
        w_qkv = jax.random.normal(ks[1], (3 * TD, C, 5), jnp.float32) / np.sqrt(C * 5)
        bn_gamma = jnp.ones((3 * TD,), jnp.float32)
        bn_beta = jnp.zeros((3 * TD,), jnp.float32)
        w_dw = jax.random.normal(ks[2], (3 * TD, 1, 5), jnp.float32) / np.sqrt(5.0)
        w_pw = jax.random.normal(ks[3], (3 * TD, DIM, 1), jnp.float32) / np.sqrt(DIM)
        w_res = jax.random.normal(ks[4], (C, 2 * TD, 1), jnp.float32) / np.sqrt(2 * TD)
        b_res = jnp.zeros((C,), jnp.float32)
        return {'x': x, 'w_qkv': w_qkv, 'bn_gamma': bn_gamma, 'bn_beta': bn_beta, 'w_dw': w_dw, 'w_pw': w_pw, 'w_res': w_res, 'b_res': b_res}
    _L0_mix_all = _L0_mix_setup()
    _L0_mix_in = {k: v for k, v in _L0_mix_all.items() if k in ('w_qkv', 'bn_gamma', 'bn_beta', 'w_dw', 'w_pw', 'w_res', 'b_res')}
    del _L0_mix_all

    def _L0_ffn_setup():
        import jax, jax.numpy as jnp
        import numpy as np
        N_EXPERTS = 8
        TOP_K = 2
        key = jax.random.key(seed)
        ks = jax.random.split(key, 5)
        B, T, C, E, H = (8, 64, 256, 8, 682)
        scale = 1.0 / np.sqrt(C)
        return {'x': jax.random.normal(ks[0], (B, T, C), dtype=jnp.float32), 'router_w': jax.random.normal(ks[1], (E, C), dtype=jnp.float32) * scale, 'w1': jax.random.normal(ks[2], (E, H, C), dtype=jnp.float32) * scale, 'w2': jax.random.normal(ks[3], (E, C, H), dtype=jnp.float32) * (1.0 / np.sqrt(H)), 'w3': jax.random.normal(ks[4], (E, H, C), dtype=jnp.float32) * scale}
    _L0_ffn_all = _L0_ffn_setup()
    _L0_ffn_in = {k: v for k, v in _L0_ffn_all.items() if k in ('router_w', 'w1', 'w2', 'w3')}
    del _L0_ffn_all

    def _L1_gnn_setup():
        import jax, jax.numpy as jnp
        import numpy as np
        N_NODES = 3125
        N_EDGES = 100000
        DIM = 256
        LEAKY_SLOPE = 0.2
        EPS = 1e-12
        key = jax.random.key(seed)
        ks = jax.random.split(key, 8)
        embeddings = jax.random.normal(ks[0], (N_NODES, DIM), dtype=jnp.float32)
        edge_src = jax.random.randint(ks[1], (N_EDGES,), 0, N_NODES, dtype=jnp.int32)
        edge_dst = jax.random.randint(ks[2], (N_EDGES,), 0, N_NODES, dtype=jnp.int32)
        edge_val = jax.random.uniform(ks[3], (N_EDGES,), dtype=jnp.float32) / 32.0
        scale = 1.0 / np.sqrt(DIM)
        W1 = jax.random.normal(ks[4], (DIM, DIM), dtype=jnp.float32) * scale
        b1 = jax.random.normal(ks[5], (DIM,), dtype=jnp.float32) * 0.01
        W2 = jax.random.normal(ks[6], (DIM, DIM), dtype=jnp.float32) * scale
        b2 = jax.random.normal(ks[7], (DIM,), dtype=jnp.float32) * 0.01
        return {'embeddings': embeddings, 'edge_src': edge_src, 'edge_dst': edge_dst, 'edge_val': edge_val, 'W1': W1, 'b1': b1, 'W2': W2, 'b2': b2}
    _L1_gnn_all = _L1_gnn_setup()
    _L1_gnn_in = {k: v for k, v in _L1_gnn_all.items() if k in ('W1', 'b1', 'W2', 'b2')}
    del _L1_gnn_all

    def _L1_mix_setup():
        import jax, jax.numpy as jnp
        import numpy as np
        D_MODEL = 256
        NHEAD = 8
        D_HEAD = D_MODEL // NHEAD
        DIM_FF = 1024
        B, L = (4, 512)
        LN_EPS = 1e-05

        def _layernorm(x, g, b):
            mu = jnp.mean(x, axis=-1, keepdims=True)
            var = jnp.mean((x - mu) ** 2, axis=-1, keepdims=True)
            return (x - mu) * jax.lax.rsqrt(var + LN_EPS) * g + b

        def _phi(x):
            return jnp.where(x > 0, x + 1.0, jnp.exp(x))
        key = jax.random.key(seed)
        ks = jax.random.split(key, 16)
        s_in = 1.0 / np.sqrt(D_MODEL)
        s_ff = 1.0 / np.sqrt(DIM_FF)
        inp = {'x': jax.random.normal(ks[0], (B, L, D_MODEL), dtype=jnp.float32), 'Wq': jax.random.normal(ks[1], (D_MODEL, D_MODEL), dtype=jnp.float32) * s_in, 'bq': jnp.zeros((D_MODEL,), jnp.float32), 'Wk': jax.random.normal(ks[2], (D_MODEL, D_MODEL), dtype=jnp.float32) * s_in, 'bk': jnp.zeros((D_MODEL,), jnp.float32), 'Wv': jax.random.normal(ks[3], (D_MODEL, D_MODEL), dtype=jnp.float32) * s_in, 'bv': jnp.zeros((D_MODEL,), jnp.float32), 'Wo': jax.random.normal(ks[4], (D_MODEL, D_MODEL), dtype=jnp.float32) * s_in, 'bo': jnp.zeros((D_MODEL,), jnp.float32), 'W1': jax.random.normal(ks[5], (D_MODEL, DIM_FF), dtype=jnp.float32) * s_in, 'b1': jnp.zeros((DIM_FF,), jnp.float32), 'W2': jax.random.normal(ks[6], (DIM_FF, D_MODEL), dtype=jnp.float32) * s_ff, 'b2': jnp.zeros((D_MODEL,), jnp.float32), 'ln1_g': jnp.ones((D_MODEL,), jnp.float32), 'ln1_b': jnp.zeros((D_MODEL,), jnp.float32), 'ln2_g': jnp.ones((D_MODEL,), jnp.float32), 'ln2_b': jnp.zeros((D_MODEL,), jnp.float32)}
        return inp
    _L1_mix_all = _L1_mix_setup()
    _L1_mix_in = {k: v for k, v in _L1_mix_all.items() if k in ('Wq', 'bq', 'Wk', 'bk', 'Wv', 'bv', 'Wo', 'bo', 'W1', 'b1', 'W2', 'b2', 'ln1_g', 'ln1_b', 'ln2_g', 'ln2_b')}
    del _L1_mix_all

    def _L1_ffn_setup():
        import jax, jax.numpy as jnp
        import numpy as np
        B, S, H, F, E, K = (8, 128, 256, 512, 16, 2)
        EPS = 1e-05
        key = jax.random.key(seed)
        ks = jax.random.split(key, 9)
        sc = 0.02
        return {'x': jax.random.normal(ks[0], (B, S, H), dtype=jnp.float32), 'gate_w': jax.random.normal(ks[1], (H, E), dtype=jnp.float32) * sc, 'gate_b': jnp.zeros((E,), dtype=jnp.float32), 'w1': jax.random.normal(ks[2], (E, H, F), dtype=jnp.float32) * sc, 'b1': jnp.zeros((E, F), dtype=jnp.float32), 'w2': jax.random.normal(ks[3], (E, F, H), dtype=jnp.float32) * sc, 'b2': jnp.zeros((E, H), dtype=jnp.float32), 'gamma': jnp.ones((H,), dtype=jnp.float32), 'beta': jnp.zeros((H,), dtype=jnp.float32)}
    _L1_ffn_all = _L1_ffn_setup()
    _L1_ffn_in = {k: v for k, v in _L1_ffn_all.items() if k in ('gate_w', 'gate_b', 'w1', 'b1', 'w2', 'b2', 'gamma', 'beta')}
    del _L1_ffn_all
    return {'x': x, 'src': src, 'dst': dst, 'edge_attr_64': edge_attr_64, 'edge_weight': edge_weight, 'L0_gnn_weight': _L0_gnn_in['weight'], 'L0_gnn_bias': _L0_gnn_in['bias'], 'L0_mix_w_qkv': _L0_mix_in['w_qkv'], 'L0_mix_bn_gamma': _L0_mix_in['bn_gamma'], 'L0_mix_bn_beta': _L0_mix_in['bn_beta'], 'L0_mix_w_dw': _L0_mix_in['w_dw'], 'L0_mix_w_pw': _L0_mix_in['w_pw'], 'L0_mix_w_res': _L0_mix_in['w_res'], 'L0_mix_b_res': _L0_mix_in['b_res'], 'L0_ffn_router_w': _L0_ffn_in['router_w'], 'L0_ffn_w1': _L0_ffn_in['w1'], 'L0_ffn_w2': _L0_ffn_in['w2'], 'L0_ffn_w3': _L0_ffn_in['w3'], 'L1_gnn_W1': _L1_gnn_in['W1'], 'L1_gnn_b1': _L1_gnn_in['b1'], 'L1_gnn_W2': _L1_gnn_in['W2'], 'L1_gnn_b2': _L1_gnn_in['b2'], 'L1_mix_Wq': _L1_mix_in['Wq'], 'L1_mix_bq': _L1_mix_in['bq'], 'L1_mix_Wk': _L1_mix_in['Wk'], 'L1_mix_bk': _L1_mix_in['bk'], 'L1_mix_Wv': _L1_mix_in['Wv'], 'L1_mix_bv': _L1_mix_in['bv'], 'L1_mix_Wo': _L1_mix_in['Wo'], 'L1_mix_bo': _L1_mix_in['bo'], 'L1_mix_W1': _L1_mix_in['W1'], 'L1_mix_b1': _L1_mix_in['b1'], 'L1_mix_W2': _L1_mix_in['W2'], 'L1_mix_b2': _L1_mix_in['b2'], 'L1_mix_ln1_g': _L1_mix_in['ln1_g'], 'L1_mix_ln1_b': _L1_mix_in['ln1_b'], 'L1_mix_ln2_g': _L1_mix_in['ln2_g'], 'L1_mix_ln2_b': _L1_mix_in['ln2_b'], 'L1_ffn_gate_w': _L1_ffn_in['gate_w'], 'L1_ffn_gate_b': _L1_ffn_in['gate_b'], 'L1_ffn_w1': _L1_ffn_in['w1'], 'L1_ffn_b1': _L1_ffn_in['b1'], 'L1_ffn_w2': _L1_ffn_in['w2'], 'L1_ffn_b2': _L1_ffn_in['b2'], 'L1_ffn_gamma': _L1_ffn_in['gamma'], 'L1_ffn_beta': _L1_ffn_in['beta']}

def reference(x, src, dst, edge_attr_64, edge_weight, L0_gnn_weight, L0_gnn_bias, L0_mix_w_qkv, L0_mix_bn_gamma, L0_mix_bn_beta, L0_mix_w_dw, L0_mix_w_pw, L0_mix_w_res, L0_mix_b_res, L0_ffn_router_w, L0_ffn_w1, L0_ffn_w2, L0_ffn_w3, L1_gnn_W1, L1_gnn_b1, L1_gnn_W2, L1_gnn_b2, L1_mix_Wq, L1_mix_bq, L1_mix_Wk, L1_mix_bk, L1_mix_Wv, L1_mix_bv, L1_mix_Wo, L1_mix_bo, L1_mix_W1, L1_mix_b1, L1_mix_W2, L1_mix_b2, L1_mix_ln1_g, L1_mix_ln1_b, L1_mix_ln2_g, L1_mix_ln2_b, L1_ffn_gate_w, L1_ffn_gate_b, L1_ffn_w1, L1_ffn_b1, L1_ffn_w2, L1_ffn_b2, L1_ffn_gamma, L1_ffn_beta):
    import jax
    import jax.numpy as jnp

    def _L0_gnn_ref(feat, edge_feat, weight, bias, src, dst):
        import jax, jax.numpy as jnp
        import numpy as np
        N_NODES = 50000
        N, F_IN = feat.shape
        ones = jnp.ones(src.shape[0], dtype=jnp.float32)
        out_deg = jax.ops.segment_sum(ones, src, num_segments=N)
        norm_out = jnp.maximum(out_deg, 1.0) ** (-0.5)
        feat_n = feat * norm_out[:, None]
        agg_h = jax.ops.segment_sum(feat_n[src], dst, num_segments=N)
        agg_e = jax.ops.segment_sum(edge_feat, dst, num_segments=N)
        rst = jnp.concatenate([agg_h, agg_e], axis=1) @ weight
        in_deg = jax.ops.segment_sum(ones, dst, num_segments=N)
        norm_in = jnp.maximum(in_deg, 1.0) ** (-0.5)
        rst = rst * norm_in[:, None] + bias
        return jax.nn.relu(rst)

    def _L0_mix_ref(x, w_qkv, bn_gamma, bn_beta, w_dw, w_pw, w_res, b_res):
        import jax, jax.numpy as jnp
        import numpy as np
        C_CURV = 1.0
        MIN_NORM = 1e-15
        BALL_EPS = 1e-05
        ATT_EPS = 1e-15
        DIM = 32

        def _norm(x):
            return jnp.clip(jnp.linalg.norm(x, axis=-1, keepdims=True), MIN_NORM)

        def proj(x, c):
            maxnorm = (1.0 - BALL_EPS) / jnp.sqrt(c)
            n = _norm(x)
            return jnp.where(n > maxnorm, x / n * maxnorm, x)

        def expmap0(u, c):
            sc = jnp.sqrt(c)
            n = _norm(u)
            return jnp.tanh(sc * n) * u / (sc * n)

        def logmap0(p, c):
            sc = jnp.sqrt(c)
            n = _norm(p)
            return jnp.arctanh(jnp.clip(sc * n, -1.0 + 1e-07, 1.0 - 1e-07)) * p / (sc * n)

        def mobius_add(x, y, c):
            x2 = jnp.sum(x * x, -1, keepdims=True)
            y2 = jnp.sum(y * y, -1, keepdims=True)
            xy = jnp.sum(x * y, -1, keepdims=True)
            num = (1 + 2 * c * xy + c * y2) * x + (1 - c * x2) * y
            den = 1 + 2 * c * xy + c * c * x2 * y2
            return num / jnp.clip(den, MIN_NORM)

        def conv1d(x, w, pad, groups=1):
            return jax.lax.conv_general_dilated(x, w, (1,), [(pad, pad)], dimension_numbers=('NCH', 'OIH', 'NCH'), feature_group_count=groups)

        def batchnorm(x, gamma, beta):
            mean = jnp.mean(x, axis=(0, 2), keepdims=True)
            var = jnp.var(x, axis=(0, 2), keepdims=True)
            xn = (x - mean) * jax.lax.rsqrt(var + 1e-05)
            return gamma[None, :, None] * xn + beta[None, :, None]

        def _reference_tuple_inner(x, w_qkv, bn_gamma, bn_beta, w_dw, w_pw, w_res, b_res):
            c = C_CURV
            h = logmap0(proj(x, c), c)
            h = jnp.transpose(h, (1, 2, 0))
            h = conv1d(h, w_qkv, pad=2)
            h = batchnorm(h, bn_gamma, bn_beta)
            h = jax.nn.relu(jnp.transpose(h, (2, 0, 1)))
            qkv = proj(expmap0(h, c), c)
            t = jnp.transpose(logmap0(proj(qkv, c), c), (1, 2, 0))
            s = conv1d(t, w_dw, pad=2, groups=t.shape[1])
            s = conv1d(s, w_pw, pad=0, groups=t.shape[1] // DIM)
            cat = jnp.concatenate([t, s], axis=1)
            ai = proj(expmap0(jnp.transpose(cat, (2, 0, 1)), c), c)
            t2 = logmap0(proj(ai, c), c)
            L, N, C2 = t2.shape
            g = C2 // (3 * DIM)
            qkv3 = jnp.transpose(t2, (1, 2, 0)).reshape(N, g, 3 * DIM, L)
            q, k, v = jnp.split(qkv3, 3, axis=2)
            q = jax.nn.relu(q)
            k = jax.nn.relu(k)
            vk = jnp.einsum('ngdl,ngel->ngde', v, k)
            out = jnp.einsum('ngde,ngdl->ngdl', vk, q)
            out = out / (jnp.sum(v, -1, keepdims=True) + ATT_EPS)
            out = jnp.transpose(out.reshape(N, g * DIM, L), (2, 0, 1))
            fx_h = proj(expmap0(out, c), c)
            ft = jnp.transpose(logmap0(proj(fx_h, c), c), (1, 2, 0))
            ft = conv1d(ft, w_res, pad=0) + b_res[None, :, None]
            fx = proj(expmap0(jnp.transpose(ft, (2, 0, 1)), c), c)
            residual = mobius_add(fx, x, c)
            return (fx, residual)
        return _reference_tuple_inner(x, w_qkv, bn_gamma, bn_beta, w_dw, w_pw, w_res, b_res)[0]

    def _L0_ffn_ref(x, router_w, w1, w2, w3):
        import jax, jax.numpy as jnp
        import numpy as np
        N_EXPERTS = 8
        TOP_K = 2
        B, T, C = x.shape
        flat = x.reshape(-1, C)
        logits = flat @ router_w.T
        probs = jax.nn.softmax(logits, axis=-1)
        topk_probs, topk_idx = jax.lax.top_k(probs, TOP_K)
        topk_probs = topk_probs / (jnp.sum(topk_probs, axis=-1, keepdims=True) + 1e-09)
        onehot = jax.nn.one_hot(topk_idx, N_EXPERTS, dtype=flat.dtype)
        gates = jnp.einsum('nk,nke->ne', topk_probs, onehot)
        h1 = jnp.einsum('nc,ehc->neh', flat, w1)
        h3 = jnp.einsum('nc,ehc->neh', flat, w3)
        h = jax.nn.silu(h1) * h3
        y = jnp.einsum('neh,ech->nec', h, w2)
        out = jnp.einsum('ne,nec->nc', gates, y)
        return out.reshape(B, T, C)

    def _L1_gnn_ref(embeddings, edge_src, edge_dst, edge_val, W1, b1, W2, b2):
        import jax, jax.numpy as jnp
        import numpy as np
        N_NODES = 3125
        N_EDGES = 100000
        DIM = 256
        LEAKY_SLOPE = 0.2
        EPS = 1e-12
        ego_emb = embeddings @ W1.T + b1
        messages = edge_val[:, None] * embeddings[edge_src]
        neighbor_emb = jax.ops.segment_sum(messages, edge_dst, num_segments=embeddings.shape[0])
        interaction_emb = neighbor_emb * embeddings
        side_emb = (neighbor_emb + interaction_emb) @ W2.T + b2
        out = ego_emb + side_emb
        out = jnp.where(out >= 0, out, LEAKY_SLOPE * out)
        norm = jnp.sqrt(jnp.sum(out * out, axis=1, keepdims=True))
        return out / jnp.maximum(norm, EPS)

    def _L1_mix_ref(x, Wq, bq, Wk, bk, Wv, bv, Wo, bo, W1, b1, W2, b2, ln1_g, ln1_b, ln2_g, ln2_b):
        import jax, jax.numpy as jnp
        import numpy as np
        D_MODEL = 256
        NHEAD = 8
        D_HEAD = D_MODEL // NHEAD
        DIM_FF = 1024
        B, L = (4, 512)
        LN_EPS = 1e-05

        def _layernorm(x, g, b):
            mu = jnp.mean(x, axis=-1, keepdims=True)
            var = jnp.mean((x - mu) ** 2, axis=-1, keepdims=True)
            return (x - mu) * jax.lax.rsqrt(var + LN_EPS) * g + b

        def _phi(x):
            return jnp.where(x > 0, x + 1.0, jnp.exp(x))
        Bq, Lq, _ = x.shape
        q = (x @ Wq + bq).reshape(Bq, Lq, NHEAD, D_HEAD)
        k = (x @ Wk + bk).reshape(Bq, Lq, NHEAD, D_HEAD)
        v = (x @ Wv + bv).reshape(Bq, Lq, NHEAD, D_HEAD)
        q_phi = _phi(q)
        k_phi = _phi(k)
        kv = jnp.einsum('blhd,blhe->bhde', k_phi, v)
        k_sum = k_phi.sum(axis=1)
        z = 1.0 / (jnp.einsum('blhd,bhd->blh', q_phi, k_sum) + 1e-06)
        out = jnp.einsum('blhd,bhde,blh->blhe', q_phi, kv, z)
        out = out.reshape(Bq, Lq, D_MODEL) @ Wo + bo
        x = _layernorm(x + out, ln1_g, ln1_b)
        ff = jax.nn.relu(x @ W1 + b1) @ W2 + b2
        x = _layernorm(x + ff, ln2_g, ln2_b)
        return x

    def _L1_ffn_ref(x, gate_w, gate_b, w1, b1, w2, b2, gamma, beta):
        import jax, jax.numpy as jnp
        import numpy as np
        B, S, H, F, E, K = (8, 128, 256, 512, 16, 2)
        EPS = 1e-05
        gate_logits = x @ gate_w + gate_b
        topk_vals, topk_idx = jax.lax.top_k(gate_logits, K)
        topk_w = jax.nn.softmax(topk_vals, axis=-1)
        h = jax.nn.relu(jnp.einsum('bsh,ehf->bsef', x, w1) + b1)
        expert_out = jnp.einsum('bsef,efh->bseh', h, w2) + b2
        sel = jnp.take_along_axis(expert_out, topk_idx[:, :, :, None], axis=2)
        moe = jnp.sum(topk_w[..., None] * sel, axis=2)
        y = x + moe
        mu = jnp.mean(y, axis=-1, keepdims=True)
        var = jnp.var(y, axis=-1, keepdims=True)
        return (y - mu) / jnp.sqrt(var + EPS) * gamma + beta
    xn = _layernorm(x, axis=-1)
    x = x + _L0_gnn_ref(xn, edge_attr_64, L0_gnn_weight, L0_gnn_bias, src, dst) + _L0_mix_ref(xn[None], L0_mix_w_qkv, L0_mix_bn_gamma, L0_mix_bn_beta, L0_mix_w_dw, L0_mix_w_pw, L0_mix_w_res, L0_mix_b_res)[0]
    x = x + _L0_ffn_ref(_layernorm(x, axis=-1)[None], L0_ffn_router_w, L0_ffn_w1, L0_ffn_w2, L0_ffn_w3)[0]
    xn = _layernorm(x, axis=-1)
    x = x + _L1_gnn_ref(xn, src, dst, edge_weight, L1_gnn_W1, L1_gnn_b1, L1_gnn_W2, L1_gnn_b2) + _L1_mix_ref(xn[None], L1_mix_Wq, L1_mix_bq, L1_mix_Wk, L1_mix_bk, L1_mix_Wv, L1_mix_bv, L1_mix_Wo, L1_mix_bo, L1_mix_W1, L1_mix_b1, L1_mix_W2, L1_mix_b2, L1_mix_ln1_g, L1_mix_ln1_b, L1_mix_ln2_g, L1_mix_ln2_b)[0]
    x = x + _L1_ffn_ref(_layernorm(x, axis=-1)[None], L1_ffn_gate_w, L1_ffn_gate_b, L1_ffn_w1, L1_ffn_b1, L1_ffn_w2, L1_ffn_b2, L1_ffn_gamma, L1_ffn_beta)[0]
    return x

_drawn_inputs = setup_inputs


def setup_inputs(seed=0):
    import zlib

    import numpy as np

    out = dict(_drawn_inputs(seed))
    spreads = {'L0_gnn_bias': (0.0, 0.1),
     'L0_mix_bn_gamma': (1.0, 0.2),
     'L0_mix_bn_beta': (0.0, 0.1),
     'L0_mix_b_res': (0.0, 0.1),
     'L1_mix_bq': (0.0, 0.8),
     'L1_mix_bk': (0.0, 0.8),
     'L1_mix_bv': (0.0, 0.1),
     'L1_mix_bo': (0.0, 0.1),
     'L1_mix_b1': (0.0, 0.279),
     'L1_mix_b2': (0.0, 0.1),
     'L1_mix_ln1_g': (1.0, 0.2),
     'L1_mix_ln1_b': (0.0, 0.1),
     'L1_mix_ln2_g': (1.0, 0.2),
     'L1_mix_ln2_b': (0.0, 0.1),
     'L1_ffn_gate_b': (0.0, 0.393),
     'L1_ffn_b1': (0.0, 0.8),
     'L1_ffn_b2': (0.0, 0.334),
     'L1_ffn_gamma': (1.0, 0.2),
     'L1_ffn_beta': (0.0, 0.1)}
    factors = {'edge_weight': 8.0,
     'L1_gnn_b1': 8.0,
     'L1_gnn_W2': 8.0,
     'L1_gnn_b2': 8.0,
     'L1_mix_Wq': 8.0,
     'L1_mix_Wk': 8.0,
     'L1_ffn_w1': 2.774}
    for name, (base, spread) in spreads.items():
        noise = np.random.default_rng([zlib.crc32(name.encode()), seed]).standard_normal(out[name].shape)
        drawn = base * np.exp(spread * noise) if base else spread * noise
        out[name] = jnp.asarray(drawn.astype(out[name].dtype))
    for name, factor in factors.items():
        out[name] = (out[name] * factor).astype(out[name].dtype)
    return out
```

```python
import math
from contextlib import ExitStack

import concourse.bass as bass
from concourse import mybir

F32 = mybir.dt.float32
I32 = mybir.dt.int32
BF16 = mybir.dt.bfloat16
ALU = mybir.AluOpType
ACT = mybir.ActivationFunctionType
AX_X = mybir.AxisListType.X

P = 128
N = 3125
D = 256
DE = 64
E = 50000
NT = -(-N // P)
NTAIL = N - (NT - 1) * P
NPAD = NT * P
ET = -(-E // P)
EPAD = ET * P
ECH = -(-ET // P)
SL = 8
SP = 4
PAIRS = -(-(ET + NT - 1) // SL) * SL
HB = 17
C0 = 768
CH0 = C0 // P
GRP = 16
GT = 5
NG = NT // GT
GN = GT * P
GH = GN // 2
FF = 1024
HEADS = 8
assert ET % HB == 0 and NT % GT == 0 and PAIRS // SL % 2 == 0
MAXNORM = 0.9999899864196777
ATANH_MAXNORM = 0.5 * math.log((1 + MAXNORM) / (1 - MAXNORM))
MINNORM = 1e-15


class Chain:

    def __init__(self, eng, sem, base=0):
        self.eng, self.sem, self.base, self.n = eng, sem, base, 0

    def did(self, ins):
        ins.then_inc(self.sem, 1)
        self.n += 1

    def settle(self):
        self.eng.wait_ge(self.sem, self.base + self.n)

    def step(self, ins):
        self.did(ins)
        self.settle()


class Memory:

    def __init__(self, nc, ctx, tag):
        self.nc, self.ctx, self.tag, self.sems = nc, ctx, tag, []

    def sb(self, name, shape, dt=F32):
        return self.ctx.enter_context(self.nc.sbuf_tensor(f"{self.tag}_{name}", shape, dt))

    def ps(self, name, shape, dt=F32):
        return self.ctx.enter_context(self.nc.psum_tensor(f"{self.tag}_{name}", shape, dt))

    def sem(self, name):
        if not self.sems:
            self.ctx.callback(self.release)
        self.sems.append(self.nc.alloc_semaphore(f"{self.tag}_{name}"))
        return self.sems[-1]

    def release(self):
        self.nc.clear_and_free_semaphores(self.sems)
        self.nc.all_engine_barrier(sem_only=True)


def row(v):
    return v.rearrange("(a n) -> a n", a=1).to_broadcast([P, v.shape[0]])


def at(buf, start, size):
    return buf[:, bass.ds(start, size)]


def refine(c, r, x, tmp):
    dve = c.eng
    c.step(dve.tensor_tensor(tmp[:, :], r[:, :], r[:, :], ALU.mult))
    c.step(dve.tensor_tensor(tmp[:, :], tmp[:, :], x[:, :], ALU.mult))
    c.step(dve.tensor_scalar(tmp[:, :], tmp[:, :], -0.5, 1.5, ALU.mult, ALU.add))
    c.step(dve.tensor_tensor(r[:, :], r[:, :], tmp[:, :], ALU.mult))


class Constants:

    def __init__(self, nc, ctx):
        m = Memory(nc, ctx, "const")
        self.ident = m.sb("ident", [P, P])
        self.before = m.sb("before", [P, P])
        self.ones = m.sb("ones", [P, P])
        self.valid = m.sb("valid", [P, NT])
        self.part = m.sb("part", [P, 1])
        built = m.sem("built")
        with nc.Block() as block:

            @block.gpsimd
            def _(pool):
                pool.memset(self.ident[:, :], 0.0).then_inc(built, 1)
                pool.memset(self.before[:, :], 0.0).then_inc(built, 1)
                pool.memset(self.ones[:, :], 1.0).then_inc(built, 1)
                pool.memset(self.valid[:, :], 1.0).then_inc(built, 1)
                pool.iota(self.part[:, :], pattern=[[0, 1]], base=0, channel_multiplier=1,
                          allow_small_or_imprecise_dtypes=True).then_inc(built, 1)
                pool.wait_ge(built, 5)
                pool.affine_select(out=self.ident[:, :], in_=self.ident[:, :], compare_op=ALU.not_equal, fill=1.0,
                                   base=0, pattern=[[-1, P]], channel_multiplier=1).then_inc(built, 1)
                pool.affine_select(out=self.before[:, :], in_=self.before[:, :], compare_op=ALU.is_ge, fill=1.0,
                                   base=0, pattern=[[-1, P]], channel_multiplier=1).then_inc(built, 1)
                pool.affine_select(out=self.valid[:, :], in_=self.valid[:, :], compare_op=ALU.is_ge, fill=0.0,
                                   base=N - 1, pattern=[[-P, NT]], channel_multiplier=-1).then_inc(built, 1)
                pool.wait_ge(built, 8)


def load_nodes(nc, x, X):
    with ExitStack() as ctx:
        m = Memory(nc, ctx, "load")
        loaded, cleared = m.sem("loaded"), m.sem("cleared")
        block = ctx.enter_context(nc.Block())
        full = (NT - 1) * P

        @block.vector
        def _(dve):
            dve.memset(X[:, (NT - 1) * D:NT * D], 0.0).then_inc(cleared, 1)

        @block.sync
        def _(sp):
            sp.dma_start(X[:, 0:(NT - 1) * D].rearrange("p (i d) -> p i d", d=D),
                         x[0:full, :].rearrange("(i p) d -> p i d", p=P)).then_inc(loaded, 16)
            sp.wait_ge(cleared, 1)
            sp.dma_start(X[0:NTAIL, (NT - 1) * D:NT * D], x[full:N, :]).then_inc(loaded, 16)
            sp.wait_ge(loaded, 32)


def layer_norm(nc, tag, src, dst, gamma=None, beta=None, add=None, table=None, scale=None, sumsq=None, eps=1e-5):
    with ExitStack() as ctx:
        m = Memory(nc, ctx, tag)
        stats = m.sb("stats", [P, NT * 6])
        mean, var, tmp, rstd = (m.sb(n, [P, NT]) for n in ("mean", "var", "tmp", "rstd"))
        row_out = m.sb("row_out", [P, 2 * D])
        square = m.sb("square", [P, D])
        chain, var_ready, root_ready = m.sem("chain"), m.sem("var_ready"), m.sem("root_ready")
        tile_ready, rows_ready = m.sem("tile_ready"), m.sem("rows_ready")
        row_stored = [m.sem(f"row_stored{k}") for k in range(2)]
        squared = m.sem("squared")
        if gamma is not None:
            gamma_row, beta_row = m.sb("gamma_row", [P, D]), m.sb("beta_row", [P, D])
            affine_loaded = m.sem("affine_loaded")
        block = ctx.enter_context(nc.Block())
        st = stats[:, :].rearrange("p (i s) -> p i s", s=6)

        @block.vector
        def _(dve):
            c = Chain(dve, chain)
            with dve.Fori(0, NT) as i:
                dve.bn_stats(at(stats, i * 6, 6), at(src, i * D, D)).then_inc(chain, 1)
            c.n = NT
            c.settle()
            c.did(dve.tensor_tensor(mean[:, :], st[:, :, 1], st[:, :, 4], ALU.add))
            c.did(dve.tensor_tensor(var[:, :], st[:, :, 2], st[:, :, 5], ALU.add))
            c.step(dve.tensor_tensor(tmp[:, :], st[:, :, 1], st[:, :, 4], ALU.subtract))
            c.did(dve.tensor_scalar(mean[:, :], mean[:, :], 0.5, None, ALU.mult))
            c.step(dve.scalar_tensor_tensor(out=tmp[:, :], in0=tmp[:, :], scalar=0.25, in1=tmp[:, :],
                                            op0=ALU.mult, op1=ALU.mult))
            c.step(dve.scalar_tensor_tensor(out=var[:, :], in0=var[:, :], scalar=1.0 / D, in1=tmp[:, :],
                                            op0=ALU.mult, op1=ALU.add))
            dve.tensor_scalar(var[:, :], var[:, :], eps, None, ALU.add).then_inc(var_ready, 1)
            dve.wait_ge(root_ready, 1)
            c.step(dve.reciprocal(rstd[:, :], tmp[:, :]))
            refine(c, rstd, var, tmp)
            if gamma is not None:
                dve.wait_ge(affine_loaded, 32)
            with dve.Fori(0, NT) as i:
                per = (1 if gamma is None else 3) + (0 if add is None else 1)
                t = Chain(dve, chain, i * per + c.n)
                x = at(src, i * D, D)
                y = x if add is not None else at(dst, i * D, D)
                ins = dve.tensor_scalar(y, x, at(mean, i, 1), at(rstd, i, 1), ALU.subtract, ALU.mult)
                if gamma is not None:
                    t.step(ins)
                    t.step(dve.tensor_tensor(y, y, gamma_row[:, :], ALU.mult))
                    ins = dve.tensor_tensor(y, y, beta_row[:, :], ALU.add)
                if add is not None:
                    t.step(ins)
                    ins = dve.tensor_tensor(at(dst, i * D, D), at(add, i * D, D), y, ALU.add)
                t.did(ins)
                assert t.n == per
                if table is not None or sumsq is not None:
                    t.settle()
                    dve.sem_inc(tile_ready, 1)

        @block.scalar
        def _(act):
            if gamma is not None:
                act.dma_start(gamma_row[:, :], row(gamma)).then_inc(affine_loaded, 16)
                act.dma_start(beta_row[:, :], row(beta)).then_inc(affine_loaded, 16)
            act.wait_ge(var_ready, 1)
            act.activation(tmp[:, :], var[:, :], ACT.Sqrt).then_inc(root_ready, 1)
            if sumsq is not None:
                with act.Fori(0, NT) as i:
                    act.wait_ge(tile_ready, i + 1)
                    act.wait_ge(squared, i)
                    act.activation(square[:, :], at(dst, i * D, D), ACT.Square,
                                   accum_out=at(sumsq, i, 1)).then_inc(squared, 1)
            if table is not None:
                def put(i, k, turn):
                    act.wait_ge(tile_ready, i + 1)
                    act.wait_ge(row_stored[k], turn * 16)
                    if scale is None:
                        ins = act.activation(row_out[:, k * D:(k + 1) * D], at(dst, i * D, D), ACT.Copy)
                    else:
                        ins = act.activation(row_out[:, k * D:(k + 1) * D], at(dst, i * D, D), ACT.Copy,
                                             scale=at(scale, i, 1))
                    ins.then_inc(rows_ready, 1)

                with act.Fori(0, NT // 2) as h:
                    for k in range(2):
                        put(h * 2 + k, k, h)
                put(NT - 1, 0, NT // 2)

        @block.sync
        def _(sp):
            if table is not None:
                def store(i, k):
                    sp.wait_ge(rows_ready, i + 1)
                    sp.dma_start(table[bass.ds(i * P, P), :], row_out[:, k * D:(k + 1) * D]).then_inc(row_stored[k], 16)

                with sp.Fori(0, NT // 2) as h:
                    for k in range(2):
                        store(h * 2 + k, k)
                store(NT - 1, 0)
                sp.wait_ge(row_stored[0], (NT // 2 + 1) * 16)
                sp.wait_ge(row_stored[1], NT // 2 * 16)


class Edges:

    def __init__(self, nc, ctx, const, src, dst, weight, src_rows, dst_rows, weight_rows, norm_out):
        m = Memory(nc, ctx, "edges")
        self.src = m.sb("src", [P, ET], I32)
        self.dst = m.sb("dst", [P, ET])
        self.weight = m.sb("weight", [P, ET])
        self.tile_of = m.sb("tile_of", [1, PAIRS], I32)
        self.window_of = m.sb("window_of", [1, PAIRS], I32)
        self.pairs = m.sb("pairs", [1, 1], I32)
        self.pair_src = m.sb("pair_src", [P, PAIRS], I32)
        self.pair_dst = m.sb("pair_dst", [P, PAIRS])
        self.pair_weight = m.sb("pair_weight", [P, PAIRS])
        with ExitStack() as inner:
            self.build(nc, Memory(nc, inner, "edgelist"), inner, const, src, dst, weight,
                       src_rows, dst_rows, weight_rows, norm_out)

    def build(self, nc, m, ctx, const, src, dst, weight, src_rows, dst_rows, weight_rows, norm_out):
        dst_i = m.sb("dst_i", [P, ET], I32)
        rows_i = m.sb("rows_i", [P, ECH * P], I32)
        rows_f = m.sb("rows_f", [P, ECH * P])
        rows_src_i, rows_src = m.sb("rows_src_i", [P, ECH * P], I32), m.sb("rows_src", [P, ECH * P])
        rows_weight = m.sb("rows_weight", [P, ECH * P])
        ends = m.sb("ends", [P, 2 * ECH])
        ends_i = m.sb("ends_i", [P, 2 * ECH], I32)
        count, start, stop = (m.sb(n, [P, ECH]) for n in ("count", "start", "stop"))
        picked = m.sb("picked", [P, 3 * ECH * P])
        totals = m.sb("totals", [P, ECH])
        tile_no, has = m.sb("tile_no", [P, ECH]), m.sb("has", [P, ECH])
        place = m.sb("place", [P, PAIRS])
        inside = m.sb("inside", [P, ECH * PAIRS])
        rest = m.sb("rest", [P, PAIRS])
        low_i, high_i = m.sb("low_i", [P, ET], I32), m.sb("high_i", [P, ET], I32)
        low, high = m.sb("low", [P, ET]), m.sb("high", [P, ET])
        node = m.sb("node", [P, P])
        is_low, is_high = m.sb("is_low", [P, HB * P], BF16), m.sb("is_high", [P, HB * NT], BF16)
        degree, root_of = m.sb("degree", [P, NT]), m.sb("root_of", [P, NT])
        p_sums = m.ps("p_sums", [P, 512])
        p_start, p_total, p_degree = p_sums[:, 0:ECH], p_sums[:, ECH:2 * ECH], p_sums[:, 128:128 + NT]
        p_list = m.ps("p_list", [P, 6 * 512])
        loaded, made, chain = m.sem("loaded"), m.sem("made"), m.sem("chain")
        counted, placed, chosen, listed = m.sem("counted"), m.sem("placed"), m.sem("chosen"), m.sem("listed")
        hot, summed, root, rooted = m.sem("hot"), m.sem("summed"), m.sem("root"), m.sem("rooted")
        block = ctx.enter_context(nc.Block())

        @block.sync
        def _(sp):
            for to, of in ((self.src, src), (dst_i, dst), (self.weight, weight)):
                sp.dma_start(to[:, :], of).then_inc(loaded, 16)
            for to, of in ((rows_i, dst_rows), (rows_src_i, src_rows), (rows_weight, weight_rows)):
                sp.dma_start(to[:, :].rearrange("p (c e) -> p c e", e=P),
                             of.rearrange("(c p) e -> p c e", p=P)).then_inc(loaded, 16)

        @block.gpsimd
        def _(pool):
            pool.iota(tile_no[:, :], pattern=[[P, ECH]], base=0, channel_multiplier=1,
                      allow_small_or_imprecise_dtypes=True).then_inc(made, 1)
            pool.iota(place[:, :], pattern=[[1, PAIRS]], base=0, channel_multiplier=0,
                      allow_small_or_imprecise_dtypes=True).then_inc(made, 1)
            pool.iota(node[:, :], pattern=[[1, P]], base=0, channel_multiplier=0,
                      allow_small_or_imprecise_dtypes=True).then_inc(made, 1)

        @block.vector
        def _(dve):
            c = Chain(dve, chain)
            dve.wait_ge(loaded, 96)
            dve.wait_ge(made, 3)
            c.did(dve.tensor_copy(rows_src[:, :], rows_src_i[:, :]))
            c.did(dve.tensor_copy(self.dst[:, :], dst_i[:, :]))
            c.did(dve.tensor_copy(rows_f[:, :], rows_i[:, :]))
            c.did(dve.tensor_scalar(low_i[:, :], self.src[:, :], P - 1, None, ALU.bitwise_and))
            c.step(dve.tensor_scalar(high_i[:, :], self.src[:, :], 7, None, ALU.arith_shift_right))
            c.did(dve.tensor_copy(low[:, :], low_i[:, :]))
            c.did(dve.tensor_copy(high[:, :], high_i[:, :]))
            r = rows_f[:, :].rearrange("p (c e) -> p c e", e=P)
            c.did(dve.tensor_reduce(ends[:, 0:ECH], r, AX_X, ALU.min))
            c.step(dve.tensor_reduce(ends[:, ECH:], r, AX_X, ALU.max))
            c.step(dve.tensor_copy(ends_i[:, :], ends[:, :]))
            c.step(dve.tensor_scalar(ends_i[:, :], ends_i[:, :], 7, None, ALU.arith_shift_right))
            c.step(dve.tensor_copy(ends[:, :], ends_i[:, :]))
            c.did(dve.tensor_scalar(has[:, :], tile_no[:, :], float(ET), None, ALU.is_lt))
            c.step(dve.scalar_tensor_tensor(out=count[:, :], in0=ends[:, ECH:], scalar=1.0, in1=ends[:, 0:ECH],
                                            op0=ALU.add, op1=ALU.subtract))
            dve.tensor_tensor(count[:, :], count[:, :], has[:, :], ALU.mult).then_inc(counted, 1)
            dve.wait_ge(placed, 2)
            c.did(dve.tensor_copy(start[:, :], p_start))
            c.step(dve.tensor_copy(totals[:, :], p_total))
            for k in range(1, ECH):
                c.step(dve.tensor_scalar(start[:, k:], start[:, k:], totals[:, k - 1:k], None, ALU.add))
            def wide(q):
                return picked[:, q * ECH * P:(q + 1) * ECH * P].rearrange("p (c m) -> p c m", m=P)

            def narrow(v):
                return v[:, :].unsqueeze(2).to_broadcast([P, ECH, P])

            c.did(dve.tensor_tensor(wide(0), narrow(ends[:, 0:ECH]), narrow(start), ALU.subtract))
            c.did(dve.tensor_copy(wide(1), narrow(tile_no)))
            c.did(dve.memset(picked[:, 2 * ECH * P:], 1.0))
            c.did(dve.tensor_tensor(stop[:, :], start[:, :], count[:, :], ALU.add))
            c.step(dve.tensor_reduce(totals[:, 0:1], totals[:, :], AX_X, ALU.add))
            c.did(dve.tensor_copy(self.pairs[:, :], totals[0:1, 0:1]))
            for k in range(ECH):
                own = inside[:, k * PAIRS:(k + 1) * PAIRS]
                c.step(dve.tensor_scalar(own, place[:, :], start[:, k:k + 1], None, ALU.is_ge))
                c.step(dve.scalar_tensor_tensor(out=own, in0=place[:, :], scalar=stop[:, k:k + 1], in1=own,
                                                op0=ALU.is_lt, op1=ALU.mult))
            dve.sem_inc(chosen, 1)
            dve.wait_ge(listed, 6)
            c.did(dve.tensor_copy(self.tile_of[:, :], p_list[0:1, 512:512 + PAIRS]))
            c.did(dve.tensor_copy(self.pair_src[:, :], p_list[:, 1536:1536 + PAIRS]))
            c.did(dve.tensor_copy(self.pair_weight[:, :], p_list[:, 2560:2560 + PAIRS]))
            c.did(dve.tensor_scalar(rest[:, :], p_list[:, 1024:1024 + PAIRS], -float(NT), float(NT), ALU.mult, ALU.add))
            w = place[:, :]
            c.step(dve.tensor_tensor(w, w, p_list[:, 0:PAIRS], ALU.add))
            c.step(dve.tensor_tensor(w, w, p_list[:, 1024:1024 + PAIRS], ALU.mult))
            c.step(dve.tensor_tensor(w, w, rest[:, :], ALU.add))
            c.did(dve.tensor_copy(self.window_of[:, :], place[0:1, :]))
            c.did(dve.scalar_tensor_tensor(out=self.pair_dst[:, :], in0=w, scalar=-float(P),
                                           in1=p_list[:, 2048:2048 + PAIRS], op0=ALU.mult, op1=ALU.add))
            c.step(dve.memset(degree[:, :], 0.0))
            base = c.n
            per = 3
            with dve.Fori(0, ET // HB) as i:
                t = Chain(dve, chain, i * per + base)
                dve.wait_ge(summed, i)
                t.did(dve.tensor_tensor(is_low[:, :].rearrange("p (t n) -> p t n", n=P),
                                        node[:, :].unsqueeze(1).to_broadcast([P, HB, P]),
                                        at(low, i * HB, HB).unsqueeze(2).to_broadcast([P, HB, P]), ALU.is_equal))
                t.step(dve.tensor_tensor(is_high[:, :].rearrange("p (t n) -> p t n", n=NT),
                                         node[:, 0:NT].unsqueeze(1).to_broadcast([P, HB, NT]),
                                         at(high, i * HB, HB).unsqueeze(2).to_broadcast([P, HB, NT]), ALU.is_equal))
                dve.sem_inc(hot, 1)
                dve.wait_ge(summed, i + 1)
                t.step(dve.tensor_tensor(degree[:, :], degree[:, :], p_degree, ALU.add))
                assert t.n == per
            c.n = base + ET // HB * per
            dve.tensor_scalar(degree[:, :], degree[:, :], 1.0, None, ALU.max).then_inc(root, 1)
            dve.wait_ge(rooted, 1)
            c.step(dve.reciprocal(norm_out[:, :], root_of[:, :]))
            refine(c, norm_out, degree, root_of)

        @block.scalar
        def _(act):
            act.wait_ge(root, 1)
            act.activation(root_of[:, :], degree[:, :], ACT.Sqrt).then_inc(rooted, 1)

        @block.tensor
        def _(pe):
            pe.wait_ge(counted, 1)
            pe.matmul(p_start, const.before[:, :], count[:, :], start=True, stop=True).then_inc(placed, 1)
            pe.matmul(p_total, const.ones[:, :], count[:, :], start=True, stop=True).then_inc(placed, 1)
            pe.wait_ge(chosen, 1)
            for q in range(6):
                of, o = ((picked, q * ECH * P), (rows_src, 0), (rows_f, 0), (rows_weight, 0))[max(q - 2, 0)]
                for k in range(ECH):
                    mm = pe.matmul(p_list[:, q * 512:q * 512 + PAIRS], of[:, o + k * P:o + (k + 1) * P],
                                   inside[:, k * PAIRS:(k + 1) * PAIRS], start=(k == 0), stop=(k == ECH - 1))
                mm.then_inc(listed, 1)
            with pe.Fori(0, ET // HB) as i:
                pe.wait_ge(hot, i + 1)
                for h in range(HB):
                    mm = pe.matmul(p_degree, is_low[:, h * P:(h + 1) * P], is_high[:, h * NT:(h + 1) * NT],
                                   start=(h == 0), stop=(h == HB - 1))
                mm.then_inc(summed, 1)


def aggregate(nc, tag, edges, table, acc, width, weighted, edge_rows=None):
    with ExitStack() as ctx:
        m = Memory(nc, ctx, tag)
        columns = m.sb("columns", [P, (NT + 1) * P])
        index = m.sb("index", [P, 2 * SL], I32)
        message = m.sb("message", [P, SL * width])
        onehot = m.sb("onehot", [P, 2 * SL * P])
        partial = [m.ps(f"partial{k}", [P, width]) for k in range(SP)]
        ready, chain = m.sem("ready"), m.sem("chain")
        indexed, marked = m.sem("indexed"), m.sem("marked")
        gathered, featured, used, added = (
            [m.sem(f"{n}{k}") for k in range(SL)] for n in ("gathered", "featured", "used", "added"))
        all_indexed, all_gathered, all_featured, all_marked, all_used, all_added, all_chain = (
            m.sem(f"all_{n}") for n in ("indexed", "gathered", "featured", "marked", "used", "added", "chain"))
        tile_taken, tile_begun, asked = m.sem("tile_taken"), m.sem("tile_begun"), m.sem("asked")
        block = ctx.enter_context(nc.Block())
        rounds = PAIRS // SL

        def msg(k):
            return message[:, k * width:(k + 1) * width]

        def pair_count(eng):
            return eng.value_load(edges.pairs[0:1, 0:1], min_val=0, max_val=ET * NT)

        def tile_of(eng, j):
            return eng.value_load(edges.tile_of[0:1, bass.ds(j, 1)], min_val=0, max_val=ET - 1)

        def window_of(eng, j):
            return eng.value_load(edges.window_of[0:1, bass.ds(j, 1)], min_val=0, max_val=NT)

        def gather(pool, k, i, sem):
            pool.sem_inc(asked, 1)
            pool.indirect_dma_start(out=message[:, k * width:k * width + D], out_offset=None, in_=table,
                                    in_offset=bass.IndirectOffsetOnAxis(ap=index[:, i:i + 1], axis=0)).then_inc(sem, 16)

        @block.gpsimd
        def _(pool):
            pool.iota(columns[:, :], pattern=[[1, (NT + 1) * P]], base=0, channel_multiplier=0,
                      allow_small_or_imprecise_dtypes=True).then_inc(ready, 1)
            pool.wait_ge(ready, 2)
            pairs = pair_count(pool)
            with pool.If(pairs <= PAIRS):
                with pool.Fori(0, rounds // 2) as q:
                    for h in range(2):
                        r = q * 2 + h
                        pool.wait_ge(indexed, r + 1)
                        for k in range(SL):
                            pool.wait_ge(used[k], r)
                            gather(pool, k, h * SL + k, gathered[k])
            with pool.Else():
                with pool.Fori(0, ET) as t:
                    pool.wait_ge(all_indexed, t + 1)
                    gather(pool, 0, 0, all_gathered)

        @block.scalar
        def _(act):
            def pick(h, r):
                return act.copy(index[:, h * SL:(h + 1) * SL], edges.pair_src[:, bass.ds(r * SL, SL)])

            pairs = pair_count(act)
            with act.If(pairs <= PAIRS):
                for h in range(2):
                    pick(h, h).then_inc(indexed, 1)
                with act.Fori(1, rounds // 2) as q:
                    for h in range(2):
                        r = q * 2 + h
                        act.wait_ge(used[SL - 1], r - 1)
                        pick(h, r).then_inc(indexed, 1)
            with act.Else():
                with act.Fori(0, ET) as t:
                    act.wait_ge(tile_taken, t)
                    act.copy(index[:, 0:1], edges.src[:, bass.ds(t, 1)]).then_inc(all_indexed, 1)

        @block.sync
        def _(sp):
            if edge_rows is not None:
                def features(k, t):
                    return sp.dma_start(message[:, k * width + D:k * width + D + DE], edge_rows[bass.ds(t * P, P), :])

                pairs = pair_count(sp)
                sp.wait_ge(ready, 2)
                with sp.If(pairs <= PAIRS):
                    with sp.Fori(0, rounds) as r:
                        for k in range(SL):
                            t = tile_of(sp, r * SL + k)
                            sp.wait_ge(used[k], r)
                            features(k, t).then_inc(featured[k], 16)
                with sp.Else():
                    with sp.Fori(0, ET) as t:
                        sp.wait_ge(tile_taken, t)
                        features(0, t).then_inc(all_featured, 16)

        @block.vector
        def _(dve):
            c = Chain(dve, chain)
            c.did(dve.memset(acc[:, :], 0.0))
            c.step(dve.memset(message[:, :], 1.0))
            dve.sem_inc(ready, 1)
            dve.wait_ge(ready, 2)

            def mark_round(h, r):
                if weighted:
                    for k in range(SL):
                        j = r * SL + k
                        ins = dve.tensor_scalar(onehot[:, (h * SL + k) * P:(h * SL + k + 1) * P], columns[:, 0:P],
                                                edges.pair_dst[:, bass.ds(j, 1)], edges.pair_weight[:, bass.ds(j, 1)],
                                                ALU.is_equal, ALU.mult)
                else:
                    ins = dve.tensor_tensor(onehot[:, h * SL * P:(h + 1) * SL * P].rearrange("p (k n) -> p k n", n=P),
                                            columns[:, 0:P].unsqueeze(1).to_broadcast([P, SL, P]),
                                            edges.pair_dst[:, bass.ds(r * SL, SL)].unsqueeze(2).to_broadcast([P, SL, P]),
                                            ALU.is_equal)
                ins.then_inc(marked, 1)

            def mark(k, t, w):
                hot = onehot[:, k * P:(k + 1) * P]
                col = columns[:, bass.ds(w * P, P)]
                if weighted:
                    return dve.tensor_scalar(hot, col, edges.dst[:, bass.ds(t, 1)], edges.weight[:, bass.ds(t, 1)],
                                             ALU.is_equal, ALU.mult)
                return dve.tensor_scalar(hot, col, edges.dst[:, bass.ds(t, 1)], None, ALU.is_equal)

            def add(k, w):
                to = acc[:, bass.ds(w * width, width)]
                return dve.tensor_tensor(to, to, partial[k % SP][:, :], ALU.add)

            pairs = pair_count(dve)
            with dve.If(pairs <= PAIRS):
                def add_round(r):
                    for k in range(SL):
                        w = window_of(dve, r * SL + k)
                        dve.wait_ge(used[k], r + 1)
                        if k:
                            dve.wait_ge(added[k - 1], r + 1)
                        else:
                            dve.wait_ge(added[SL - 1], r)
                        add(k, w).then_inc(added[k], 1)

                mark_round(0, 0)
                with dve.Fori(0, rounds // 2 - 1) as q:
                    for h in range(2):
                        mark_round(1 - h, q * 2 + h + 1)
                        add_round(q * 2 + h)
                mark_round(1, rounds - 1)
                add_round(rounds - 2)
                add_round(rounds - 1)
            with dve.Else():
                with dve.Fori(0, ET) as t:
                    with dve.Fori(0, NT) as w:
                        j = t * NT + w
                        dve.wait_ge(all_used, j)
                        mark(0, t, w).then_inc(all_marked, 1)
                        dve.wait_ge(all_used, j + 1)
                        dve.wait_ge(all_added, j)
                        add(0, w).then_inc(all_added, 1)

        @block.tensor
        def _(pe):
            def product(k, h=0):
                hot = onehot[:, (h * SL + k) * P:(h * SL + k + 1) * P]
                return pe.matmul(partial[k % SP][:, :], hot, msg(k), start=True, stop=True)

            pairs = pair_count(pe)
            with pe.If(pairs <= PAIRS):
                with pe.Fori(0, rounds // 2) as q:
                    for h in range(2):
                        r = q * 2 + h
                        pe.wait_ge(marked, r + 1)
                        for k in range(SL):
                            pe.wait_ge(gathered[k], (r + 1) * 16)
                            if edge_rows is not None:
                                pe.wait_ge(featured[k], (r + 1) * 16)
                            if k < SP:
                                pe.wait_ge(added[k + SL - SP], r)
                            else:
                                pe.wait_ge(added[k - SP], r + 1)
                            product(k, h).then_inc(used[k], 1)
            with pe.Else():
                with pe.Fori(0, ET) as t:
                    pe.wait_ge(all_gathered, (t + 1) * 16)
                    if edge_rows is not None:
                        pe.wait_ge(all_featured, (t + 1) * 16)
                    pe.sem_inc(tile_begun, 1)
                    with pe.Fori(0, NT) as w:
                        j = t * NT + w
                        pe.wait_ge(all_marked, j + 1)
                        pe.wait_ge(all_added, j)
                        product(0).then_inc(all_used, 1)
                    pe.wait_ge(all_used, (t + 1) * NT)
                    pe.sem_inc(tile_taken, 1)


def map_scale(nc, sumsq, scale):
    with ExitStack() as ctx:
        m = Memory(nc, ctx, "map")
        norm, inv, short, sq, poly, up, down, tmp = (
            m.sb(n, [P, NT]) for n in ("norm", "inv", "short", "sq", "poly", "up", "down", "tmp"))
        chain, floored, rooted, argued, logged = (m.sem(n) for n in ("chain", "floored", "rooted", "argued", "logged"))
        block = ctx.enter_context(nc.Block())

        @block.vector
        def _(dve):
            c = Chain(dve, chain)
            ts, tt = dve.tensor_scalar, dve.tensor_tensor
            c.step(ts(sq[:, :], sumsq[:, :], MINNORM * MINNORM, None, ALU.max))
            dve.sem_inc(floored, 1)
            dve.wait_ge(rooted, 1)
            c.step(dve.reciprocal(inv[:, :], norm[:, :]))
            refine(c, inv, sq, tmp)
            c.step(tt(norm[:, :], sq[:, :], inv[:, :], ALU.mult))
            c.step(ts(short[:, :], norm[:, :], MAXNORM, None, ALU.min))
            c.did(ts(up[:, :], short[:, :], 1.0, None, ALU.add))
            c.step(ts(down[:, :], short[:, :], -1.0, 1.0, ALU.mult, ALU.add))
            dve.sem_inc(argued, 1)
            c.step(tt(sq[:, :], short[:, :], short[:, :], ALU.mult))
            c.step(ts(poly[:, :], sq[:, :], 1.0 / 17, 1.0 / 15, ALU.mult, ALU.add))
            for d in (13, 11, 9, 7, 5, 3, 1):
                c.step(tt(poly[:, :], poly[:, :], sq[:, :], ALU.mult))
                c.step(ts(poly[:, :], poly[:, :], 1.0 / d, None, ALU.add))
            c.step(tt(poly[:, :], poly[:, :], short[:, :], ALU.mult))
            dve.wait_ge(logged, 2)
            c.step(tt(up[:, :], up[:, :], down[:, :], ALU.subtract))
            c.step(ts(up[:, :], up[:, :], 0.5, None, ALU.mult))
            c.step(ts(tmp[:, :], short[:, :], 0.3, None, ALU.is_gt))
            c.step(tt(up[:, :], up[:, :], tmp[:, :], ALU.mult))
            c.step(ts(tmp[:, :], tmp[:, :], -1.0, 1.0, ALU.mult, ALU.add))
            c.step(tt(poly[:, :], poly[:, :], tmp[:, :], ALU.mult))
            c.step(tt(poly[:, :], poly[:, :], up[:, :], ALU.add))
            c.step(tt(scale[:, :], poly[:, :], inv[:, :], ALU.mult))

        @block.scalar
        def _(act):
            act.wait_ge(floored, 1)
            act.activation(norm[:, :], sq[:, :], ACT.Sqrt).then_inc(rooted, 1)
            act.wait_ge(argued, 1)
            for x in (up, down):
                act.activation(x[:, :], x[:, :], ACT.Ln).then_inc(logged, 1)


def qkv_channels(nc, const, XN, scale, w, YT, stats):
    with ExitStack() as ctx:
        m = Memory(nc, ctx, "qkv")
        weight = m.sb("weight", [P, 2 * C0])
        rows = m.sb("rows", [P, GT * D])
        turned = m.sb("turned", [P, 2 * GN])
        p_turn = [m.ps(f"p_turn{k}", [P, 512]) for k in range(2)]
        p_out = [m.ps(f"p_out{k}", [P, 1024]) for k in range(2)]
        loaded, scaled, turning, kept, made, stored = (
            m.sem(n) for n in ("loaded", "scaled", "turning", "kept", "made", "stored"))
        block = ctx.enter_context(nc.Block())

        @block.sync
        def _(sp):
            sp.dma_start(weight[:, :], w).then_inc(loaded, 16)

        @block.vector
        def _(dve):
            with dve.Fori(0, NG) as g:
                dve.wait_ge(turning, g * GT)
                for t in range(GT):
                    dve.tensor_scalar(rows[:, t * D:(t + 1) * D], at(XN, (g * GT + t) * D, D),
                                      at(scale, g * GT + t, 1), None, ALU.mult).then_inc(scaled, 1)
                for q in range(CH0):
                    dve.wait_ge(stored, g * CH0 + q + 1)
                    for h in range(2):
                        dve.bn_stats(at(stats, (q * NG + g) * 12 + h * 6, 6), at(YT, q * NPAD + g * GN + h * GH, GH))

        @block.tensor
        def _(pe):
            pe.wait_ge(loaded, 16)
            with pe.Fori(0, NG) as g:
                for t in range(GT):
                    pe.wait_ge(scaled, g * GT + t + 1)
                    pe.wait_ge(kept, g * GT + max(t - 1, 0)) if t else pe.wait_ge(kept, g * GT)
                    for c in range(2):
                        mm = pe.transpose(p_turn[t % 2][:, c * P:(c + 1) * P],
                                          rows[:, t * D + c * P:t * D + (c + 1) * P], const.ident[:, :])
                    mm.then_inc(turning, 1)
                pe.wait_ge(kept, (g + 1) * GT)
                for q in range(CH0):
                    if q < 2:
                        pe.wait_ge(stored, g * CH0)
                    else:
                        pe.wait_ge(stored, g * CH0 + q - 1)
                    for h in range(2):
                        for c in range(2):
                            mm = pe.matmul(p_out[q % 2][:, h * 512:h * 512 + GH],
                                           weight[:, c * C0 + q * P:c * C0 + (q + 1) * P],
                                           turned[:, c * GN + h * GH:c * GN + (h + 1) * GH], start=(c == 0), stop=(c == 1))
                    mm.then_inc(made, 1)

        @block.scalar
        def _(act):
            with act.Fori(0, NG) as g:
                act.wait_ge(made, g * CH0)
                for t in range(GT):
                    act.wait_ge(turning, g * GT + t + 1)
                    act.copy(turned[:, :].rearrange("p (c n) -> p c n", c=2)[:, :, t * P:(t + 1) * P],
                             p_turn[t % 2][:, 0:D].rearrange("p (c n) -> p c n", c=2)).then_inc(kept, 1)
                for q in range(CH0):
                    act.wait_ge(made, g * CH0 + q + 1)
                    act.copy(at(YT, q * NPAD + g * GN, GN).rearrange("p (h n) -> p h n", h=2),
                             p_out[q % 2][:, :].rearrange("p (h n) -> p h n", h=2)[:, :, 0:GH]).then_inc(stored, 1)


def batch_norm(nc, stats, gamma, beta, bn_scale, bn_shift):
    with ExitStack() as ctx:
        m = Memory(nc, ctx, "bn")
        gamma_c, beta_c = m.sb("gamma_c", [P, CH0]), m.sb("beta_c", [P, CH0])
        pair = m.sb("pair", [P, 2 * CH0])
        mean, var, root, tmp = (m.sb(n, [P, CH0]) for n in ("mean", "var", "root", "tmp"))
        loaded, chain, ready, rooted = (m.sem(n) for n in ("loaded", "chain", "ready", "rooted"))
        block = ctx.enter_context(nc.Block())

        @block.sync
        def _(sp):
            sp.dma_start(gamma_c[:, :], gamma).then_inc(loaded, 16)
            sp.dma_start(beta_c[:, :], beta).then_inc(loaded, 16)

        @block.vector
        def _(dve):
            c = Chain(dve, chain)
            for q in range(CH0):
                c.did(dve.bn_aggr(pair[:, 2 * q:2 * q + 2], stats[:, q * NG * 12:(q + 1) * NG * 12]))
            c.settle()
            pv = pair[:, :].rearrange("p (q s) -> p q s", s=2)
            c.did(dve.tensor_scalar(mean[:, :], pv[:, :, 0], NPAD / N, None, ALU.mult))
            c.step(dve.scalar_tensor_tensor(out=tmp[:, :], in0=pv[:, :, 0], scalar=-(NPAD * (NPAD - N)) / (N * N),
                                            in1=pv[:, :, 0], op0=ALU.mult, op1=ALU.mult))
            c.step(dve.scalar_tensor_tensor(out=var[:, :], in0=pv[:, :, 1], scalar=NPAD / N, in1=tmp[:, :],
                                            op0=ALU.mult, op1=ALU.add))
            c.step(dve.tensor_scalar(var[:, :], var[:, :], 1e-5, None, ALU.add))
            dve.sem_inc(ready, 1)
            dve.wait_ge(rooted, 1)
            c.step(dve.reciprocal(bn_scale[:, :], root[:, :]))
            refine(c, bn_scale, var, tmp)
            dve.wait_ge(loaded, 32)
            c.step(dve.tensor_tensor(bn_scale[:, :], bn_scale[:, :], gamma_c[:, :], ALU.mult))
            c.step(dve.tensor_tensor(tmp[:, :], mean[:, :], bn_scale[:, :], ALU.mult))
            c.step(dve.tensor_tensor(bn_shift[:, :], beta_c[:, :], tmp[:, :], ALU.subtract))

        @block.scalar
        def _(act):
            act.wait_ge(ready, 1)
            act.activation(root[:, :], var[:, :], ACT.Sqrt).then_inc(rooted, 1)


def limited(c, out, sumsq, tmp, limit, root):
    dve = c.eng
    c.step(dve.tensor_scalar(tmp[:, 0:1], sumsq, MINNORM * MINNORM, None, ALU.max))
    root()
    c.step(dve.tensor_scalar(out, tmp[:, 1:2], limit, None, ALU.min))
    c.step(dve.reciprocal(tmp[:, 1:2], tmp[:, 1:2]))
    c.step(dve.tensor_tensor(out, out, tmp[:, 1:2], ALU.mult))


def graph_and_mixer(nc, const, acc, X, YT, bn_scale, bn_shift, FT, sumsq, gw, gbias, w_dw, w_pw, w_res, b_res):
    AW = D + DE + 1
    with ExitStack() as ctx:
        m = Memory(nc, ctx, "mix")
        g_w = m.sb("g_w", [P, 3 * D])
        g_b, r_b = m.sb("g_b", [P, D]), m.sb("r_b", [P, D])
        taps = m.sb("taps", [P, CH0])
        blocks = m.sb("blocks", [P, C0])
        r_w = m.sb("r_w", [P, 4 * D])
        norm_in, deg, dtmp = m.sb("norm_in", [P, NT]), m.sb("deg", [P, NT]), m.sb("dtmp", [P, NT])
        rT = m.sb("rT", [P, C0])
        agg = m.sb("agg", [P, D + DE])
        aggT = m.sb("aggT", [P, 3 * P])
        square = m.sb("square", [P, C0])
        sums = m.sb("sums", [P, 3])
        tmp = m.sb("tmp", [P, 8])
        k_sum = m.sb("k_sum", [P, GRP])
        kr = m.sb("kr", [P, 512])
        den, prod = m.sb("den", [P, 512]), m.sb("prod", [P, 512])
        prodT = m.sb("prodT", [P, 512])
        g_out = m.sb("g_out", [P, D])
        cat = m.ps("cat", [P, 2 * C0])
        p_prod, p_res, p_agg, p_gnn = (m.ps(n, [P, 512]) for n in ("p_prod", "p_res", "p_agg", "p_gnn"))
        loaded, cleared, chain, dwed = m.sem("loaded"), m.sem("cleared"), m.sem("chain"), m.sem("dwed")
        deg_ready, deg_rooted = m.sem("deg_ready"), m.sem("deg_rooted")
        relued, catted, squared, asked_root, rooted = (
            m.sem(n) for n in ("relued", "catted", "squared", "asked_root", "rooted"))
        staged, agg_turned, agg_kept, gnn_done, gnn_added = (
            m.sem(n) for n in ("staged", "agg_turned", "agg_kept", "gnn_done", "gnn_added"))
        prod_ready, prod_turned, prod_kept, res_done, res_ready, ft_squared = (
            m.sem(n) for n in ("prod_ready", "prod_turned", "prod_kept", "res_done", "res_ready", "ft_squared"))
        block = ctx.enter_context(nc.Block())

        @block.sync
        def _(sp):
            sp.wait_ge(cleared, 2)
            sp.dma_start(g_w[:, 0:2 * D].rearrange("p (k d) -> p k d", d=D),
                         gw[0:2 * P, :].rearrange("(k p) d -> p k d", p=P)).then_inc(loaded, 16)
            sp.dma_start(g_w[0:DE, 2 * D:3 * D], gw[2 * P:, :]).then_inc(loaded, 16)
            sp.dma_start(g_b[:, :], row(gbias)).then_inc(loaded, 16)
            sp.dma_start(r_b[:, :], row(b_res)).then_inc(loaded, 16)
            sp.dma_start(taps[:, :], w_dw).then_inc(loaded, 16)
            sp.dma_start(r_w[:, :], w_res).then_inc(loaded, 16)
            for b in range(4):
                sp.dma_start(blocks[32 * b:32 * b + 32, :].rearrange("i (q b o) -> i q b o", b=4, o=32)[:, :, b, :],
                             w_pw[b, :, :].rearrange("i (q o) -> i q o", o=32)).then_inc(loaded, 16)

        @block.gpsimd
        def _(pool):
            pool.memset(blocks[:, :], 0.0).then_inc(cleared, 1)
            pool.memset(g_w[:, :], 0.0).then_inc(cleared, 1)

        @block.vector
        def _(dve):
            c = Chain(dve, chain)
            ts, tt, stt = dve.tensor_scalar, dve.tensor_tensor, dve.scalar_tensor_tensor
            c.step(ts(deg[:, :], acc[:, :].rearrange("p (i a) -> p i a", a=AW)[:, 0:NT, AW - 1], 1.0, None, ALU.max))
            dve.sem_inc(deg_ready, 1)
            dve.wait_ge(deg_rooted, 1)
            c.step(dve.reciprocal(norm_in[:, :], dtmp[:, :]))
            refine(c, norm_in, deg, dtmp)
            dve.wait_ge(loaded, 160)
            for q in range(CH0):
                c.did(ts(blocks[:, q * P:(q + 1) * P], blocks[:, q * P:(q + 1) * P], taps[:, q:q + 1], None, ALU.mult))
            c.settle()
            dve.sem_inc(dwed, 1)
            base, per = c.n, 29
            q_, k_, v_ = (cat[:, :].rearrange("p (g c) -> p g c", c=96)[:, :, 32 * n:32 * n + 32] for n in range(3))
            third = lambda b: b[:, :].rearrange("p (g c) -> p g c", c=32)
            with dve.Fori(0, NT) as i:
                t = Chain(dve, chain, i * per + base)
                roots = [0]

                def root():
                    dve.sem_inc(asked_root, 1)
                    roots[0] += 1
                    dve.wait_ge(rooted, i * 3 + roots[0])

                dve.wait_ge(agg_turned, i)
                t.step(ts(agg[:, :], at(acc, i * AW, D + DE), at(norm_in, i, 1), None, ALU.mult))
                dve.sem_inc(staged, 1)
                dve.wait_ge(catted, i + 1)
                dve.wait_ge(squared, i * 3 + 2)
                dve.wait_ge(prod_kept, i)
                t.step(ts(third(kr), k_, 0.0, None, ALU.max))
                t.did(dve.tensor_reduce(k_sum[:, :], third(kr), AX_X, ALU.add))
                limited(t, tmp[:, 2:3], sums[:, 0:1], tmp, ATANH_MAXNORM, root)
                t.step(tt(tmp[:, 3:4], sums[:, 0:1], sums[:, 1:2], ALU.add))
                t.step(stt(out=tmp[:, 3:4], in0=tmp[:, 3:4], scalar=tmp[:, 2:3], in1=tmp[:, 2:3],
                           op0=ALU.mult, op1=ALU.mult))
                limited(t, tmp[:, 4:5], tmp[:, 3:4], tmp, ATANH_MAXNORM, root)
                t.step(tt(tmp[:, 4:5], tmp[:, 4:5], tmp[:, 2:3], ALU.mult))
                t.did(stt(out=tmp[:, 5:6], in0=tmp[:, 4:5], scalar=tmp[:, 4:5], in1=tmp[:, 4:5],
                          op0=ALU.mult, op1=ALU.mult))
                t.step(ts(third(den), v_, tmp[:, 4:5], 1e-15, ALU.mult, ALU.add))
                t.step(dve.reciprocal(den[:, :], den[:, :]))
                t.step(tt(third(prod), v_, third(den), ALU.mult))
                t.step(stt(out=third(prod), in0=q_, scalar=0.0, in1=third(prod), op0=ALU.max, op1=ALU.mult))
                t.step(tt(third(prod), third(prod), k_sum[:, :].unsqueeze(2).to_broadcast([P, GRP, 32]), ALU.mult))
                dve.sem_inc(prod_ready, 1)
                dve.wait_ge(gnn_done, i + 1)
                t.step(tt(g_out[:, :], p_gnn[:, 0:D], g_b[:, :], ALU.add))
                t.did(stt(out=at(X, i * D, D), in0=g_out[:, :], scalar=0.0, in1=at(X, i * D, D),
                          op0=ALU.max, op1=ALU.add))
                dve.wait_ge(squared, i * 3 + 3)
                t.step(stt(out=tmp[:, 6:7], in0=sums[:, 2:3], scalar=tmp[:, 5:6], in1=tmp[:, 5:6],
                           op0=ALU.mult, op1=ALU.mult))
                limited(t, tmp[:, 6:7], tmp[:, 6:7], tmp, ATANH_MAXNORM, root)
                t.step(tt(tmp[:, 7:8], tmp[:, 6:7], tmp[:, 5:6], ALU.mult))
                dve.wait_ge(res_done, i + 1)
                t.step(stt(out=at(FT, i * D, D), in0=p_res[:, 0:D], scalar=tmp[:, 7:8], in1=r_b[:, :],
                           op0=ALU.mult, op1=ALU.add))
                dve.sem_inc(res_ready, 1)
                assert t.n == per, t.n

        @block.scalar
        def _(act):
            act.wait_ge(deg_ready, 1)
            act.activation(dtmp[:, :], deg[:, :], ACT.Sqrt).then_inc(deg_rooted, 1)
            with act.Fori(0, NT) as i:
                act.wait_ge(catted, i)
                for q in range(CH0):
                    act.activation(rT[:, q * P:(q + 1) * P], at(YT, i * P + q * NPAD, P), ACT.Relu,
                                   scale=bn_scale[:, q:q + 1], bias=bn_shift[:, q:q + 1]).then_inc(relued, 1)
                act.wait_ge(agg_turned, i + 1)
                act.copy(aggT[:, 0:2 * P], p_agg[:, 0:2 * P]).then_inc(agg_kept, 1)
                act.copy(aggT[0:DE, 2 * P:], p_agg[0:DE, 2 * P:3 * P]).then_inc(agg_kept, 1)
                act.wait_ge(catted, i + 1)
                act.wait_ge(res_ready, i)
                act.wait_ge(ft_squared, i)
                for h in range(2):
                    act.wait_ge(squared, i * 3 + h)
                    act.activation(square[:, :], cat[:, h * C0:(h + 1) * C0], ACT.Square,
                                   accum_out=sums[:, h:h + 1]).then_inc(squared, 1)
                for n in range(2):
                    act.wait_ge(asked_root, i * 3 + n + 1)
                    act.activation(tmp[:, 1:2], tmp[:, 0:1], ACT.Sqrt).then_inc(rooted, 1)
                act.wait_ge(prod_turned, i + 1)
                act.copy(prodT[:, :], p_prod[:, :]).then_inc(prod_kept, 1)
                act.wait_ge(squared, i * 3 + 2)
                act.activation(square[:, 0:512], prod[:, :], ACT.Square, accum_out=sums[:, 2:3]).then_inc(squared, 1)
                act.wait_ge(asked_root, i * 3 + 3)
                act.activation(tmp[:, 1:2], tmp[:, 0:1], ACT.Sqrt).then_inc(rooted, 1)
                act.wait_ge(res_ready, i + 1)
                act.wait_ge(squared, i * 3 + 3)
                act.activation(square[:, 0:D], at(FT, i * D, D), ACT.Square, accum_out=at(sumsq, i, 1)).then_inc(ft_squared, 1)

        @block.tensor
        def _(pe):
            pe.wait_ge(loaded, 160)
            pe.wait_ge(dwed, 1)
            with pe.Fori(0, NT) as i:
                pe.wait_ge(prod_ready, i)
                pe.wait_ge(squared, i * 3)
                pe.wait_ge(relued, (i + 1) * CH0)
                for q in range(CH0):
                    pe.transpose(cat[:, q * P:(q + 1) * P], rT[:, q * P:(q + 1) * P], const.ident[:, :])
                for q in range(CH0):
                    mm = pe.matmul(cat[:, C0 + q * P:C0 + (q + 1) * P], rT[:, q * P:(q + 1) * P],
                                   blocks[:, q * P:(q + 1) * P], start=True, stop=True)
                mm.then_inc(catted, 1)
                pe.wait_ge(staged, i + 1)
                pe.wait_ge(agg_kept, i * 2)
                for k in range(3):
                    w = P if k < 2 else DE
                    mm = pe.transpose(p_agg[0:w, k * P:(k + 1) * P], agg[:, k * P:k * P + w], const.ident[:, :])
                mm.then_inc(agg_turned, 1)
                pe.wait_ge(agg_kept, (i + 1) * 2)
                pe.wait_ge(res_ready, i)
                for k in range(3):
                    w = P if k < 2 else DE
                    mm = pe.matmul(p_gnn[:, 0:D], aggT[0:w, k * P:(k + 1) * P], g_w[0:w, k * D:(k + 1) * D],
                                   start=(k == 0), stop=(k == 2))
                mm.then_inc(gnn_done, 1)
                pe.wait_ge(prod_ready, i + 1)
                for k in range(4):
                    mm = pe.transpose(p_prod[:, k * P:(k + 1) * P], prod[:, k * P:(k + 1) * P], const.ident[:, :])
                mm.then_inc(prod_turned, 1)
                pe.wait_ge(prod_kept, i + 1)
                for k in range(4):
                    mm = pe.matmul(p_res[:, 0:D], prodT[:, k * P:(k + 1) * P], r_w[:, k * D:(k + 1) * D],
                                   start=(k == 0), stop=(k == 3))
                mm.then_inc(res_done, 1)


def add_mapped(nc, X, FT, sumsq):
    with ExitStack() as ctx:
        m = Memory(nc, ctx, "mapped")
        sq, norm, inv, tmp = (m.sb(n, [P, NT]) for n in ("sq", "norm", "inv", "tmp"))
        chain, floored, rooted, known, tanhed = (m.sem(n) for n in ("chain", "floored", "rooted", "known", "tanhed"))
        block = ctx.enter_context(nc.Block())

        @block.vector
        def _(dve):
            c = Chain(dve, chain)
            c.step(dve.tensor_scalar(sq[:, :], sumsq[:, :], MINNORM * MINNORM, None, ALU.max))
            dve.sem_inc(floored, 1)
            dve.wait_ge(rooted, 1)
            c.step(dve.reciprocal(inv[:, :], norm[:, :]))
            refine(c, inv, sq, tmp)
            c.step(dve.tensor_tensor(norm[:, :], sq[:, :], inv[:, :], ALU.mult))
            dve.sem_inc(known, 1)
            dve.wait_ge(tanhed, 1)
            c.step(dve.scalar_tensor_tensor(out=inv[:, :], in0=tmp[:, :], scalar=MAXNORM, in1=inv[:, :],
                                            op0=ALU.min, op1=ALU.mult))
            with dve.Fori(0, NT) as i:
                dve.scalar_tensor_tensor(out=at(X, i * D, D), in0=at(FT, i * D, D), scalar=at(inv, i, 1),
                                         in1=at(X, i * D, D), op0=ALU.mult, op1=ALU.add)

        @block.scalar
        def _(act):
            act.wait_ge(floored, 1)
            act.activation(norm[:, :], sq[:, :], ACT.Sqrt).then_inc(rooted, 1)
            act.wait_ge(known, 1)
            act.activation(tmp[:, :], norm[:, :], ACT.Tanh).then_inc(tanhed, 1)


def graph_and_kv(nc, const, acc, X, XN, XNT, kv, g_w, g_bias, kv_w, kv_bias):
    with ExitStack() as ctx:
        m = Memory(nc, ctx, "kv")
        gw, kw = m.sb("gw", [P, 4 * D]), m.sb("kw", [P, 4 * D])
        gb, gb2, kb = m.sb("gb", [P, D]), m.sb("gb2", [P, D]), m.sb("kb", [P, 2 * D])
        xs, us, xuT = m.sb("xs", [P, D]), m.sb("us", [P, D]), m.sb("xuT", [P, 2 * D])
        k, neg, v = m.sb("k", [P, D]), m.sb("neg", [P, D]), m.sb("v", [P, 2 * (P + 1)])
        square, sumsq = m.sb("square", [P, D]), m.sb("sumsq", [P, NT])
        inv, tmp, sq = m.sb("inv", [P, NT]), m.sb("tmp", [P, NT]), m.sb("sq", [P, NT])
        p_x, p_kv, p_g, p_a = (m.ps(n, [P, 512]) for n in ("p_x", "p_kv", "p_g", "p_a"))
        loaded, chain, x_staged, u_staged, turned, kept, kv_made, g_made, cut, exped, k_ready, summed, added, g_ready, squared, root, rooted = (
            m.sem(n) for n in ("loaded", "chain", "x_staged", "u_staged", "turned", "kept", "kv_made", "g_made", "cut",
                               "exped", "k_ready", "summed", "added", "g_ready", "squared", "root", "rooted"))
        block = ctx.enter_context(nc.Block())
        v_ = v[:, :].rearrange("p (c n) -> p c n", c=2)

        @block.sync
        def _(sp):
            sp.dma_start(gw[:, :], g_w).then_inc(loaded, 16)
            sp.dma_start(kw[:, :], kv_w).then_inc(loaded, 16)
            sp.dma_start(gb[:, :], row(g_bias[0, :])).then_inc(loaded, 16)
            sp.dma_start(gb2[:, :], row(g_bias[1, :])).then_inc(loaded, 16)
            sp.dma_start(kb[:, :], row(kv_bias)).then_inc(loaded, 16)

        @block.vector
        def _(dve):
            c = Chain(dve, chain)
            ts, tt, stt = dve.tensor_scalar, dve.tensor_tensor, dve.scalar_tensor_tensor
            c.did(dve.memset(kv[:, :], 0.0))
            c.did(dve.memset(v[:, :], 1.0))
            dve.wait_ge(loaded, 80)
            c.step(tt(gb[:, :], gb[:, :], gb2[:, :], ALU.add))
            base, per = c.n, 10
            with dve.Fori(0, NT) as i:
                t = Chain(dve, chain, i * per + base)
                nb = at(acc, i * D, D)
                dve.wait_ge(turned, i)
                t.step(tt(us[:, :], nb, at(XN, i * D, D), ALU.mult))
                t.step(tt(us[:, :], us[:, :], nb, ALU.add))
                dve.sem_inc(u_staged, 1)
                dve.wait_ge(kv_made, i + 1)
                dve.wait_ge(summed, i)
                t.did(tt(v_[:, :, 0:P], p_kv[:, D:2 * D].rearrange("p (c n) -> p c n", c=2),
                         kb[:, D:2 * D].rearrange("p (c n) -> p c n", c=2), ALU.add))
                t.step(tt(k[:, :], p_kv[:, 0:D], kb[:, 0:D], ALU.add))
                t.step(ts(neg[:, :], k[:, :], 0.0, None, ALU.min))
                dve.sem_inc(cut, 1)
                dve.wait_ge(g_made, i + 1)
                t.step(tt(nb, p_g[:, 0:D], gb[:, :], ALU.add))
                t.step(stt(out=nb, in0=nb, scalar=0.2, in1=nb, op0=ALU.mult, op1=ALU.max))
                dve.sem_inc(g_ready, 1)
                dve.wait_ge(exped, i + 1)
                t.step(stt(out=k[:, :], in0=k[:, :], scalar=0.0, in1=neg[:, :], op0=ALU.max, op1=ALU.add))
                t.step(ts(k[:, :], k[:, :], at(const.valid, i, 1), None, ALU.mult))
                dve.sem_inc(k_ready, 1)
                dve.wait_ge(summed, i + 1)
                t.step(tt(kv[:, :], kv[:, :], p_a[:, 0:2 * (P + 1)], ALU.add))
                dve.sem_inc(added, 1)
                assert t.n == per, t.n
            c.n = base + NT * per
            dve.wait_ge(squared, NT)
            c.step(ts(sq[:, :], sumsq[:, :], 1e-24, None, ALU.max))
            dve.sem_inc(root, 1)
            dve.wait_ge(rooted, 1)
            c.step(dve.reciprocal(inv[:, :], tmp[:, :]))
            refine(c, inv, sq, tmp)
            with dve.Fori(0, NT) as i:
                stt(out=at(X, i * D, D), in0=at(acc, i * D, D), scalar=at(inv, i, 1), in1=at(X, i * D, D),
                    op0=ALU.mult, op1=ALU.add)

        @block.scalar
        def _(act):
            with act.Fori(0, NT) as i:
                act.wait_ge(turned, i)
                act.copy(xs[:, :], at(XN, i * D, D)).then_inc(x_staged, 1)
                act.wait_ge(turned, i + 1)
                act.wait_ge(g_made, i)
                act.copy(xuT[:, :], p_x[:, :]).then_inc(kept, 1)
                act.copy(XNT[:, :].rearrange("p (c n) -> p c n", c=2)[:, :, bass.ds(i * P, P)],
                         p_x[:, 0:D].rearrange("p (c n) -> p c n", c=2)).then_inc(kept, 1)
                act.wait_ge(cut, i + 1)
                act.activation(neg[:, :], neg[:, :], ACT.Exp).then_inc(exped, 1)
                act.wait_ge(g_ready, i + 1)
                act.wait_ge(squared, i)
                act.activation(square[:, :], at(acc, i * D, D), ACT.Square, accum_out=at(sumsq, i, 1)).then_inc(squared, 1)
            act.wait_ge(root, 1)
            act.activation(tmp[:, :], sq[:, :], ACT.Sqrt).then_inc(rooted, 1)

        @block.tensor
        def _(pe):
            pe.wait_ge(loaded, 80)
            with pe.Fori(0, NT) as i:
                pe.wait_ge(kept, i * 2)
                pe.wait_ge(x_staged, i + 1)
                pe.wait_ge(u_staged, i + 1)
                for h in range(4):
                    mm = pe.transpose(p_x[:, h * P:(h + 1) * P], (xs, us)[h // 2][:, (h % 2) * P:(h % 2 + 1) * P],
                                      const.ident[:, :])
                mm.then_inc(turned, 1)
                pe.wait_ge(kept, (i + 1) * 2)
                pe.wait_ge(cut, i)
                for h in range(2):
                    mm = pe.matmul(p_kv[:, :], xuT[:, h * P:(h + 1) * P], kw[:, h * 2 * D:(h + 1) * 2 * D],
                                   start=(h == 0), stop=(h == 1))
                mm.then_inc(kv_made, 1)
                pe.wait_ge(g_ready, i)
                for h in range(4):
                    mm = pe.matmul(p_g[:, 0:D], xuT[:, h * P:(h + 1) * P], gw[:, h * D:(h + 1) * D],
                                   start=(h == 0), stop=(h == 3))
                mm.then_inc(g_made, 1)
                pe.wait_ge(k_ready, i + 1)
                pe.wait_ge(added, i)
                for h in range(2):
                    mm = pe.matmul(p_a[:, h * (P + 1):(h + 1) * (P + 1)], k[:, h * P:(h + 1) * P],
                                   v[:, h * (P + 1):(h + 1) * (P + 1)], start=True, stop=True)
                mm.then_inc(summed, 1)


def attend(nc, const, XN, XNT, kv, q_w, q_bias, o_w, o_bias):
    HW = P + HEADS // 2
    with ExitStack() as ctx:
        m = Memory(nc, ctx, "att")
        qw, ow, ob, qb = m.sb("qw", [P, 2 * D]), m.sb("ow", [P, 2 * D]), m.sb("ob", [P, D]), m.sb("qb", [P, 2])
        heads = m.sb("heads", [P, 2 * HW])
        pos, neg = m.sb("pos", [P, 2 * GN]), m.sb("neg", [P, 2 * GN])
        z, o, oT, res = m.sb("z", [P, HEADS]), m.sb("o", [P, D]), m.sb("oT", [P, D]), m.sb("res", [P, D])
        p_q = [m.ps(f"p_q{k}", [P, 1024]) for k in range(2)]
        p_n, p_t, p_o = (m.ps(n, [P, 512]) for n in ("p_n", "p_t", "p_o"))
        loaded, chain, q_made, cut, exped, q_ready, summed, o_ready, turned, kept, made, taken, headed = (
            m.sem(n) for n in ("loaded", "chain", "q_made", "cut", "exped", "q_ready", "summed", "o_ready", "turned",
                               "kept", "made", "taken", "headed"))
        block = ctx.enter_context(nc.Block())
        halves = lambda b, w: b.rearrange("p (h n) -> p h n", h=2)[:, :, 0:w]

        @block.sync
        def _(sp):
            sp.dma_start(qw[:, :], q_w).then_inc(loaded, 16)
            sp.dma_start(qb[:, :], q_bias).then_inc(loaded, 16)
            sp.dma_start(ow[:, :], o_w).then_inc(loaded, 16)
            sp.dma_start(ob[:, :], row(o_bias)).then_inc(loaded, 16)

        @block.vector
        def _(dve):
            c = Chain(dve, chain)
            ts, tt = dve.tensor_scalar, dve.tensor_tensor
            c.step(dve.memset(heads[:, :], 0.0))
            for h in range(2):
                for b in range(4):
                    r = slice(32 * b, 32 * b + 32)
                    c.did(dve.tensor_copy(heads[r, h * HW + 32 * b:h * HW + 32 * b + 32],
                                          kv[r, h * (P + 1) + 32 * b:h * (P + 1) + 32 * b + 32]))
                    c.did(dve.tensor_copy(heads[r, h * HW + P + b:h * HW + P + b + 1],
                                          kv[r, h * (P + 1) + P:(h + 1) * (P + 1)]))
            c.settle()
            dve.sem_inc(headed, 1)
            dve.wait_ge(loaded, 64)
            base, per = c.n, 5 + GT * 5
            with dve.Fori(0, NG) as g:
                t = Chain(dve, chain, g * per + base)
                dve.wait_ge(summed, g * GT)
                for h in range(2):
                    dve.wait_ge(q_made, g * 2 + h + 1)
                    t.did(ts(halves(pos[:, h * GN:(h + 1) * GN], GH), halves(p_q[h][:, :], GH), qb[:, h:h + 1], 0.0,
                             ALU.add, ALU.max))
                    t.did(ts(halves(neg[:, h * GN:(h + 1) * GN], GH), halves(p_q[h][:, :], GH), qb[:, h:h + 1], 0.0,
                             ALU.add, ALU.min))
                t.settle()
                dve.sem_inc(cut, 1)
                dve.wait_ge(exped, g + 1)
                t.step(tt(pos[:, :], pos[:, :], neg[:, :], ALU.add))
                dve.sem_inc(q_ready, 1)
                for n in range(GT):
                    i = g * GT + n
                    dve.wait_ge(summed, i + 1)
                    t.step(ts(z[:, :].rearrange("p (c h) -> p c h", c=2),
                              p_n[:, 0:2 * HW].rearrange("p (c n) -> p c n", c=2)[:, :, P:HW], 1e-6, None, ALU.add))
                    t.step(dve.reciprocal(z[:, :], z[:, :]))
                    dve.wait_ge(turned, i)
                    for h in range(2):
                        last = tt(o[:, h * P:(h + 1) * P].rearrange("p (h e) -> p h e", e=32),
                                  p_n[:, h * HW:h * HW + P].rearrange("p (h e) -> p h e", e=32),
                                  z[:, 4 * h:4 * h + 4].unsqueeze(2).to_broadcast([P, 4, 32]), ALU.mult)
                        if h == 0:
                            t.did(last)
                    last.then_inc(o_ready, 1)
                    dve.wait_ge(made, i + 1)
                    t.step(tt(res[:, :], p_o[:, 0:D], ob[:, :], ALU.add))
                    dve.sem_inc(taken, 1)
                    t.step(tt(at(XN, i * D, D), at(XN, i * D, D), res[:, :], ALU.add))
                assert t.n == per, t.n

        @block.scalar
        def _(act):
            with act.Fori(0, NG) as g:
                act.wait_ge(cut, g + 1)
                act.activation(neg[:, :], neg[:, :], ACT.Exp).then_inc(exped, 1)
                for n in range(GT):
                    i = g * GT + n
                    act.wait_ge(turned, i + 1)
                    act.wait_ge(made, i)
                    act.copy(oT[:, :], p_t[:, 0:D]).then_inc(kept, 1)

        @block.tensor
        def _(pe):
            pe.wait_ge(loaded, 64)
            pe.wait_ge(headed, 1)
            with pe.Fori(0, NG) as g:
                pe.wait_ge(cut, g)
                for h in range(2):
                    for s in range(2):
                        for c in range(2):
                            mm = pe.matmul(p_q[h][:, s * 512:s * 512 + GH], qw[:, c * D + h * P:c * D + (h + 1) * P],
                                           at(XNT, g * GN + c * NPAD + s * GH, GH), start=(c == 0), stop=(c == 1))
                    mm.then_inc(q_made, 1)
                pe.wait_ge(q_ready, g + 1)
                for n in range(GT):
                    i = g * GT + n
                    pe.wait_ge(o_ready, i)
                    for h in range(2):
                        mm = pe.matmul(p_n[:, h * HW:(h + 1) * HW], pos[:, h * GN + n * P:h * GN + (n + 1) * P],
                                       heads[:, h * HW:(h + 1) * HW], start=True, stop=True)
                    mm.then_inc(summed, 1)
                    pe.wait_ge(o_ready, i + 1)
                    pe.wait_ge(kept, i)
                    for h in range(2):
                        mm = pe.transpose(p_t[:, h * P:(h + 1) * P], o[:, h * P:(h + 1) * P], const.ident[:, :])
                    mm.then_inc(turned, 1)
                    pe.wait_ge(kept, i + 1)
                    pe.wait_ge(taken, i)
                    for h in range(2):
                        mm = pe.matmul(p_o[:, 0:D], oT[:, h * P:(h + 1) * P], ow[:, h * D:(h + 1) * D],
                                       start=(h == 0), stop=(h == 1))
                    mm.then_inc(made, 1)


def feed_forward(nc, const, XN, w1, b1, w2, b2):
    M = FF // P
    with ExitStack() as ctx:
        m = Memory(nc, ctx, "ff")
        w1_, w2_, b1_, b2_ = m.sb("w1", [P, 2 * FF]), m.sb("w2", [P, M * D]), m.sb("b1", [P, M]), m.sb("b2", [P, D])
        rows, xT, hT, res = m.sb("rows", [P, GT * D]), m.sb("xT", [P, 2 * GN]), m.sb("hT", [P, M * GN]), m.sb("res", [P, D])
        p_t, p_y = ([m.ps(f"{n}{k}", [P, 512]) for k in range(2)] for n in ("p_t", "p_y"))
        p_h = [m.ps(f"p_h{k}", [P, 1024]) for k in range(2)]
        loaded, chain, staged, turned, kept, h_made, h_ready, made, taken = (
            m.sem(n) for n in ("loaded", "chain", "staged", "turned", "kept", "h_made", "h_ready", "made", "taken"))
        block = ctx.enter_context(nc.Block())

        @block.sync
        def _(sp):
            sp.dma_start(w1_[:, :], w1).then_inc(loaded, 16)
            sp.dma_start(w2_[:, :], w2).then_inc(loaded, 16)
            sp.dma_start(b1_[:, :], b1).then_inc(loaded, 16)
            sp.dma_start(b2_[:, :], row(b2)).then_inc(loaded, 16)

        @block.vector
        def _(dve):
            dve.wait_ge(loaded, 64)
            with dve.Fori(0, NG) as g:
                dve.wait_ge(turned, g * GT)
                dve.tensor_copy(rows[:, :], at(XN, g * GT * D, GT * D)).then_inc(staged, 1)
                t = Chain(dve, chain, g * 2 * GT)
                for n in range(GT):
                    i = g * GT + n
                    dve.wait_ge(made, i + 1)
                    t.step(dve.tensor_tensor(res[:, :], p_y[n % 2][:, 0:D], b2_[:, :], ALU.add))
                    dve.sem_inc(taken, 1)
                    t.step(dve.tensor_tensor(at(XN, i * D, D), at(XN, i * D, D), res[:, :], ALU.add))

        @block.scalar
        def _(act):
            act.wait_ge(loaded, 64)
            with act.Fori(0, NG) as g:
                act.wait_ge(h_made, g * M)
                for n in range(GT):
                    act.wait_ge(turned, g * GT + n + 1)
                    act.copy(xT[:, :].rearrange("p (c n) -> p c n", c=2)[:, :, n * P:(n + 1) * P],
                             p_t[n % 2][:, 0:D].rearrange("p (c n) -> p c n", c=2)).then_inc(kept, 1)
                act.wait_ge(made, g * GT)
                for q in range(M):
                    act.wait_ge(h_made, g * M + q + 1)
                    act.activation(hT[:, q * GN:(q + 1) * GN].rearrange("p (h n) -> p h n", h=2),
                                   p_h[q % 2][:, :].rearrange("p (h n) -> p h n", h=2)[:, :, 0:GH], ACT.Relu,
                                   bias=b1_[:, q:q + 1]).then_inc(h_ready, 1)

        @block.tensor
        def _(pe):
            pe.wait_ge(loaded, 64)
            with pe.Fori(0, NG) as g:
                pe.wait_ge(staged, g + 1)
                for n in range(GT):
                    pe.wait_ge(kept, g * GT + max(n - 1, 0))
                    for c in range(2):
                        mm = pe.transpose(p_t[n % 2][:, c * P:(c + 1) * P], rows[:, n * D + c * P:n * D + (c + 1) * P],
                                          const.ident[:, :])
                    mm.then_inc(turned, 1)
                pe.wait_ge(kept, (g + 1) * GT)
                for q in range(M):
                    pe.wait_ge(h_ready, g * M + max(q - 1, 0))
                    for s in range(2):
                        for c in range(2):
                            mm = pe.matmul(p_h[q % 2][:, s * 512:s * 512 + GH], w1_[:, c * FF + q * P:c * FF + (q + 1) * P],
                                           xT[:, c * GN + s * GH:c * GN + (s + 1) * GH], start=(c == 0), stop=(c == 1))
                    mm.then_inc(h_made, 1)
                pe.wait_ge(h_ready, (g + 1) * M)
                for n in range(GT):
                    pe.wait_ge(taken, g * GT + max(n - 1, 0))
                    for q in range(M):
                        mm = pe.matmul(p_y[n % 2][:, 0:D], hT[:, q * GN + n * P:q * GN + (n + 1) * P],
                                       w2_[:, q * D:(q + 1) * D], start=(q == 0), stop=(q == M - 1))
                    mm.then_inc(made, 1)


class Routing:

    def __init__(self, nc, ctx, tag, ne):
        m = Memory(nc, ctx, tag)
        self.ne, self.tag = ne, tag
        self.tiles = -(-((2 * N + ne * (P - 1)) // P) // 2) * 2
        self.gate = [m.sb(f"gate{k}", [P, NT]) for k in range(2)]
        self.slot = [m.sb(f"slot{k}", [P, NT], I32) for k in range(2)]
        self.expert = m.sb("expert", [1, self.tiles + 2], I32)

    def route(self, nc, const, XN, w, bias, rows_out):
        with ExitStack() as ctx:
            self.build(nc, Memory(nc, ctx, f"{self.tag}r"), ctx, const, XN, w, bias, rows_out)

    def build(self, nc, m, ctx, const, XN, w, bias, rows_out):
        ne, tj = self.ne, self.tiles
        W = NT * ne
        weight, bias_row = m.sb("weight", [P, 2 * ne]), m.sb("bias_row", [P, ne])
        rows, turned = m.sb("rows", [P, GT * D]), m.sb("turned", [P, GT * D])
        logit, work, cand, pos, ends = (m.sb(n, [P, W]) for n in ("logit", "work", "cand", "pos", "ends"))
        hot = [m.sb(f"hot{k}", [P, W]) for k in range(2)]
        first, second, total, pick, big = (m.sb(n, [P, NT]) for n in ("first", "second", "total", "pick", "big"))
        number, base, size = m.sb("number", [P, ne]), m.sb("base", [P, ne]), m.sb("size", [P, ne])
        size_i = m.sb("size_i", [P, ne], I32)
        scatter_i = [m.sb(f"scatter_i{k}", [P, NT], I32) for k in range(2)]
        place, mine = m.sb("place", [1, tj + 2]), m.sb("mine", [1, tj + 2])
        zero = m.sb("zero", [P, 8 * D])
        out_row = m.sb("out_row", [P, 2 * D])
        out_index = m.sb("out_index", [P, 4], I32)
        p_t = [m.ps(f"p_t{k}", [P, 512]) for k in range(2)]
        p_l, p_before, p_total = (m.ps(n, [P, 512]) for n in ("p_l", "p_before", "p_total"))
        loaded, made_c, staged, turning, kept, made, taken, chain, cleared, zeroed, exped, asked_exp, counted, ranked = (
            m.sem(n) for n in ("loaded", "made_c", "staged", "turning", "kept", "made", "taken", "chain", "cleared", "zeroed",
                               "exped", "asked_exp", "counted", "ranked"))
        slotted, row_ready, asked, index_put = (m.sem(n) for n in ("slotted", "row_ready", "asked", "index_put"))
        scattered = [m.sem(f"scattered{k}") for k in range(2)]
        block = ctx.enter_context(nc.Block())
        three = lambda b: b[:, :].rearrange("p (i e) -> p i e", e=ne)
        over = lambda b: b[:, :].unsqueeze(2).to_broadcast([P, NT, ne])
        numbers = number[:, :].unsqueeze(1).to_broadcast([P, NT, ne])
        slots = (tj + 2) * P
        fills = -(-(tj + 2) // 8)

        @block.sync
        def _(sp):
            sp.dma_start(weight[:, :], w).then_inc(loaded, 16)
            if bias is not None:
                sp.dma_start(bias_row[:, :], row(bias)).then_inc(loaded, 16)
            sp.wait_ge(cleared, 1)
            flat = rows_out.rearrange("(t p) d -> p t d", p=P)
            for f in range(fills):
                n = min(8, tj + 2 - 8 * f)
                sp.dma_start(flat[:, 8 * f:8 * f + n, :], zero[:, 0:n * D].rearrange("p (t d) -> p t d", d=D))\
                    .then_inc(zeroed, 16)

        @block.gpsimd
        def _(pool):
            pool.memset(zero[:, :], 0.0).then_inc(cleared, 1)
            pool.iota(number[:, :], pattern=[[1, ne]], base=0, channel_multiplier=0,
                      allow_small_or_imprecise_dtypes=True).then_inc(made_c, 1)
            pool.iota(place[:, :], pattern=[[1, tj + 2]], base=0, channel_multiplier=0,
                      allow_small_or_imprecise_dtypes=True).then_inc(made_c, 1)
            pool.wait_ge(zeroed, fills * 16)

            def scatter(i, k):
                pool.wait_ge(row_ready, i + 1)
                pool.sem_inc(asked, 1)
                for s in range(2):
                    pool.indirect_dma_start(
                        out=rows_out, out_offset=bass.IndirectOffsetOnAxis(ap=out_index[:, 2 * k + s:2 * k + s + 1], axis=0),
                        in_=out_row[:, k * D:(k + 1) * D], in_offset=None, bounds_check=slots - 1,
                        oob_is_err=False).then_inc(scattered[k], 16)

            with pool.Fori(0, NT // 2) as h:
                for k in range(2):
                    scatter(h * 2 + k, k)
            scatter(NT - 1, 0)
            pool.wait_ge(scattered[0], (NT // 2 + 1) * 32)
            pool.wait_ge(scattered[1], NT // 2 * 32)

        @block.vector
        def _(dve):
            ts, tt, stt = dve.tensor_scalar, dve.tensor_tensor, dve.scalar_tensor_tensor
            dve.wait_ge(loaded, 16 if bias is None else 32)
            with dve.Fori(0, NG) as g:
                dve.wait_ge(turning, g * GT)
                dve.tensor_copy(rows[:, :], at(XN, g * GT * D, GT * D)).then_inc(staged, 1)
                dve.wait_ge(made, g + 1)
                if bias is None:
                    ins = dve.tensor_copy(at(logit, g * GT * ne, GT * ne), p_l[:, 0:GT * ne])
                else:
                    ins = tt(at(logit, g * GT * ne, GT * ne).rearrange("p (i e) -> p i e", e=ne),
                             p_l[:, 0:GT * ne].rearrange("p (i e) -> p i e", e=ne),
                             bias_row[:, :].unsqueeze(1).to_broadcast([P, GT, ne]), ALU.add)
                ins.then_inc(taken, 1)
            c = Chain(dve, chain)
            dve.wait_ge(taken, NG)
            dve.wait_ge(made_c, 2)
            c.step(dve.tensor_copy(work[:, :], logit[:, :]))
            for k, top in enumerate((first, second)):
                c.step(dve.tensor_reduce(top[:, :], three(work), AX_X, ALU.max))
                c.step(tt(three(cand), three(work), over(top), ALU.is_equal))
                c.step(ts(cand[:, :], cand[:, :], -64.0, 64.0, ALU.mult, ALU.add))
                c.step(tt(three(cand), three(cand), numbers, ALU.add))
                c.step(dve.tensor_reduce(pick[:, :], three(cand), AX_X, ALU.min))
                c.step(tt(three(hot[k]), numbers, over(pick), ALU.is_equal))
                if k == 0:
                    c.step(stt(out=work[:, :], in0=hot[0][:, :], scalar=-1e30, in1=work[:, :], op0=ALU.mult, op1=ALU.add))
            c.step(tt(work[:, :], hot[0][:, :], hot[1][:, :], ALU.add))
            c.step(tt(three(work), three(work), over(const.valid), ALU.mult))
            dve.sem_inc(counted, 1)
            c.step(tt(second[:, :], second[:, :], first[:, :], ALU.subtract))
            c.step(tt(three(cand), three(logit), over(first), ALU.subtract))
            dve.sem_inc(asked_exp, 1)
            dve.wait_ge(exped, 2)
            if bias is None:
                c.step(dve.tensor_reduce(total[:, :], three(cand), AX_X, ALU.add))
                c.step(dve.reciprocal(total[:, :], total[:, :]))
                c.step(tt(second[:, :], second[:, :], total[:, :], ALU.mult))
                c.step(stt(out=first[:, :], in0=total[:, :], scalar=1e-9, in1=second[:, :], op0=ALU.add, op1=ALU.add))
                c.step(dve.reciprocal(first[:, :], first[:, :]))
                c.did(tt(self.gate[0][:, :], total[:, :], first[:, :], ALU.mult))
                c.step(tt(self.gate[1][:, :], second[:, :], first[:, :], ALU.mult))
            else:
                c.step(ts(first[:, :], second[:, :], 1.0, None, ALU.add))
                c.step(dve.reciprocal(self.gate[0][:, :], first[:, :]))
                c.step(tt(self.gate[1][:, :], second[:, :], self.gate[0][:, :], ALU.mult))
            dve.wait_ge(ranked, 2)
            c.did(dve.tensor_copy(pos[:, :], p_before[:, 0:W]))
            c.step(dve.tensor_copy(cand[:, :], p_total[:, 0:W]))
            for e in range(ne):
                c.did(dve.tensor_tensor_scan(three(ends)[:, :, e], const.ones[:, 0:NT], three(cand)[:, :, e], 0.0,
                                             ALU.mult, ALU.add))
            c.settle()
            c.did(ts(size[:, :], three(ends)[:, NT - 1, :], float(P - 1), None, ALU.add))
            c.step(tt(cand[:, :], ends[:, :], cand[:, :], ALU.subtract))
            c.did(tt(pos[:, :], pos[:, :], cand[:, :], ALU.add))
            c.step(dve.tensor_copy(size_i[:, :], size[:, :]))
            c.step(ts(size_i[:, :], size_i[:, :], 7, None, ALU.arith_shift_right))
            c.step(dve.tensor_copy(size[:, :], size_i[:, :]))
            c.step(dve.tensor_tensor_scan(base[:, :], const.ones[:, 0:ne], size[:, :], 0.0, ALU.mult, ALU.add))
            c.step(ts(mine[:, :], place[:, :], base[0:1, 0:1], None, ALU.is_ge))
            for e in range(1, ne - 1):
                c.step(stt(out=mine[:, :], in0=place[:, :], scalar=base[0:1, e:e + 1], in1=mine[:, :],
                           op0=ALU.is_ge, op1=ALU.add))
            c.did(dve.tensor_copy(self.expert[:, :], mine[:, :]))
            c.step(tt(base[:, :], base[:, :], size[:, :], ALU.subtract))
            c.step(ts(base[:, :], base[:, :], float(P), None, ALU.mult))
            c.step(tt(three(pos), three(pos), base[:, :].unsqueeze(1).to_broadcast([P, NT, ne]), ALU.add))
            c.step(ts(big[:, :], const.valid[:, :], -float(slots), float(slots), ALU.mult, ALU.add))
            for k in range(2):
                c.step(tt(cand[:, :], hot[k][:, :], pos[:, :], ALU.mult))
                c.step(dve.tensor_reduce(pick[:, :], three(cand), AX_X, ALU.add))
                c.step(tt(pick[:, :], pick[:, :], const.valid[:, :], ALU.mult))
                c.did(dve.tensor_copy(self.slot[k][:, :], pick[:, :]))
                c.step(tt(total[:, :], pick[:, :], big[:, :], ALU.add))
                c.step(dve.tensor_copy(scatter_i[k][:, :], total[:, :]))
            dve.sem_inc(slotted, 1)

        @block.scalar
        def _(act):
            with act.Fori(0, NG) as g:
                act.wait_ge(made, g)
                for n in range(GT):
                    act.wait_ge(turning, g * GT + n + 1)
                    act.copy(turned[:, n * D:(n + 1) * D], p_t[n % 2][:, 0:D]).then_inc(kept, 1)
            act.wait_ge(asked_exp, 1)
            act.activation(second[:, :], second[:, :], ACT.Exp).then_inc(exped, 1)
            act.activation(cand[:, :], cand[:, :], ACT.Exp).then_inc(exped, 1)
            act.wait_ge(slotted, 1)

            def put(i, k, turn):
                act.wait_ge(scattered[k], turn * 32)
                for s in range(2):
                    act.copy(out_index[:, 2 * k + s:2 * k + s + 1], scatter_i[s][:, bass.ds(i, 1)]).then_inc(index_put, 1)
                act.wait_ge(index_put, 2 * (i + 1))
                act.copy(out_row[:, k * D:(k + 1) * D], at(XN, i * D, D)).then_inc(row_ready, 1)

            with act.Fori(0, NT // 2) as h:
                for k in range(2):
                    put(h * 2 + k, k, h)
            put(NT - 1, 0, NT // 2)

        @block.tensor
        def _(pe):
            pe.wait_ge(loaded, 16 if bias is None else 32)
            with pe.Fori(0, NG) as g:
                pe.wait_ge(staged, g + 1)
                for n in range(GT):
                    pe.wait_ge(kept, g * GT + max(n - 1, 0))
                    for c in range(2):
                        mm = pe.transpose(p_t[n % 2][:, c * P:(c + 1) * P], rows[:, n * D + c * P:n * D + (c + 1) * P],
                                          const.ident[:, :])
                    mm.then_inc(turning, 1)
                pe.wait_ge(kept, (g + 1) * GT)
                pe.wait_ge(taken, g)
                for n in range(GT):
                    for c in range(2):
                        mm = pe.matmul(p_l[:, n * ne:(n + 1) * ne], turned[:, n * D + c * P:n * D + (c + 1) * P],
                                       weight[:, c * ne:(c + 1) * ne], start=(c == 0), stop=(c == 1))
                mm.then_inc(made, 1)
            pe.wait_ge(counted, 1)
            pe.matmul(p_before[:, 0:W], const.before[:, :], work[:, :], start=True, stop=True).then_inc(ranked, 1)
            pe.matmul(p_total[:, 0:W], const.ones[:, :], work[:, :], start=True, stop=True).then_inc(ranked, 1)


H0 = 682
U0 = H0 // 2
HC = 6
HK = H0 // HC + 1
E0, E1, H1 = 8, 16, 512


def gated_experts(nc, const, routing, rows_in, rows_out, w13, w2):
    with ExitStack() as ctx:
        m = Memory(nc, ctx, "ex0")
        up = m.sb("up", [P, E0 * 4 * H0])
        down = m.sb("down", [P, E0 * HC * D])
        x, xT, y = (m.sb(n, [P, 2 * D]) for n in ("x", "xT", "y"))
        act_h, h, hT = m.sb("act_h", [P, 2 * U0]), m.sb("h", [P, 2 * HC * HK]), m.sb("hT", [P, 2 * HC * P])
        p_x, p_y = m.ps("p_x", [P, 512]), m.ps("p_y", [P, 512])
        p_h = [m.ps(f"p_h{k}", [P, 1024]) for k in range(2)]
        p_t = m.ps("p_t", [P, 1024])
        loaded, x_turned, x_kept, u_made, silued, h_ready, h_turned, hT_kept, made, kept, padded = (
            m.sem(n) for n in ("loaded", "x_turned", "x_kept", "u_made", "silued", "h_ready", "h_turned", "hT_kept", "made",
                               "kept", "padded"))
        x_loaded = [m.sem(f"x_loaded{k}") for k in range(2)]
        stored = [m.sem(f"stored{k}") for k in range(2)]
        block = ctx.enter_context(nc.Block())
        steps = routing.tiles // 2

        @block.sync
        def _(sp):
            for k in range(2):
                sp.dma_start(x[:, k * D:(k + 1) * D], rows_in[k * P:(k + 1) * P, :]).then_inc(x_loaded[k], 16)
            for e in range(E0):
                sp.dma_start(up[:, e * 4 * H0:(e + 1) * 4 * H0], w13[:, e * 4 * H0:(e + 1) * 4 * H0]).then_inc(loaded, 16)
                sp.dma_start(down[0:HK, e * HC * D:(e + 1) * HC * D], w2[:, e * HC * D:(e + 1) * HC * D]).then_inc(loaded, 16)
            with sp.Fori(0, steps) as r:
                for k in range(2):
                    sp.wait_ge(x_turned, r + 1)
                    sp.dma_start(x[:, k * D:(k + 1) * D], rows_in[bass.ds((r * 2 + 2 + k) * P, P), :]).then_inc(x_loaded[k], 16)
                for k in range(2):
                    sp.wait_ge(kept, r * 2 + k + 1)
                    sp.dma_start(rows_out[bass.ds((r * 2 + k) * P, P), :], y[:, k * D:(k + 1) * D]).then_inc(stored[k], 16)
            for k in range(2):
                sp.wait_ge(stored[k], steps * 16)
                sp.wait_ge(x_loaded[k], (steps + 1) * 16)

        @block.tensor
        def _(pe):
            def turn_x(r):
                for k in range(2):
                    pe.wait_ge(x_loaded[k], r * 16 + 16)
                pe.wait_ge(x_kept, r)
                for q in range(4):
                    mm = pe.transpose(p_x[:, q * P:(q + 1) * P], x[:, q * P:(q + 1) * P], const.ident[:, :])
                mm.then_inc(x_turned, 1)

            turn_x(0)
            pe.wait_ge(loaded, 2 * E0 * 16)
            pe.wait_ge(padded, 1)
            with pe.Fori(0, steps) as r:
                ex = [pe.value_load(routing.expert[0:1, bass.ds(r * 2 + k, 1)], min_val=0, max_val=E0 - 1) for k in range(2)]

                def hidden(k, u):
                    pe.wait_ge(h_ready, r * 4 + max(2 * k + u - 1, 0))
                    for w in range(2):
                        for c in range(2):
                            mm = pe.matmul(p_h[u][:, w * 512:w * 512 + U0], xT[:, k * D + c * P:k * D + (c + 1) * P],
                                           at(up, ex[k] * (4 * H0) + ((c * 2 + w) * H0 + u * U0), U0),
                                           start=(c == 0), stop=(c == 1))
                    mm.then_inc(u_made, 1)

                def turn_h(k):
                    pe.wait_ge(h_ready, r * 4 + 2 * k + 2)
                    pe.wait_ge(hT_kept, (r * 2 + k) * 2)
                    for q in range(HC):
                        mm = pe.transpose(p_t[0:HK, (q // 3) * 512 + (q % 3) * P:(q // 3) * 512 + (q % 3 + 1) * P],
                                          h[:, (k * HC + q) * HK:(k * HC + q + 1) * HK], const.ident[:, :])
                    mm.then_inc(h_turned, 1)

                def out(k):
                    pe.wait_ge(kept, r * 2 + k)
                    for q in range(HC):
                        if q % 3 == 0:
                            pe.wait_ge(hT_kept, (r * 2 + k) * 2 + q // 3 + 1)
                        K = min(HK, H0 - q * HK)
                        mm = pe.matmul(p_y[:, 0:D], hT[0:K, (k * HC + q) * P:(k * HC + q + 1) * P],
                                       down[0:K, bass.ds(ex[k] * (HC * D) + q * D, D)], start=(q == 0), stop=(q == HC - 1))
                    mm.then_inc(made, 1)

                pe.wait_ge(x_kept, r + 1)
                hidden(0, 0)
                hidden(0, 1)
                hidden(1, 0)
                turn_h(0)
                hidden(1, 1)
                turn_x(r + 1)
                out(0)
                turn_h(1)
                out(1)

        @block.scalar
        def _(act):
            def keep_x(r):
                act.wait_ge(x_turned, r + 1)
                act.wait_ge(u_made, r * 4)
                act.copy(xT[:, :], p_x[:, :]).then_inc(x_kept, 1)

            def keep_y(r, k):
                act.wait_ge(made, r * 2 + k + 1)
                act.wait_ge(stored[k], r * 16)
                act.copy(y[:, k * D:(k + 1) * D], p_y[:, 0:D]).then_inc(kept, 1)

            keep_x(0)
            with act.Fori(0, steps) as r:
                for n in range(4):
                    u = n % 2
                    act.wait_ge(u_made, r * 4 + n + 1)
                    act.wait_ge(h_ready, r * 4 + max(n - 1, 0))
                    act.activation(act_h[:, u * U0:(u + 1) * U0], p_h[u][:, 0:U0], ACT.Silu).then_inc(silued, 1)
                keep_x(r + 1)
                keep_y(r, 0)
                keep_y(r, 1)

        @block.vector
        def _(dve):
            dve.memset(h[:, :], 0.0).then_inc(padded, 1)
            dve.wait_ge(padded, 1)
            with dve.Fori(0, steps) as r:
                def gate(k, u):
                    dve.wait_ge(silued, r * 4 + 2 * k + u + 1)
                    dve.wait_ge(h_turned, r * 2)
                    dve.tensor_tensor(h[:, k * HC * HK + u * U0:k * HC * HK + (u + 1) * U0], act_h[:, u * U0:(u + 1) * U0],
                                      p_h[u][:, 512:512 + U0], ALU.mult).then_inc(h_ready, 1)

                def keep_h(k):
                    dve.wait_ge(h_turned, r * 2 + k + 1)
                    dve.wait_ge(made, r * 2 + max(k - 1, 0))
                    for q in range(2):
                        dve.tensor_copy(hT[0:HK, (k * HC + 3 * q) * P:(k * HC + 3 * q + 3) * P],
                                        p_t[0:HK, q * 512:q * 512 + 3 * P]).then_inc(hT_kept, 1)

                gate(0, 0)
                gate(0, 1)
                gate(1, 0)
                keep_h(0)
                gate(1, 1)
                keep_h(1)


def relu_experts(nc, const, routing, rows_in, rows_out, w1, b1, w2, b2):
    HQ = H1 // P
    with ExitStack() as ctx:
        m = Memory(nc, ctx, "ex1")
        up, down = m.sb("up", [P, E1 * 2 * H1]), m.sb("down", [P, E1 * HQ * D])
        up_b, down_b = m.sb("up_b", [P, E1 * HQ]), m.sb("down_b", [P, E1 * D])
        x, xT, y = (m.sb(n, [P, 2 * D]) for n in ("x", "xT", "y"))
        h, hT = m.sb("h", [P, 2 * H1]), m.sb("hT", [P, 2 * H1])
        p_x, p_y = m.ps("p_x", [P, 512]), m.ps("p_y", [P, 512])
        p_h, p_t = ([m.ps(f"{n}{k}", [P, 512]) for k in range(2)] for n in ("p_h", "p_t"))
        loaded, x_turned, x_kept, h_made, h_kept, h_turned, h_ready, made, kept = (
            m.sem(n) for n in ("loaded", "x_turned", "x_kept", "h_made", "h_kept", "h_turned", "h_ready", "made", "kept"))
        x_loaded = [m.sem(f"x_loaded{k}") for k in range(2)]
        stored = [m.sem(f"stored{k}") for k in range(2)]
        block = ctx.enter_context(nc.Block())
        steps = routing.tiles // 2

        @block.sync
        def _(sp):
            for k in range(2):
                sp.dma_start(x[:, k * D:(k + 1) * D], rows_in[k * P:(k + 1) * P, :]).then_inc(x_loaded[k], 16)
            for e in range(0, E1, 4):
                sp.dma_start(up[:, e * 2 * H1:(e + 4) * 2 * H1], w1[:, e * 2 * H1:(e + 4) * 2 * H1]).then_inc(loaded, 16)
                sp.dma_start(down[:, e * HQ * D:(e + 4) * HQ * D], w2[:, e * HQ * D:(e + 4) * HQ * D]).then_inc(loaded, 16)
            sp.dma_start(up_b[:, :], b1).then_inc(loaded, 16)
            sp.dma_start(down_b[:, :], row(b2)).then_inc(loaded, 16)
            with sp.Fori(0, steps) as r:
                for k in range(2):
                    sp.wait_ge(x_turned, r + 1)
                    sp.dma_start(x[:, k * D:(k + 1) * D], rows_in[bass.ds((r * 2 + 2 + k) * P, P), :]).then_inc(x_loaded[k], 16)
                for k in range(2):
                    sp.wait_ge(kept, r * 2 + k + 1)
                    sp.dma_start(rows_out[bass.ds((r * 2 + k) * P, P), :], y[:, k * D:(k + 1) * D]).then_inc(stored[k], 16)
            for k in range(2):
                sp.wait_ge(stored[k], steps * 16)
                sp.wait_ge(x_loaded[k], (steps + 1) * 16)

        @block.tensor
        def _(pe):
            def turn_x(r):
                for k in range(2):
                    pe.wait_ge(x_loaded[k], r * 16 + 16)
                pe.wait_ge(x_kept, r)
                for q in range(4):
                    mm = pe.transpose(p_x[:, q * P:(q + 1) * P], x[:, q * P:(q + 1) * P], const.ident[:, :])
                mm.then_inc(x_turned, 1)

            turn_x(0)
            pe.wait_ge(loaded, 10 * 16)
            with pe.Fori(0, steps) as r:
                ex = [pe.value_load(routing.expert[0:1, bass.ds(r * 2 + k, 1)], min_val=0, max_val=E1 - 1) for k in range(2)]

                def hidden(k):
                    pe.wait_ge(h_kept, r * 2)
                    for c in range(2):
                        mm = pe.matmul(p_h[k][:, :], xT[:, k * D + c * P:k * D + (c + 1) * P],
                                       at(up, ex[k] * (2 * H1) + c * H1, H1), start=(c == 0), stop=(c == 1))
                    mm.then_inc(h_made, 1)

                def turn_h(k):
                    pe.wait_ge(h_kept, r * 2 + k + 1)
                    pe.wait_ge(h_ready, r * 2)
                    for q in range(HQ):
                        mm = pe.transpose(p_t[k][:, q * P:(q + 1) * P], h[:, k * H1 + q * P:k * H1 + (q + 1) * P],
                                          const.ident[:, :])
                    mm.then_inc(h_turned, 1)

                def out(k):
                    pe.wait_ge(kept, r * 2 + k)
                    pe.wait_ge(h_ready, r * 2 + k + 1)
                    for q in range(HQ):
                        mm = pe.matmul(p_y[:, 0:D], hT[:, k * H1 + q * P:k * H1 + (q + 1) * P],
                                       at(down, ex[k] * (HQ * D) + q * D, D), start=(q == 0), stop=(q == HQ - 1))
                    mm.then_inc(made, 1)

                pe.wait_ge(x_kept, r + 1)
                hidden(0)
                hidden(1)
                turn_h(0)
                turn_x(r + 1)
                turn_h(1)
                out(0)
                out(1)

        @block.scalar
        def _(act):
            def keep_x(r):
                act.wait_ge(x_turned, r + 1)
                act.wait_ge(h_made, r * 2)
                act.copy(xT[:, :], p_x[:, :]).then_inc(x_kept, 1)

            keep_x(0)
            with act.Fori(0, steps) as r:
                for k in range(2):
                    act.wait_ge(h_made, r * 2 + k + 1)
                    act.wait_ge(h_turned, r * 2)
                    act.copy(h[:, k * H1:(k + 1) * H1], p_h[k][:, :]).then_inc(h_kept, 1)
                keep_x(r + 1)

        @block.vector
        def _(dve):
            dve.wait_ge(loaded, 10 * 16)
            with dve.Fori(0, steps) as r:
                ex = [dve.value_load(routing.expert[0:1, bass.ds(r * 2 + k, 1)], min_val=0, max_val=E1 - 1) for k in range(2)]
                for k in range(2):
                    dve.wait_ge(h_turned, r * 2 + k + 1)
                    dve.wait_ge(made, r * 2)
                    for q in range(HQ):
                        ins = dve.tensor_scalar(hT[:, k * H1 + q * P:k * H1 + (q + 1) * P], p_t[k][:, q * P:(q + 1) * P],
                                                at(up_b, ex[k] * HQ + q, 1), 0.0, ALU.add, ALU.max)
                    ins.then_inc(h_ready, 1)
                for k in range(2):
                    dve.wait_ge(made, r * 2 + k + 1)
                    dve.wait_ge(stored[k], r * 16)
                    dve.tensor_tensor(y[:, k * D:(k + 1) * D], p_y[:, 0:D], at(down_b, ex[k] * D, D), ALU.add)\
                        .then_inc(kept, 1)


def combine(nc, routing, rows, to, base=None):
    with ExitStack() as ctx:
        m = Memory(nc, ctx, "comb" if base is None else "comb1")
        index = m.sb("index", [P, 2 * GT], I32)
        got = m.sb("got", [P, 2 * GT * D])
        loaded, chain, asked = m.sem("loaded"), m.sem("chain"), m.sem("asked")
        indexed = m.sem("indexed")
        gathered = [m.sem(f"gathered{k}") for k in range(2 * GT)]
        taken = m.sem("taken")
        block = ctx.enter_context(nc.Block())

        @block.sync
        def _(sp):
            if base is not None:
                sp.dma_start(to[:, :].rearrange("p (i d) -> p i d", d=D), base.rearrange("(i p) d -> p i d", p=P))\
                    .then_inc(loaded, 16)

        @block.scalar
        def _(act):
            with act.Fori(0, NG) as g:
                for n in range(GT):
                    for s in range(2):
                        act.wait_ge(gathered[2 * n + s], g * 16)
                        act.copy(index[:, 2 * n + s:2 * n + s + 1], routing.slot[s][:, bass.ds(g * GT + n, 1)])\
                            .then_inc(indexed, 1)

        @block.gpsimd
        def _(pool):
            with pool.Fori(0, NG) as g:
                for n in range(GT):
                    for s in range(2):
                        k = 2 * n + s
                        pool.wait_ge(indexed, g * 2 * GT + k + 1)
                        pool.wait_ge(taken, g * 2 * GT)
                        pool.sem_inc(asked, 1)
                        pool.indirect_dma_start(out=got[:, k * D:(k + 1) * D], out_offset=None, in_=rows,
                                                in_offset=bass.IndirectOffsetOnAxis(ap=index[:, k:k + 1], axis=0))\
                            .then_inc(gathered[k], 16)

        @block.vector
        def _(dve):
            if base is not None:
                dve.wait_ge(loaded, 16)
            with dve.Fori(0, NG) as g:
                for n in range(GT):
                    for s in range(2):
                        k = 2 * n + s
                        dve.wait_ge(gathered[k], g * 16 + 16)
                        dve.wait_ge(taken, g * 2 * GT + k)
                        y = at(to, (g * GT + n) * D, D)
                        dve.scalar_tensor_tensor(out=y, in0=got[:, k * D:(k + 1) * D],
                                                 scalar=routing.gate[s][:, bass.ds(g * GT + n, 1)], in1=y,
                                                 op0=ALU.mult, op1=ALU.add).then_inc(taken, 1)


def store_nodes(nc, X, out):
    with ExitStack() as ctx:
        m = Memory(nc, ctx, "store")
        stored = m.sem("stored")
        block = ctx.enter_context(nc.Block())
        full = (NT - 1) * P

        @block.sync
        def _(sp):
            sp.dma_start(out[0:full, :].rearrange("(i p) d -> p i d", p=P),
                         X[:, 0:(NT - 1) * D].rearrange("p (i d) -> p i d", d=D)).then_inc(stored, 16)
            sp.dma_start(out[full:N, :], X[0:NTAIL, (NT - 1) * D:NT * D]).then_inc(stored, 16)
            sp.wait_ge(stored, 32)


def build(nc, a, out):
    def scratch(name, rows):
        return nc.dram_tensor(name, [rows, D], F32).ap()

    with ExitStack() as ctx:
        const = Constants(nc, ctx)
        m = Memory(nc, ctx, "main")
        X = m.sb("X", [P, NT * D])
        load_nodes(nc, a["x"], X)
        norm_out, sumsq = m.sb("norm_out", [P, NT]), m.sb("sumsq", [P, NT])
        edges = Edges(nc, ctx, const, a["src"], a["dst"], a["edge_weight"], a["src_rows"],
                      a["dst_rows"], a["weight_rows"], norm_out)
        table0, table1, base1 = scratch("table0", NPAD), scratch("table1", NPAD), scratch("base1", NPAD)
        tiles0, tiles1 = (-(-((2 * N + e * (P - 1)) // P) // 2) * 2 for e in (E0, E1))
        in0, in1 = scratch("in0", (tiles0 + 2) * P), scratch("in1", (tiles1 + 2) * P)
        out0, out1 = scratch("out0", tiles0 * P), scratch("out1", tiles1 * P)

        with ExitStack() as part:
            p = Memory(nc, part, "layer0")
            XN = p.sb("XN", [P, NT * D])
            acc = p.sb("acc", [P, (NT + 1) * (D + DE + 1)])
            layer_norm(nc, "ln0", X, XN, table=table0, scale=norm_out, sumsq=sumsq)
            aggregate(nc, "agg0", edges, table0, acc, D + DE + 1, False, a["edge_rows"])
            scale, stats = p.sb("scale", [P, NT]), p.sb("stats", [P, CH0 * NG * 12])
            bn_scale, bn_shift = p.sb("bn_scale", [P, CH0]), p.sb("bn_shift", [P, CH0])
            YT = p.sb("YT", [P, CH0 * NPAD])
            map_scale(nc, sumsq, scale)
            qkv_channels(nc, const, XN, scale, a["m0_qkv"], YT, stats)
            batch_norm(nc, stats, a["m0_gamma"], a["m0_beta"], bn_scale, bn_shift)
            graph_and_mixer(nc, const, acc, X, YT, bn_scale, bn_shift, XN, sumsq, a["g0_w"], a["g0_b"],
                            a["m0_dw"], a["m0_pw"], a["m0_res"], a["m0_res_b"])
            add_mapped(nc, X, XN, sumsq)
        with ExitStack() as part:
            routing = Routing(nc, part, "route0", E0)
            with ExitStack() as inner:
                XN = Memory(nc, inner, "moe0x").sb("XN", [P, NT * D])
                layer_norm(nc, "ln1", X, XN)
                routing.route(nc, const, XN, a["f0_router"], None, in0)
            gated_experts(nc, const, routing, in0, out0, a["f0_w13"], a["f0_w2"])
            combine(nc, routing, out0, X)
        with ExitStack() as part:
            p = Memory(nc, part, "layer1")
            XN = p.sb("XN", [P, NT * D])
            acc = p.sb("acc", [P, (NT + 1) * D])
            layer_norm(nc, "ln2", X, XN, table=table1)
            aggregate(nc, "agg1", edges, table1, acc, D, True)
            XNT, kv = p.sb("XNT", [P, 2 * NPAD]), p.sb("kv", [P, 2 * (P + 1)])
            graph_and_kv(nc, const, acc, X, XN, XNT, kv, a["g1_w"], a["g1_b"], a["m1_kv"], a["m1_kv_b"])
            attend(nc, const, XN, XNT, kv, a["m1_q"], a["m1_q_b"], a["m1_o"], a["m1_o_b"])
            layer_norm(nc, "ln3", XN, XN, a["m1_g1"], a["m1_n1"])
            feed_forward(nc, const, XN, a["m1_w1"], a["m1_b1"], a["m1_w2"], a["m1_b2"])
            layer_norm(nc, "ln4", XN, X, a["m1_g2"], a["m1_n2"], add=X)
        with ExitStack() as part:
            routing = Routing(nc, part, "route1", E1)
            with ExitStack() as inner:
                XN = Memory(nc, inner, "moe1x").sb("XN", [P, NT * D])
                layer_norm(nc, "ln5", X, XN, table=base1)
                routing.route(nc, const, XN, a["f1_router"], a["f1_router_b"], in1)
            relu_experts(nc, const, routing, in1, out1, a["f1_w1"], a["f1_b1"], a["f1_w2"], a["f1_b2"])
            Y = Memory(nc, part, "last").sb("Y", [P, NT * D])
            combine(nc, routing, out1, Y, base1)
            layer_norm(nc, "ln6", Y, X, a["f1_gamma"], a["f1_beta"], add=X)
        store_nodes(nc, X, out)


def chunks(w):
    k, n = w.shape
    return w.reshape(k // P, P, n).transpose(1, 0, 2).reshape(P, -1)


def columns(v):
    return v.reshape(-1, P).T


def kernel(**inputs):
    import numpy as np
    import concourse.bacc as bacc
    from concourse.bass_utils import run_bass_kernel_spmd

    i = {k: np.asarray(v) for k, v in inputs.items()}

    def edge_columns(v, fill):
        return np.concatenate([v, np.full(EPAD - E, fill, v.dtype)]).reshape(ET, P).T

    def edge_tiles(v, fill):
        return np.concatenate([v, np.full(ECH * P * P - E, fill, v.dtype)]).reshape(ECH * P, P)

    spare = NPAD - 1
    a = {
        "x": i["x"],
        "src": edge_columns(i["src"], spare),
        "dst": edge_columns(i["dst"], spare),
        "edge_weight": edge_columns(i["edge_weight"], 0),
        "src_rows": edge_tiles(i["src"], spare),
        "dst_rows": edge_tiles(i["dst"], spare),
        "weight_rows": edge_tiles(i["edge_weight"], 0),
        "edge_rows": np.concatenate([i["edge_attr_64"], np.zeros((EPAD - E, DE), i["edge_attr_64"].dtype)]),
        "g0_w": i["L0_gnn_weight"], "g0_b": i["L0_gnn_bias"],
        "m0_qkv": chunks(i["L0_mix_w_qkv"][:, :, 2].T),
        "m0_gamma": columns(i["L0_mix_bn_gamma"]), "m0_beta": columns(i["L0_mix_bn_beta"]),
        "m0_dw": columns(i["L0_mix_w_dw"][:, 0, 2]),
        "m0_pw": i["L0_mix_w_pw"][:, :, 0].reshape(CH0, 4, 32, 32).transpose(1, 3, 0, 2).reshape(4, 32, -1),
        "m0_res": chunks(i["L0_mix_w_res"][:, :, 0].T), "m0_res_b": i["L0_mix_b_res"],
        "f0_router": chunks(i["L0_ffn_router_w"].T),
        "f0_w13": np.stack([i["L0_ffn_w1"], i["L0_ffn_w3"]]).reshape(2, E0, H0, 2, P).transpose(4, 1, 3, 0, 2).reshape(P, -1),
        "f0_w2": np.concatenate([i["L0_ffn_w2"].transpose(2, 0, 1), np.zeros((HC * HK - H0, E0, D), i["L0_ffn_w2"].dtype)])
                 .reshape(HC, HK, E0, D).transpose(1, 2, 0, 3).reshape(HK, -1),
        "g1_w": chunks(np.concatenate([i["L1_gnn_W1"].T, i["L1_gnn_W2"].T])),
        "g1_b": np.stack([i["L1_gnn_b1"], i["L1_gnn_b2"]]),
        "m1_kv": chunks(np.concatenate([i["L1_mix_Wk"], i["L1_mix_Wv"]], 1)),
        "m1_kv_b": np.concatenate([i["L1_mix_bk"], i["L1_mix_bv"]]),
        "m1_q": chunks(i["L1_mix_Wq"]), "m1_q_b": columns(i["L1_mix_bq"]),
        "m1_o": chunks(i["L1_mix_Wo"]), "m1_o_b": i["L1_mix_bo"],
        "m1_w1": chunks(i["L1_mix_W1"]), "m1_b1": columns(i["L1_mix_b1"]),
        "m1_w2": chunks(i["L1_mix_W2"]), "m1_b2": i["L1_mix_b2"],
        "m1_g1": i["L1_mix_ln1_g"], "m1_n1": i["L1_mix_ln1_b"],
        "m1_g2": i["L1_mix_ln2_g"], "m1_n2": i["L1_mix_ln2_b"],
        "f1_router": chunks(i["L1_ffn_gate_w"]), "f1_router_b": i["L1_ffn_gate_b"],
        "f1_w1": i["L1_ffn_w1"].reshape(E1, 2, P, H1).transpose(2, 0, 1, 3).reshape(P, -1),
        "f1_b1": i["L1_ffn_b1"].reshape(E1, H1 // P, P).transpose(2, 0, 1).reshape(P, -1),
        "f1_w2": i["L1_ffn_w2"].reshape(E1, H1 // P, P, D).transpose(2, 0, 1, 3).reshape(P, -1),
        "f1_b2": i["L1_ffn_b2"].reshape(-1),
        "f1_gamma": i["L1_ffn_gamma"], "f1_beta": i["L1_ffn_beta"],
    }
    a = {k: np.ascontiguousarray(v) for k, v in a.items()}
    nc = bacc.Bacc("TRN2", target_bir_lowering=False, num_devices=1)
    aps = {k: nc.dram_tensor(f"in_{k}", v.shape, mybir.dt.from_np(v.dtype), kind="ExternalInput").ap() for k, v in a.items()}
    out = nc.dram_tensor("out_0", (N, D), F32, kind="ExternalOutput").ap()
    build(nc, aps, out)
    r = run_bass_kernel_spmd(nc, [{f"in_{k}": v for k, v in a.items()}], core_ids=[0])
    return r.results[0]["out_0"]
```

```python
import math
from contextlib import ExitStack

import concourse.bass as bass
from concourse import mybir

F32 = mybir.dt.float32
I32 = mybir.dt.int32
BF16 = mybir.dt.bfloat16
ALU = mybir.AluOpType
ACT = mybir.ActivationFunctionType
AX_X = mybir.AxisListType.X

P = 128
N = 3125
D = 256
DE = 64
E = 50000
NT = -(-N // P)
NTAIL = N - (NT - 1) * P
NPAD = NT * P
ET = -(-E // P)
EPAD = ET * P
ECH = -(-ET // P)
SL = 8
SP = 4
PAIRS = -(-(ET + NT - 1) // SL) * SL
HB = 17
C0 = 768
CH0 = C0 // P
GRP = 16
GT = 5
NG = NT // GT
GN = GT * P
GH = GN // 2
FF = 1024
HEADS = 8
assert ET % HB == 0 and NT % GT == 0 and PAIRS // SL % 2 == 0
MAXNORM = 0.9999899864196777
ATANH_MAXNORM = 0.5 * math.log((1 + MAXNORM) / (1 - MAXNORM))
MINNORM = 1e-15


class Chain:

    def __init__(self, eng, sem, base=0):
        self.eng, self.sem, self.base, self.n = eng, sem, base, 0

    def did(self, ins):
        ins.then_inc(self.sem, 1)
        self.n += 1

    def settle(self):
        self.eng.wait_ge(self.sem, self.base + self.n)

    def step(self, ins):
        self.did(ins)
        self.settle()


class Memory:

    def __init__(self, nc, ctx, tag):
        self.nc, self.ctx, self.tag, self.sems = nc, ctx, tag, []

    def sb(self, name, shape, dt=F32):
        return self.ctx.enter_context(self.nc.sbuf_tensor(f"{self.tag}_{name}", shape, dt))

    def ps(self, name, shape, dt=F32):
        return self.ctx.enter_context(self.nc.psum_tensor(f"{self.tag}_{name}", shape, dt))

    def sem(self, name):
        if not self.sems:
            self.ctx.callback(self.release)
        self.sems.append(self.nc.alloc_semaphore(f"{self.tag}_{name}"))
        return self.sems[-1]

    def release(self):
        self.nc.clear_and_free_semaphores(self.sems)
        self.nc.all_engine_barrier(sem_only=True)


def row(v):
    return v.rearrange("(a n) -> a n", a=1).to_broadcast([P, v.shape[0]])


def at(buf, start, size):
    return buf[:, bass.ds(start, size)]


def refine(c, r, x, tmp):
    dve = c.eng
    c.step(dve.tensor_tensor(tmp[:, :], r[:, :], r[:, :], ALU.mult))
    c.step(dve.tensor_tensor(tmp[:, :], tmp[:, :], x[:, :], ALU.mult))
    c.step(dve.tensor_scalar(tmp[:, :], tmp[:, :], -0.5, 1.5, ALU.mult, ALU.add))
    c.step(dve.tensor_tensor(r[:, :], r[:, :], tmp[:, :], ALU.mult))


class Constants:

    def __init__(self, nc, ctx):
        m = Memory(nc, ctx, "const")
        self.ident = m.sb("ident", [P, P])
        self.before = m.sb("before", [P, P])
        self.ones = m.sb("ones", [P, P])
        self.valid = m.sb("valid", [P, NT])
        self.part = m.sb("part", [P, 1])
        self.zero = m.sb("zero", [P, D])
        built = m.sem("built")
        with nc.Block() as block:

            @block.gpsimd
            def _(pool):
                pool.memset(self.ident[:, :], 0.0).then_inc(built, 1)
                pool.memset(self.before[:, :], 0.0).then_inc(built, 1)
                pool.memset(self.ones[:, :], 1.0).then_inc(built, 1)
                pool.memset(self.valid[:, :], 1.0).then_inc(built, 1)
                pool.iota(self.part[:, :], pattern=[[0, 1]], base=0, channel_multiplier=1,
                          allow_small_or_imprecise_dtypes=True).then_inc(built, 1)
                pool.wait_ge(built, 5)
                pool.affine_select(out=self.ident[:, :], in_=self.ident[:, :], compare_op=ALU.not_equal, fill=1.0,
                                   base=0, pattern=[[-1, P]], channel_multiplier=1).then_inc(built, 1)
                pool.affine_select(out=self.before[:, :], in_=self.before[:, :], compare_op=ALU.is_ge, fill=1.0,
                                   base=0, pattern=[[-1, P]], channel_multiplier=1).then_inc(built, 1)
                pool.affine_select(out=self.valid[:, :], in_=self.valid[:, :], compare_op=ALU.is_ge, fill=0.0,
                                   base=N - 1, pattern=[[-P, NT]], channel_multiplier=-1).then_inc(built, 1)
                pool.memset(self.zero[:, :], 0.0).then_inc(built, 1)
                pool.wait_ge(built, 9)


def start_loads(nc, pieces, loaded):
    with nc.Block() as block:

        @block.sync
        def _(sp):
            for to, of in pieces:
                sp.dma_start(to, of).then_inc(loaded, 16)


def fills(slots):
    return -(-slots.shape[0] // (8 * P))


def start_clearing(nc, const, slots, cleared):
    flat = slots.rearrange("(t p) d -> p t d", p=P)
    tiles = slots.shape[0] // P
    start_loads(nc, [(flat[:, t:min(t + 8, tiles), :],
                      const.zero[:, :].unsqueeze(1).to_broadcast([P, min(8, tiles - t), D])) for t in range(0, tiles, 8)],
                cleared)


def load_nodes(nc, x, X):
    with ExitStack() as ctx:
        m = Memory(nc, ctx, "load")
        loaded, cleared = m.sem("loaded"), m.sem("cleared")
        block = ctx.enter_context(nc.Block())
        full = (NT - 1) * P

        @block.vector
        def _(dve):
            dve.memset(X[:, (NT - 1) * D:NT * D], 0.0).then_inc(cleared, 1)

        @block.sync
        def _(sp):
            sp.dma_start(X[:, 0:(NT - 1) * D].rearrange("p (i d) -> p i d", d=D),
                         x[0:full, :].rearrange("(i p) d -> p i d", p=P)).then_inc(loaded, 16)
            sp.wait_ge(cleared, 1)
            sp.dma_start(X[0:NTAIL, (NT - 1) * D:NT * D], x[full:N, :]).then_inc(loaded, 16)
            sp.wait_ge(loaded, 32)


def layer_norm(nc, tag, src, dst, gamma=None, beta=None, add=None, table=None, scale=None, sumsq=None, eps=1e-5):
    with ExitStack() as ctx:
        m = Memory(nc, ctx, tag)
        stats = m.sb("stats", [P, NT * 6])
        mean, var, tmp, rstd = (m.sb(n, [P, NT]) for n in ("mean", "var", "tmp", "rstd"))
        row_out = m.sb("row_out", [P, 2 * D])
        square = m.sb("square", [P, D])
        chain, var_ready, root_ready = m.sem("chain"), m.sem("var_ready"), m.sem("root_ready")
        tile_ready, rows_ready = m.sem("tile_ready"), m.sem("rows_ready")
        row_stored = [m.sem(f"row_stored{k}") for k in range(2)]
        squared = m.sem("squared")
        if gamma is not None:
            gamma_row, beta_row = m.sb("gamma_row", [P, D]), m.sb("beta_row", [P, D])
            shift = m.sb("shift", [P, NT])
            affine_loaded, shift_ready, normed = m.sem("affine_loaded"), m.sem("shift_ready"), m.sem("normed")
        block = ctx.enter_context(nc.Block())
        st = stats[:, :].rearrange("p (i s) -> p i s", s=6)

        @block.vector
        def _(dve):
            c = Chain(dve, chain)
            with dve.Fori(0, NG) as g:
                for n in range(GT):
                    dve.bn_stats(at(stats, (g * GT + n) * 6, 6), at(src, (g * GT + n) * D, D)).then_inc(chain, 1)
            c.n = NT
            c.settle()
            c.did(dve.tensor_tensor(mean[:, :], st[:, :, 1], st[:, :, 4], ALU.add))
            c.did(dve.tensor_tensor(var[:, :], st[:, :, 2], st[:, :, 5], ALU.add))
            c.step(dve.tensor_tensor(tmp[:, :], st[:, :, 1], st[:, :, 4], ALU.subtract))
            c.did(dve.tensor_scalar(mean[:, :], mean[:, :], 0.5, None, ALU.mult))
            c.step(dve.scalar_tensor_tensor(out=tmp[:, :], in0=tmp[:, :], scalar=0.25, in1=tmp[:, :],
                                            op0=ALU.mult, op1=ALU.mult))
            c.step(dve.scalar_tensor_tensor(out=var[:, :], in0=var[:, :], scalar=1.0 / D, in1=tmp[:, :],
                                            op0=ALU.mult, op1=ALU.add))
            dve.tensor_scalar(var[:, :], var[:, :], eps, None, ALU.add).then_inc(var_ready, 1)
            dve.wait_ge(root_ready, 1)
            c.step(dve.reciprocal(rstd[:, :], tmp[:, :]))
            refine(c, rstd, var, tmp)
            if gamma is None:
                with dve.Fori(0, NG) as g:
                    for n in range(GT):
                        i = g * GT + n
                        dve.tensor_scalar(at(dst, i * D, D), at(src, i * D, D), at(mean, i, 1), at(rstd, i, 1),
                                          ALU.subtract, ALU.mult).then_inc(tile_ready, 1)
            else:
                c.step(dve.scalar_tensor_tensor(out=shift[:, :], in0=mean[:, :], scalar=-1.0, in1=rstd[:, :],
                                                op0=ALU.mult, op1=ALU.mult))
                dve.sem_inc(shift_ready, 1)
                dve.wait_ge(affine_loaded, 32)
                base, per = c.n, 2 if add is None else 3
                group = lambda b, g: at(b, g * GT * D, GT * D).rearrange("p (n d) -> p n d", d=D)
                over = lambda r: r[:, :].unsqueeze(1).to_broadcast([P, GT, D])
                with dve.Fori(0, NG) as g:
                    t = Chain(dve, chain, g * per + base)
                    dve.wait_ge(normed, (g + 1) * GT)
                    y = group(src, g)
                    t.step(dve.tensor_tensor(y, y, over(gamma_row), ALU.mult))
                    if add is None:
                        t.did(dve.tensor_tensor(group(dst, g), y, over(beta_row), ALU.add))
                    else:
                        t.step(dve.tensor_tensor(y, y, over(beta_row), ALU.add))
                        t.did(dve.tensor_tensor(group(dst, g), y, group(add, g), ALU.add))
                    assert t.n == per

        @block.scalar
        def _(act):
            if gamma is not None:
                act.dma_start(gamma_row[:, :], row(gamma)).then_inc(affine_loaded, 16)
                act.dma_start(beta_row[:, :], row(beta)).then_inc(affine_loaded, 16)
            act.wait_ge(var_ready, 1)
            act.activation(tmp[:, :], var[:, :], ACT.Sqrt).then_inc(root_ready, 1)
            if gamma is not None:
                act.wait_ge(shift_ready, 1)
                with act.Fori(0, NG) as g:
                    for n in range(GT):
                        i = g * GT + n
                        x = at(src, i * D, D)
                        act.activation(x, x, ACT.Identity, scale=at(rstd, i, 1), bias=at(shift, i, 1)).then_inc(normed, 1)
            if sumsq is not None:
                with act.Fori(0, NT) as i:
                    act.wait_ge(tile_ready, i + 1)
                    act.wait_ge(squared, i)
                    act.activation(square[:, :], at(dst, i * D, D), ACT.Square,
                                   accum_out=at(sumsq, i, 1)).then_inc(squared, 1)
            if scale is not None:
                def put(i, k, turn):
                    act.wait_ge(tile_ready, i + 1)
                    act.wait_ge(row_stored[k], turn * 16)
                    act.activation(row_out[:, k * D:(k + 1) * D], at(dst, i * D, D), ACT.Copy,
                                   scale=at(scale, i, 1)).then_inc(rows_ready, 1)

                with act.Fori(0, NT // 2) as h:
                    for k in range(2):
                        put(h * 2 + k, k, h)
                put(NT - 1, 0, NT // 2)

        @block.sync
        def _(sp):
            if table is not None and scale is None:
                with sp.Fori(0, NG) as g:
                    sp.wait_ge(tile_ready, (g + 1) * GT)
                    sp.dma_start(table[bass.ds(g * GT * P, GT * P), :].rearrange("(n p) d -> p n d", p=P),
                                 at(dst, g * GT * D, GT * D).rearrange("p (n d) -> p n d", d=D)).then_inc(row_stored[0], 16)
                sp.wait_ge(row_stored[0], NG * 16)
            if scale is not None:
                def store(i, k):
                    sp.wait_ge(rows_ready, i + 1)
                    sp.dma_start(table[bass.ds(i * P, P), :], row_out[:, k * D:(k + 1) * D]).then_inc(row_stored[k], 16)

                with sp.Fori(0, NT // 2) as h:
                    for k in range(2):
                        store(h * 2 + k, k)
                store(NT - 1, 0)
                sp.wait_ge(row_stored[0], (NT // 2 + 1) * 16)
                sp.wait_ge(row_stored[1], NT // 2 * 16)


class Edges:

    def __init__(self, nc, ctx, const, src, dst, weight, src_rows, dst_rows, weight_rows, norm_out):
        m = Memory(nc, ctx, "edges")
        self.src = m.sb("src", [P, ET], I32)
        self.dst = m.sb("dst", [P, ET])
        self.weight = m.sb("weight", [P, ET])
        self.tile_of = m.sb("tile_of", [1, PAIRS], I32)
        self.window_of = m.sb("window_of", [1, PAIRS], I32)
        self.pairs = m.sb("pairs", [1, 1], I32)
        self.pair_src = m.sb("pair_src", [P, PAIRS], I32)
        self.pair_dst = m.sb("pair_dst", [P, PAIRS])
        self.pair_weight = m.sb("pair_weight", [P, PAIRS])
        with ExitStack() as inner:
            self.build(nc, Memory(nc, inner, "edgelist"), inner, const, src, dst, weight,
                       src_rows, dst_rows, weight_rows, norm_out)

    def build(self, nc, m, ctx, const, src, dst, weight, src_rows, dst_rows, weight_rows, norm_out):
        dst_i = m.sb("dst_i", [P, ET], I32)
        rows_i = m.sb("rows_i", [P, ECH * P], I32)
        rows_f = m.sb("rows_f", [P, ECH * P])
        rows_src_i, rows_src = m.sb("rows_src_i", [P, ECH * P], I32), m.sb("rows_src", [P, ECH * P])
        rows_weight = m.sb("rows_weight", [P, ECH * P])
        ends = m.sb("ends", [P, 2 * ECH])
        ends_i = m.sb("ends_i", [P, 2 * ECH], I32)
        count, start, stop = (m.sb(n, [P, ECH]) for n in ("count", "start", "stop"))
        picked = m.sb("picked", [P, 3 * ECH * P])
        totals = m.sb("totals", [P, ECH])
        tile_no, has = m.sb("tile_no", [P, ECH]), m.sb("has", [P, ECH])
        place = m.sb("place", [P, PAIRS])
        inside = m.sb("inside", [P, ECH * PAIRS])
        rest = m.sb("rest", [P, PAIRS])
        low_i, high_i = m.sb("low_i", [P, ET], I32), m.sb("high_i", [P, ET], I32)
        low, high = m.sb("low", [P, ET]), m.sb("high", [P, ET])
        node = m.sb("node", [P, P])
        is_low, is_high = m.sb("is_low", [P, HB * P], BF16), m.sb("is_high", [P, HB * NT], BF16)
        degree, root_of = m.sb("degree", [P, NT]), m.sb("root_of", [P, NT])
        p_sums = m.ps("p_sums", [P, 512])
        p_start, p_total, p_degree = p_sums[:, 0:ECH], p_sums[:, ECH:2 * ECH], p_sums[:, 128:128 + NT]
        p_list = m.ps("p_list", [P, 6 * 512])
        loaded, made, chain = m.sem("loaded"), m.sem("made"), m.sem("chain")
        counted, placed, chosen, listed = m.sem("counted"), m.sem("placed"), m.sem("chosen"), m.sem("listed")
        hot, summed, root, rooted = m.sem("hot"), m.sem("summed"), m.sem("root"), m.sem("rooted")
        block = ctx.enter_context(nc.Block())

        @block.sync
        def _(sp):
            for to, of in ((self.src, src), (dst_i, dst), (self.weight, weight)):
                sp.dma_start(to[:, :], of).then_inc(loaded, 16)
            for to, of in ((rows_i, dst_rows), (rows_src_i, src_rows), (rows_weight, weight_rows)):
                sp.dma_start(to[:, :].rearrange("p (c e) -> p c e", e=P),
                             of.rearrange("(c p) e -> p c e", p=P)).then_inc(loaded, 16)

        @block.gpsimd
        def _(pool):
            pool.iota(tile_no[:, :], pattern=[[P, ECH]], base=0, channel_multiplier=1,
                      allow_small_or_imprecise_dtypes=True).then_inc(made, 1)
            pool.iota(place[:, :], pattern=[[1, PAIRS]], base=0, channel_multiplier=0,
                      allow_small_or_imprecise_dtypes=True).then_inc(made, 1)
            pool.iota(node[:, :], pattern=[[1, P]], base=0, channel_multiplier=0,
                      allow_small_or_imprecise_dtypes=True).then_inc(made, 1)

        @block.vector
        def _(dve):
            c = Chain(dve, chain)
            dve.wait_ge(loaded, 96)
            dve.wait_ge(made, 3)
            c.did(dve.tensor_copy(rows_src[:, :], rows_src_i[:, :]))
            c.did(dve.tensor_copy(self.dst[:, :], dst_i[:, :]))
            c.did(dve.tensor_copy(rows_f[:, :], rows_i[:, :]))
            c.did(dve.tensor_scalar(low_i[:, :], self.src[:, :], P - 1, None, ALU.bitwise_and))
            c.step(dve.tensor_scalar(high_i[:, :], self.src[:, :], 7, None, ALU.arith_shift_right))
            c.did(dve.tensor_copy(low[:, :], low_i[:, :]))
            c.did(dve.tensor_copy(high[:, :], high_i[:, :]))
            r = rows_f[:, :].rearrange("p (c e) -> p c e", e=P)
            c.did(dve.tensor_reduce(ends[:, 0:ECH], r, AX_X, ALU.min))
            c.step(dve.tensor_reduce(ends[:, ECH:], r, AX_X, ALU.max))
            c.step(dve.tensor_copy(ends_i[:, :], ends[:, :]))
            c.step(dve.tensor_scalar(ends_i[:, :], ends_i[:, :], 7, None, ALU.arith_shift_right))
            c.step(dve.tensor_copy(ends[:, :], ends_i[:, :]))
            c.did(dve.tensor_scalar(has[:, :], tile_no[:, :], float(ET), None, ALU.is_lt))
            c.step(dve.scalar_tensor_tensor(out=count[:, :], in0=ends[:, ECH:], scalar=1.0, in1=ends[:, 0:ECH],
                                            op0=ALU.add, op1=ALU.subtract))
            dve.tensor_tensor(count[:, :], count[:, :], has[:, :], ALU.mult).then_inc(counted, 1)
            dve.wait_ge(placed, 2)
            c.did(dve.tensor_copy(start[:, :], p_start))
            c.step(dve.tensor_copy(totals[:, :], p_total))
            for k in range(1, ECH):
                c.step(dve.tensor_scalar(start[:, k:], start[:, k:], totals[:, k - 1:k], None, ALU.add))
            def wide(q):
                return picked[:, q * ECH * P:(q + 1) * ECH * P].rearrange("p (c m) -> p c m", m=P)

            def narrow(v):
                return v[:, :].unsqueeze(2).to_broadcast([P, ECH, P])

            c.did(dve.tensor_tensor(wide(0), narrow(ends[:, 0:ECH]), narrow(start), ALU.subtract))
            c.did(dve.tensor_copy(wide(1), narrow(tile_no)))
            c.did(dve.memset(picked[:, 2 * ECH * P:], 1.0))
            c.did(dve.tensor_tensor(stop[:, :], start[:, :], count[:, :], ALU.add))
            c.step(dve.tensor_reduce(totals[:, 0:1], totals[:, :], AX_X, ALU.add))
            c.did(dve.tensor_copy(self.pairs[:, :], totals[0:1, 0:1]))
            for k in range(ECH):
                own = inside[:, k * PAIRS:(k + 1) * PAIRS]
                c.step(dve.tensor_scalar(own, place[:, :], start[:, k:k + 1], None, ALU.is_ge))
                c.step(dve.scalar_tensor_tensor(out=own, in0=place[:, :], scalar=stop[:, k:k + 1], in1=own,
                                                op0=ALU.is_lt, op1=ALU.mult))
            dve.sem_inc(chosen, 1)
            dve.wait_ge(listed, 6)
            c.did(dve.tensor_copy(self.tile_of[:, :], p_list[0:1, 512:512 + PAIRS]))
            c.did(dve.tensor_copy(self.pair_src[:, :], p_list[:, 1536:1536 + PAIRS]))
            c.did(dve.tensor_copy(self.pair_weight[:, :], p_list[:, 2560:2560 + PAIRS]))
            c.did(dve.tensor_scalar(rest[:, :], p_list[:, 1024:1024 + PAIRS], -float(NT), float(NT), ALU.mult, ALU.add))
            w = place[:, :]
            c.step(dve.tensor_tensor(w, w, p_list[:, 0:PAIRS], ALU.add))
            c.step(dve.tensor_tensor(w, w, p_list[:, 1024:1024 + PAIRS], ALU.mult))
            c.step(dve.tensor_tensor(w, w, rest[:, :], ALU.add))
            c.did(dve.tensor_copy(self.window_of[:, :], place[0:1, :]))
            c.did(dve.scalar_tensor_tensor(out=self.pair_dst[:, :], in0=w, scalar=-float(P),
                                           in1=p_list[:, 2048:2048 + PAIRS], op0=ALU.mult, op1=ALU.add))
            c.step(dve.memset(degree[:, :], 0.0))
            base = c.n
            per = 3
            with dve.Fori(0, ET // HB) as i:
                t = Chain(dve, chain, i * per + base)
                dve.wait_ge(summed, i)
                t.did(dve.tensor_tensor(is_low[:, :].rearrange("p (t n) -> p t n", n=P),
                                        node[:, :].unsqueeze(1).to_broadcast([P, HB, P]),
                                        at(low, i * HB, HB).unsqueeze(2).to_broadcast([P, HB, P]), ALU.is_equal))
                t.step(dve.tensor_tensor(is_high[:, :].rearrange("p (t n) -> p t n", n=NT),
                                         node[:, 0:NT].unsqueeze(1).to_broadcast([P, HB, NT]),
                                         at(high, i * HB, HB).unsqueeze(2).to_broadcast([P, HB, NT]), ALU.is_equal))
                dve.sem_inc(hot, 1)
                dve.wait_ge(summed, i + 1)
                t.step(dve.tensor_tensor(degree[:, :], degree[:, :], p_degree, ALU.add))
                assert t.n == per
            c.n = base + ET // HB * per
            dve.tensor_scalar(degree[:, :], degree[:, :], 1.0, None, ALU.max).then_inc(root, 1)
            dve.wait_ge(rooted, 1)
            c.step(dve.reciprocal(norm_out[:, :], root_of[:, :]))
            refine(c, norm_out, degree, root_of)

        @block.scalar
        def _(act):
            act.wait_ge(root, 1)
            act.activation(root_of[:, :], degree[:, :], ACT.Sqrt).then_inc(rooted, 1)

        @block.tensor
        def _(pe):
            pe.wait_ge(counted, 1)
            pe.matmul(p_start, const.before[:, :], count[:, :], start=True, stop=True).then_inc(placed, 1)
            pe.matmul(p_total, const.ones[:, :], count[:, :], start=True, stop=True).then_inc(placed, 1)
            pe.wait_ge(chosen, 1)
            for q in range(6):
                of, o = ((picked, q * ECH * P), (rows_src, 0), (rows_f, 0), (rows_weight, 0))[max(q - 2, 0)]
                for k in range(ECH):
                    mm = pe.matmul(p_list[:, q * 512:q * 512 + PAIRS], of[:, o + k * P:o + (k + 1) * P],
                                   inside[:, k * PAIRS:(k + 1) * PAIRS], start=(k == 0), stop=(k == ECH - 1))
                mm.then_inc(listed, 1)
            with pe.Fori(0, ET // HB) as i:
                pe.wait_ge(hot, i + 1)
                for h in range(HB):
                    mm = pe.matmul(p_degree, is_low[:, h * P:(h + 1) * P], is_high[:, h * NT:(h + 1) * NT],
                                   start=(h == 0), stop=(h == HB - 1))
                mm.then_inc(summed, 1)


def aggregate(nc, tag, edges, table, acc, width, weighted, edge_rows=None):
    with ExitStack() as ctx:
        m = Memory(nc, ctx, tag)
        columns = m.sb("columns", [P, (NT + 1) * P])
        index = m.sb("index", [P, 2 * SL], I32)
        message = m.sb("message", [P, 2 * SL * width])
        onehot = m.sb("onehot", [P, 2 * SL * P])
        partial = [m.ps(f"partial{k}", [P, width]) for k in range(SP)]
        ready, chain = m.sem("ready"), m.sem("chain")
        indexed, marked = m.sem("indexed"), m.sem("marked")
        gathered, featured = ([m.sem(f"{n}{k}") for k in range(2 * SL)] for n in ("gathered", "featured"))
        used, added = ([m.sem(f"{n}{k}") for k in range(SL)] for n in ("used", "added"))
        weighed = m.sem("weighed")
        all_indexed, all_gathered, all_featured, all_marked, all_used, all_added, all_chain = (
            m.sem(f"all_{n}") for n in ("indexed", "gathered", "featured", "marked", "used", "added", "chain"))
        tile_taken, tile_begun, asked = m.sem("tile_taken"), m.sem("tile_begun"), m.sem("asked")
        block = ctx.enter_context(nc.Block())
        rounds = PAIRS // SL

        def msg(k):
            return message[:, k * width:(k + 1) * width]

        def pair_count(eng):
            return eng.value_load(edges.pairs[0:1, 0:1], min_val=0, max_val=ET * NT)

        def tile_of(eng, j):
            return eng.value_load(edges.tile_of[0:1, bass.ds(j, 1)], min_val=0, max_val=ET - 1)

        def window_of(eng, j):
            return eng.value_load(edges.window_of[0:1, bass.ds(j, 1)], min_val=0, max_val=NT)

        def gather(pool, k, i, sem):
            pool.sem_inc(asked, 1)
            pool.indirect_dma_start(out=message[:, k * width:k * width + D], out_offset=None, in_=table,
                                    in_offset=bass.IndirectOffsetOnAxis(ap=index[:, i:i + 1], axis=0)).then_inc(sem, 16)

        @block.gpsimd
        def _(pool):
            pool.iota(columns[:, :], pattern=[[1, (NT + 1) * P]], base=0, channel_multiplier=0,
                      allow_small_or_imprecise_dtypes=True).then_inc(ready, 1)
            pool.wait_ge(ready, 2)
            pairs = pair_count(pool)
            with pool.If(pairs <= PAIRS):
                for h in range(2):
                    pool.wait_ge(indexed, h + 1)
                    for k in range(SL):
                        gather(pool, h * SL + k, h * SL + k, gathered[h * SL + k])
                with pool.Fori(1, rounds // 2) as q:
                    for h in range(2):
                        r = q * 2 + h
                        pool.wait_ge(indexed, r + 1)
                        for k in range(SL):
                            pool.wait_ge(used[k], r - 1)
                            gather(pool, h * SL + k, h * SL + k, gathered[h * SL + k])
            with pool.Else():
                with pool.Fori(0, ET) as t:
                    pool.wait_ge(all_indexed, t + 1)
                    gather(pool, 0, 0, all_gathered)

        @block.scalar
        def _(act):
            def pick(h, r):
                return act.copy(index[:, h * SL:(h + 1) * SL], edges.pair_src[:, bass.ds(r * SL, SL)])

            pairs = pair_count(act)
            with act.If(pairs <= PAIRS):
                def weigh(h, r):
                    act.wait_ge(marked, r + 1)
                    for k in range(SL):
                        hot = onehot[:, (h * SL + k) * P:(h * SL + k + 1) * P]
                        ins = act.activation(hot, hot, ACT.Copy, scale=edges.pair_weight[:, bass.ds(r * SL + k, 1)])
                    ins.then_inc(weighed, 1)

                for h in range(2):
                    pick(h, h).then_inc(indexed, 1)
                if weighted:
                    for h in range(2):
                        weigh(h, h)
                with act.Fori(1, rounds // 2) as q:
                    for h in range(2):
                        r = q * 2 + h
                        act.wait_ge(used[SL - 1], r - 1)
                        pick(h, r).then_inc(indexed, 1)
                        if weighted:
                            weigh(h, r)
            with act.Else():
                with act.Fori(0, ET) as t:
                    act.wait_ge(tile_taken, t)
                    act.copy(index[:, 0:1], edges.src[:, bass.ds(t, 1)]).then_inc(all_indexed, 1)

        @block.sync
        def _(sp):
            if edge_rows is not None:
                def features(k, t):
                    return sp.dma_start(message[:, k * width + D:k * width + D + DE], edge_rows[bass.ds(t * P, P), :])

                pairs = pair_count(sp)
                sp.wait_ge(ready, 2)
                with sp.If(pairs <= PAIRS):
                    for j in range(2 * SL):
                        features(j, tile_of(sp, j)).then_inc(featured[j], 16)
                    with sp.Fori(1, rounds // 2) as q:
                        for h in range(2):
                            r = q * 2 + h
                            for k in range(SL):
                                t = tile_of(sp, r * SL + k)
                                sp.wait_ge(used[k], r - 1)
                                features(h * SL + k, t).then_inc(featured[h * SL + k], 16)
                with sp.Else():
                    with sp.Fori(0, ET) as t:
                        sp.wait_ge(tile_taken, t)
                        features(0, t).then_inc(all_featured, 16)

        @block.vector
        def _(dve):
            c = Chain(dve, chain)
            c.did(dve.memset(acc[:, :], 0.0))
            c.step(dve.memset(message[:, :], 1.0))
            dve.sem_inc(ready, 1)
            dve.wait_ge(ready, 2)

            def mark_round(h, r):
                dve.tensor_tensor(onehot[:, h * SL * P:(h + 1) * SL * P].rearrange("p (k n) -> p k n", n=P),
                                  columns[:, 0:P].unsqueeze(1).to_broadcast([P, SL, P]),
                                  edges.pair_dst[:, bass.ds(r * SL, SL)].unsqueeze(2).to_broadcast([P, SL, P]),
                                  ALU.is_equal).then_inc(marked, 1)

            def mark(k, t, w):
                hot = onehot[:, k * P:(k + 1) * P]
                col = columns[:, bass.ds(w * P, P)]
                if weighted:
                    return dve.tensor_scalar(hot, col, edges.dst[:, bass.ds(t, 1)], edges.weight[:, bass.ds(t, 1)],
                                             ALU.is_equal, ALU.mult)
                return dve.tensor_scalar(hot, col, edges.dst[:, bass.ds(t, 1)], None, ALU.is_equal)

            def add(k, w):
                to = acc[:, bass.ds(w * width, width)]
                return dve.tensor_tensor(to, to, partial[k % SP][:, :], ALU.add)

            pairs = pair_count(dve)
            with dve.If(pairs <= PAIRS):
                def add_round(r):
                    for k in range(SL):
                        w = window_of(dve, r * SL + k)
                        dve.wait_ge(used[k], r + 1)
                        if k:
                            dve.wait_ge(added[k - 1], r + 1)
                        else:
                            dve.wait_ge(added[SL - 1], r)
                        add(k, w).then_inc(added[k], 1)

                mark_round(0, 0)
                with dve.Fori(0, rounds // 2 - 1) as q:
                    for h in range(2):
                        mark_round(1 - h, q * 2 + h + 1)
                        add_round(q * 2 + h)
                mark_round(1, rounds - 1)
                add_round(rounds - 2)
                add_round(rounds - 1)
            with dve.Else():
                with dve.Fori(0, ET) as t:
                    with dve.Fori(0, NT) as w:
                        j = t * NT + w
                        dve.wait_ge(all_used, j)
                        mark(0, t, w).then_inc(all_marked, 1)
                        dve.wait_ge(all_used, j + 1)
                        dve.wait_ge(all_added, j)
                        add(0, w).then_inc(all_added, 1)

        @block.tensor
        def _(pe):
            def product(k, h=0):
                hot = onehot[:, (h * SL + k) * P:(h * SL + k + 1) * P]
                return pe.matmul(partial[k % SP][:, :], hot, msg(h * SL + k), start=True, stop=True)

            pairs = pair_count(pe)
            with pe.If(pairs <= PAIRS):
                with pe.Fori(0, rounds // 2) as q:
                    for h in range(2):
                        r = q * 2 + h
                        pe.wait_ge(weighed if weighted else marked, r + 1)
                        for k in range(SL):
                            pe.wait_ge(gathered[h * SL + k], (q + 1) * 16)
                            if edge_rows is not None:
                                pe.wait_ge(featured[h * SL + k], (q + 1) * 16)
                            if k < SP:
                                pe.wait_ge(added[k + SL - SP], r)
                            else:
                                pe.wait_ge(added[k - SP], r + 1)
                            product(k, h).then_inc(used[k], 1)
            with pe.Else():
                with pe.Fori(0, ET) as t:
                    pe.wait_ge(all_gathered, (t + 1) * 16)
                    if edge_rows is not None:
                        pe.wait_ge(all_featured, (t + 1) * 16)
                    pe.sem_inc(tile_begun, 1)
                    with pe.Fori(0, NT) as w:
                        j = t * NT + w
                        pe.wait_ge(all_marked, j + 1)
                        pe.wait_ge(all_added, j)
                        product(0).then_inc(all_used, 1)
                    pe.wait_ge(all_used, (t + 1) * NT)
                    pe.sem_inc(tile_taken, 1)


def map_scale(nc, sumsq, scale):
    with ExitStack() as ctx:
        m = Memory(nc, ctx, "map")
        norm, inv, short, sq, poly, up, down, tmp = (
            m.sb(n, [P, NT]) for n in ("norm", "inv", "short", "sq", "poly", "up", "down", "tmp"))
        chain, floored, rooted, argued, logged = (m.sem(n) for n in ("chain", "floored", "rooted", "argued", "logged"))
        block = ctx.enter_context(nc.Block())

        @block.vector
        def _(dve):
            c = Chain(dve, chain)
            ts, tt = dve.tensor_scalar, dve.tensor_tensor
            c.step(ts(sq[:, :], sumsq[:, :], MINNORM * MINNORM, None, ALU.max))
            dve.sem_inc(floored, 1)
            dve.wait_ge(rooted, 1)
            c.step(dve.reciprocal(inv[:, :], norm[:, :]))
            refine(c, inv, sq, tmp)
            c.step(tt(norm[:, :], sq[:, :], inv[:, :], ALU.mult))
            c.step(ts(short[:, :], norm[:, :], MAXNORM, None, ALU.min))
            c.did(ts(up[:, :], short[:, :], 1.0, None, ALU.add))
            c.step(ts(down[:, :], short[:, :], -1.0, 1.0, ALU.mult, ALU.add))
            dve.sem_inc(argued, 1)
            c.step(tt(sq[:, :], short[:, :], short[:, :], ALU.mult))
            c.step(ts(poly[:, :], sq[:, :], 1.0 / 17, 1.0 / 15, ALU.mult, ALU.add))
            for d in (13, 11, 9, 7, 5, 3, 1):
                c.step(tt(poly[:, :], poly[:, :], sq[:, :], ALU.mult))
                c.step(ts(poly[:, :], poly[:, :], 1.0 / d, None, ALU.add))
            c.step(tt(poly[:, :], poly[:, :], short[:, :], ALU.mult))
            dve.wait_ge(logged, 2)
            c.step(tt(up[:, :], up[:, :], down[:, :], ALU.subtract))
            c.step(ts(up[:, :], up[:, :], 0.5, None, ALU.mult))
            c.step(ts(tmp[:, :], short[:, :], 0.3, None, ALU.is_gt))
            c.step(tt(up[:, :], up[:, :], tmp[:, :], ALU.mult))
            c.step(ts(tmp[:, :], tmp[:, :], -1.0, 1.0, ALU.mult, ALU.add))
            c.step(tt(poly[:, :], poly[:, :], tmp[:, :], ALU.mult))
            c.step(tt(poly[:, :], poly[:, :], up[:, :], ALU.add))
            c.step(tt(scale[:, :], poly[:, :], inv[:, :], ALU.mult))

        @block.scalar
        def _(act):
            act.wait_ge(floored, 1)
            act.activation(norm[:, :], sq[:, :], ACT.Sqrt).then_inc(rooted, 1)
            act.wait_ge(argued, 1)
            for x in (up, down):
                act.activation(x[:, :], x[:, :], ACT.Ln).then_inc(logged, 1)


def qkv_channels(nc, const, XN, scale, w, YT, stats):
    with ExitStack() as ctx:
        m = Memory(nc, ctx, "qkv")
        weight = m.sb("weight", [P, 2 * C0])
        rows = m.sb("rows", [P, GT * D])
        turned = m.sb("turned", [P, 2 * GN])
        p_turn = [m.ps(f"p_turn{k}", [P, 512]) for k in range(2)]
        p_out = [m.ps(f"p_out{k}", [P, 1024]) for k in range(2)]
        loaded, scaled, turning, kept, made, stored = (
            m.sem(n) for n in ("loaded", "scaled", "turning", "kept", "made", "stored"))
        block = ctx.enter_context(nc.Block())

        @block.sync
        def _(sp):
            sp.dma_start(weight[:, :], w).then_inc(loaded, 16)

        @block.vector
        def _(dve):
            with dve.Fori(0, NG) as g:
                dve.wait_ge(turning, g * GT)
                for t in range(GT):
                    dve.tensor_scalar(rows[:, t * D:(t + 1) * D], at(XN, (g * GT + t) * D, D),
                                      at(scale, g * GT + t, 1), None, ALU.mult).then_inc(scaled, 1)
                for q in range(CH0):
                    dve.wait_ge(stored, g * CH0 + q + 1)
                    for h in range(2):
                        dve.bn_stats(at(stats, (q * NG + g) * 12 + h * 6, 6), at(YT, q * NPAD + g * GN + h * GH, GH))

        @block.tensor
        def _(pe):
            pe.wait_ge(loaded, 16)
            with pe.Fori(0, NG) as g:
                for t in range(GT):
                    pe.wait_ge(scaled, g * GT + t + 1)
                    pe.wait_ge(kept, g * GT + max(t - 1, 0)) if t else pe.wait_ge(kept, g * GT)
                    for c in range(2):
                        mm = pe.transpose(p_turn[t % 2][:, c * P:(c + 1) * P],
                                          rows[:, t * D + c * P:t * D + (c + 1) * P], const.ident[:, :])
                    mm.then_inc(turning, 1)
                pe.wait_ge(kept, (g + 1) * GT)
                for q in range(CH0):
                    if q < 2:
                        pe.wait_ge(stored, g * CH0)
                    else:
                        pe.wait_ge(stored, g * CH0 + q - 1)
                    for h in range(2):
                        for c in range(2):
                            mm = pe.matmul(p_out[q % 2][:, h * 512:h * 512 + GH],
                                           weight[:, c * C0 + q * P:c * C0 + (q + 1) * P],
                                           turned[:, c * GN + h * GH:c * GN + (h + 1) * GH], start=(c == 0), stop=(c == 1))
                    mm.then_inc(made, 1)

        @block.scalar
        def _(act):
            with act.Fori(0, NG) as g:
                act.wait_ge(made, g * CH0)
                for t in range(GT):
                    act.wait_ge(turning, g * GT + t + 1)
                    act.copy(turned[:, :].rearrange("p (c n) -> p c n", c=2)[:, :, t * P:(t + 1) * P],
                             p_turn[t % 2][:, 0:D].rearrange("p (c n) -> p c n", c=2)).then_inc(kept, 1)
                for q in range(CH0):
                    act.wait_ge(made, g * CH0 + q + 1)
                    act.copy(at(YT, q * NPAD + g * GN, GN).rearrange("p (h n) -> p h n", h=2),
                             p_out[q % 2][:, :].rearrange("p (h n) -> p h n", h=2)[:, :, 0:GH]).then_inc(stored, 1)


def batch_norm(nc, stats, gamma, beta, bn_scale, bn_shift):
    with ExitStack() as ctx:
        m = Memory(nc, ctx, "bn")
        gamma_c, beta_c = m.sb("gamma_c", [P, CH0]), m.sb("beta_c", [P, CH0])
        pair = m.sb("pair", [P, 2 * CH0])
        mean, var, root, tmp = (m.sb(n, [P, CH0]) for n in ("mean", "var", "root", "tmp"))
        loaded, chain, ready, rooted = (m.sem(n) for n in ("loaded", "chain", "ready", "rooted"))
        block = ctx.enter_context(nc.Block())

        @block.sync
        def _(sp):
            sp.dma_start(gamma_c[:, :], gamma).then_inc(loaded, 16)
            sp.dma_start(beta_c[:, :], beta).then_inc(loaded, 16)

        @block.vector
        def _(dve):
            c = Chain(dve, chain)
            for q in range(CH0):
                c.did(dve.bn_aggr(pair[:, 2 * q:2 * q + 2], stats[:, q * NG * 12:(q + 1) * NG * 12]))
            c.settle()
            pv = pair[:, :].rearrange("p (q s) -> p q s", s=2)
            c.did(dve.tensor_scalar(mean[:, :], pv[:, :, 0], NPAD / N, None, ALU.mult))
            c.step(dve.scalar_tensor_tensor(out=tmp[:, :], in0=pv[:, :, 0], scalar=-(NPAD * (NPAD - N)) / (N * N),
                                            in1=pv[:, :, 0], op0=ALU.mult, op1=ALU.mult))
            c.step(dve.scalar_tensor_tensor(out=var[:, :], in0=pv[:, :, 1], scalar=NPAD / N, in1=tmp[:, :],
                                            op0=ALU.mult, op1=ALU.add))
            c.step(dve.tensor_scalar(var[:, :], var[:, :], 1e-5, None, ALU.add))
            dve.sem_inc(ready, 1)
            dve.wait_ge(rooted, 1)
            c.step(dve.reciprocal(bn_scale[:, :], root[:, :]))
            refine(c, bn_scale, var, tmp)
            dve.wait_ge(loaded, 32)
            c.step(dve.tensor_tensor(bn_scale[:, :], bn_scale[:, :], gamma_c[:, :], ALU.mult))
            c.step(dve.tensor_tensor(tmp[:, :], mean[:, :], bn_scale[:, :], ALU.mult))
            c.step(dve.tensor_tensor(bn_shift[:, :], beta_c[:, :], tmp[:, :], ALU.subtract))

        @block.scalar
        def _(act):
            act.wait_ge(ready, 1)
            act.activation(root[:, :], var[:, :], ACT.Sqrt).then_inc(rooted, 1)


def graph_and_mixer(nc, const, acc, X, YT, bn_scale, bn_shift, FT, sumsq, gw, gbias, w_dw, w_pw, w_res, b_res):
    AW = D + DE + 1
    with ExitStack() as ctx:
        m = Memory(nc, ctx, "mix")
        g_w = m.sb("g_w", [P, 3 * D])
        g_b, r_b = m.sb("g_b", [P, D]), m.sb("r_b", [P, D])
        taps = m.sb("taps", [P, CH0])
        blocks = m.sb("blocks", [P, C0])
        r_w = m.sb("r_w", [P, 4 * D])
        norm_in, deg, dtmp = m.sb("norm_in", [P, NT]), m.sb("deg", [P, NT]), m.sb("dtmp", [P, NT])
        rT = m.sb("rT", [P, C0])
        agg = m.sb("agg", [P, D + DE])
        aggT = m.sb("aggT", [P, 3 * P])
        square = m.sb("square", [P, C0])
        sums, norms = m.sb("sums", [P, 4]), m.sb("norms", [P, 4])
        size, least, inv, a, b = (m.sb(n, [P, 1]) for n in ("size", "least", "inv", "a", "b"))
        k_sum = m.sb("k_sum", [P, GRP])
        kr = m.sb("kr", [P, 2 * 512])
        den, prod, prodT = m.sb("den", [P, 512]), m.sb("prod", [P, 512]), m.sb("prodT", [P, 512])
        g_out = m.sb("g_out", [P, D])
        b3, prod_sums, c_b3, c_tmp = (m.sb(n, [P, NT]) for n in ("b3", "prod_sums", "c_b3", "c_tmp"))
        cat = [m.ps(f"cat{k}", [P, 2 * C0]) for k in range(2)]
        p_graph, p_mix = m.ps("p_graph", [P, 512]), m.ps("p_mix", [P, 512])
        loaded, cleared, chain, dwed = m.sem("loaded"), m.sem("cleared"), m.sem("chain"), m.sem("dwed")
        deg_ready, deg_rooted, act_chain = m.sem("deg_ready"), m.sem("deg_rooted"), m.sem("act_chain")
        relued, rT_staged, catted, cat_free, k_made = (
            m.sem(n) for n in ("relued", "rT_staged", "catted", "cat_free", "k_made"))
        staged, agg_turned, agg_kept, gnn_done, gnn_taken = (
            m.sem(n) for n in ("staged", "agg_turned", "agg_kept", "gnn_done", "gnn_taken"))
        prod_ready, prod_turned, prod_kept, prod_squared, res_done, res_kept = (
            m.sem(n) for n in ("prod_ready", "prod_turned", "prod_kept", "prod_squared", "res_done", "res_kept"))
        sums_ready, prods_rooted, ft_ready = m.sem("sums_ready"), m.sem("prods_rooted"), m.sem("ft_ready")
        block = ctx.enter_context(nc.Block())

        def parts(buf, n):
            return buf[:, :].rearrange("p (g c) -> p g c", c=96)[:, :, 32 * n:32 * n + 32]

        @block.sync
        def _(sp):
            sp.wait_ge(cleared, 2)
            sp.dma_start(g_w[:, 0:2 * D].rearrange("p (k d) -> p k d", d=D),
                         gw[0:2 * P, :].rearrange("(k p) d -> p k d", p=P)).then_inc(loaded, 16)
            sp.dma_start(g_w[0:DE, 2 * D:3 * D], gw[2 * P:, :]).then_inc(loaded, 16)
            sp.dma_start(g_b[:, :], row(gbias)).then_inc(loaded, 16)
            sp.dma_start(r_b[:, :], row(b_res)).then_inc(loaded, 16)
            sp.dma_start(taps[:, :], w_dw).then_inc(loaded, 16)
            sp.dma_start(r_w[:, :], w_res).then_inc(loaded, 16)
            for b_ in range(4):
                sp.dma_start(blocks[32 * b_:32 * b_ + 32, :].rearrange("i (q b o) -> i q b o", b=4, o=32)[:, :, b_, :],
                             w_pw[b_, :, :].rearrange("i (q o) -> i q o", o=32)).then_inc(loaded, 16)

        @block.gpsimd
        def _(pool):
            pool.memset(blocks[:, :], 0.0).then_inc(cleared, 1)
            pool.memset(g_w[:, :], 0.0).then_inc(cleared, 1)

            pool.wait_ge(relued, 2 * CH0)
            with pool.Fori(0, NT) as i:
                pool.wait_ge(catted, i)
                pool.tensor_copy(rT[:, :].rearrange("p (q n) -> p q n", n=P),
                                 YT[:, :].rearrange("p (q n) -> p q n", n=NPAD)[:, :, bass.ds(i * P, P)]).then_inc(rT_staged, 1)
                pool.wait_ge(agg_turned, i)
                pool.tensor_copy(agg[:, :], at(acc, i * AW, D + DE)).then_inc(staged, 1)

        @block.vector
        def _(dve):
            c = Chain(dve, chain)
            ts, tt, stt = dve.tensor_scalar, dve.tensor_tensor, dve.scalar_tensor_tensor
            c.step(ts(deg[:, :], acc[:, :].rearrange("p (i a) -> p i a", a=AW)[:, 0:NT, AW - 1], 1.0, None, ALU.max))
            dve.sem_inc(deg_ready, 1)
            for q in range(CH0 // 2):
                y = YT[:, q * NPAD:(q + 1) * NPAD]
                c.step(ts(y, y, bn_scale[:, q:q + 1], bn_shift[:, q:q + 1], ALU.mult, ALU.add))
                ts(y, y, 0.0, None, ALU.max).then_inc(relued, 2)
            dve.wait_ge(deg_rooted, 1)
            c.step(dve.reciprocal(norm_in[:, :], dtmp[:, :]))
            refine(c, norm_in, deg, dtmp)
            dve.wait_ge(loaded, 160)
            for q in range(CH0):
                c.did(ts(blocks[:, q * P:(q + 1) * P], blocks[:, q * P:(q + 1) * P], taps[:, q:q + 1], None, ALU.mult))
            c.settle()
            dve.sem_inc(dwed, 1)
            third = lambda buf: buf[:, :].rearrange("p (g c) -> p g c", c=32)

            def scales(t, n, k):
                t.step(ts(size[:, :], norms[:, 2 * k:2 * k + 1], MINNORM, None, ALU.max))
                yield
                t.did(ts(least[:, :], size[:, :], ATANH_MAXNORM, None, ALU.min))
                t.step(dve.reciprocal(inv[:, :], size[:, :]))
                yield
                t.step(tt(a[:, :], least[:, :], inv[:, :], ALU.mult))
                yield
                t.step(ts(size[:, :], norms[:, 2 * k + 1:2 * k + 2], a[:, 0:1], MINNORM, ALU.mult, ALU.max))
                t.did(dve.tensor_reduce(k_sum[:, :], kr[:, k * 512:(k + 1) * 512].rearrange("p (g c) -> p g c", c=32),
                                        AX_X, ALU.add))
                t.did(ts(least[:, :], size[:, :], ATANH_MAXNORM, None, ALU.min))
                t.step(dve.reciprocal(inv[:, :], size[:, :]))
                t.step(stt(out=b[:, :], in0=least[:, :], scalar=inv[:, 0:1], in1=a[:, :], op0=ALU.mult, op1=ALU.mult))
                t.did(stt(out=at(b3, n, 1), in0=b[:, :], scalar=b[:, 0:1], in1=b[:, :], op0=ALU.mult, op1=ALU.mult))
                yield

            def tile(t, i, k, last=False):
                following = scales(t, i + 1, 1 - k)
                t.step(ts(third(den), parts(cat[k], 2), b[:, 0:1], 1e-15, ALU.mult, ALU.add))
                t.step(dve.reciprocal(den[:, :], den[:, :]))
                dve.wait_ge(prod_turned, i)
                dve.wait_ge(prod_squared, i)
                t.step(tt(third(prod), parts(cat[k], 2), third(den), ALU.mult))
                stt(out=third(prod), in0=parts(cat[k], 0), scalar=0.0, in1=third(prod), op0=ALU.max, op1=ALU.mult)\
                    .then_inc(cat_free, 1)
                dve.wait_ge(cat_free, i + 1)
                tt(third(prod), third(prod), k_sum[:, :].unsqueeze(2).to_broadcast([P, GRP, 32]), ALU.mult)\
                    .then_inc(prod_ready, 1)
                if not last:
                    dve.wait_ge(k_made, i + 2)
                    next(following)
                dve.wait_ge(gnn_done, i + 1)
                stt(out=g_out[:, :], in0=p_graph[:, 0:D], scalar=at(norm_in, i, 1), in1=g_b[:, :],
                    op0=ALU.mult, op1=ALU.add).then_inc(gnn_taken, 1)
                if not last:
                    next(following)
                dve.wait_ge(gnn_taken, i + 1)
                t.did(stt(out=at(X, i * D, D), in0=g_out[:, :], scalar=0.0, in1=at(X, i * D, D), op0=ALU.max, op1=ALU.add))
                if not last:
                    next(following)
                    dve.wait_ge(prod_ready, i + 1)
                    next(following)
                t.settle()

            dve.wait_ge(k_made, 1)
            for _ in scales(c, 0, 0):
                pass
            c.settle()
            base, per = c.n, 14
            with dve.Fori(0, NT // 2) as h:
                for k in range(2):
                    t = Chain(dve, chain, (h * 2 + k) * per + base)
                    tile(t, h * 2 + k, k)
                    assert t.n == per, t.n
            c.n = base + (NT - 1) * per
            tile(c, NT - 1, 0, last=True)
            dve.wait_ge(prods_rooted, 1)
            c.step(tt(c_tmp[:, :], prod_sums[:, :], b3[:, :], ALU.mult))
            c.step(ts(c_tmp[:, :], c_tmp[:, :], MINNORM, None, ALU.max))
            c.did(ts(c_b3[:, :], c_tmp[:, :], ATANH_MAXNORM, None, ALU.min))
            c.step(dve.reciprocal(c_tmp[:, :], c_tmp[:, :]))
            c.step(tt(c_b3[:, :], c_b3[:, :], c_tmp[:, :], ALU.mult))
            c.step(tt(c_b3[:, :], c_b3[:, :], b3[:, :], ALU.mult))
            dve.wait_ge(res_kept, NT)
            with dve.Fori(0, NT) as i:
                stt(out=at(FT, i * D, D), in0=at(FT, i * D, D), scalar=at(c_b3, i, 1), in1=r_b[:, :],
                    op0=ALU.mult, op1=ALU.add).then_inc(ft_ready, 1)

        @block.scalar
        def _(act):
            for q in range(CH0 // 2, CH0):
                y = YT[:, q * NPAD:(q + 1) * NPAD]
                act.activation(y, y, ACT.Relu, scale=bn_scale[:, q:q + 1], bias=bn_shift[:, q:q + 1]).then_inc(relued, 2)
            act.wait_ge(deg_ready, 1)
            act.activation(dtmp[:, :], deg[:, :], ACT.Sqrt).then_inc(deg_rooted, 1)

            def norm(n, k):
                c = Chain(act, act_chain, n * 3)
                act.wait_ge(catted, n + 1)
                c.step(act.activation(square[:, :], cat[k][:, 0:C0], ACT.Square, accum_out=sums[:, 2 * k:2 * k + 1]))
                c.step(act.activation(square[:, :], cat[k][:, C0:], ACT.Square, accum_out=sums[:, 2 * k + 1:2 * k + 2]))
                act.activation(norms[:, 2 * k:2 * k + 1], sums[:, 2 * k:2 * k + 1], ACT.Sqrt)
                c.did(act.activation(norms[:, 2 * k + 1:2 * k + 2], sums[:, 2 * k + 1:2 * k + 2], ACT.Sqrt,
                                     bias=sums[:, 2 * k:2 * k + 1]))
                act.activation(kr[:, k * 512:(k + 1) * 512].rearrange("p (g c) -> p g c", c=32), parts(cat[k], 1),
                               ACT.Relu).then_inc(k_made, 1)

            def keep_agg(n):
                act.wait_ge(agg_turned, n + 1)
                act.copy(aggT[:, 0:2 * P], p_graph[:, 0:2 * P])
                act.copy(aggT[0:DE, 2 * P:], p_graph[0:DE, 2 * P:3 * P]).then_inc(agg_kept, 1)

            def keep_res(i):
                act.wait_ge(res_done, i + 1)
                act.copy(at(FT, i * D, D), p_mix[:, 0:D]).then_inc(res_kept, 1)

            def keep_prod(i):
                act.wait_ge(prod_turned, i + 1)
                act.copy(prodT[:, :], p_mix[:, :]).then_inc(prod_kept, 1)

            def square_prod(i, norms_done):
                act.wait_ge(act_chain, norms_done * 3)
                act.activation(square[:, 0:512], prod[:, :], ACT.Square, accum_out=at(prod_sums, i, 1)).then_inc(prod_squared, 1)
                act.wait_ge(prod_squared, i + 1)

            def tile(i, k, first=False):
                norm(i + 1, 1 - k)
                if not first:
                    keep_res(i - 1)
                keep_prod(i)
                keep_agg(i + 1)
                square_prod(i, i + 2)

            norm(0, 0)
            keep_agg(0)
            tile(0, 0, first=True)
            with act.Fori(0, NT // 2 - 1) as h:
                for k in range(2):
                    tile(h * 2 + k + 1, 1 - k)
            tile(NT - 2, 1)
            keep_res(NT - 2)
            keep_prod(NT - 1)
            square_prod(NT - 1, NT)
            keep_res(NT - 1)
            act.activation(prod_sums[:, :], prod_sums[:, :], ACT.Sqrt).then_inc(prods_rooted, 1)
            with act.Fori(0, NT) as i:
                act.wait_ge(ft_ready, i + 1)
                act.activation(square[:, 0:D], at(FT, i * D, D), ACT.Square, accum_out=at(sumsq, i, 1)).then_inc(sums_ready, 1)
                act.wait_ge(sums_ready, i + 1)

        @block.tensor
        def _(pe):
            def make_cat(n, k):
                pe.wait_ge(rT_staged, n + 1)
                for q in range(CH0):
                    pe.transpose(cat[k][:, q * P:(q + 1) * P], rT[:, q * P:(q + 1) * P], const.ident[:, :])
                for q in range(CH0):
                    mm = pe.matmul(cat[k][:, C0 + q * P:C0 + (q + 1) * P], rT[:, q * P:(q + 1) * P],
                                   blocks[:, q * P:(q + 1) * P], start=True, stop=True)
                mm.then_inc(catted, 1)

            def turn_agg(n):
                pe.wait_ge(staged, n + 1)
                for q in range(3):
                    w = P if q < 2 else DE
                    mm = pe.transpose(p_graph[0:w, q * P:(q + 1) * P], agg[:, q * P:q * P + w], const.ident[:, :])
                mm.then_inc(agg_turned, 1)

            def make_graph(i):
                pe.wait_ge(agg_kept, i + 1)
                for q in range(3):
                    w = P if q < 2 else DE
                    mm = pe.matmul(p_graph[:, 0:D], aggT[0:w, q * P:(q + 1) * P], g_w[0:w, q * D:(q + 1) * D],
                                   start=(q == 0), stop=(q == 2))
                mm.then_inc(gnn_done, 1)

            def turn_prod(i):
                pe.wait_ge(prod_ready, i + 1)
                for q in range(4):
                    mm = pe.transpose(p_mix[:, q * P:(q + 1) * P], prod[:, q * P:(q + 1) * P], const.ident[:, :])
                mm.then_inc(prod_turned, 1)

            def make_res(i):
                pe.wait_ge(prod_kept, i + 1)
                for q in range(4):
                    mm = pe.matmul(p_mix[:, 0:D], prodT[:, q * P:(q + 1) * P], r_w[:, q * D:(q + 1) * D],
                                   start=(q == 0), stop=(q == 3))
                mm.then_inc(res_done, 1)

            def tile(i, k, first=False):
                if not first:
                    pe.wait_ge(cat_free, i)
                make_cat(i + 1, 1 - k)
                if not first:
                    make_res(i - 1)
                make_graph(i)
                if not first:
                    pe.wait_ge(res_kept, i)
                turn_prod(i)
                pe.wait_ge(gnn_taken, i + 1)
                turn_agg(i + 1)

            pe.wait_ge(loaded, 160)
            pe.wait_ge(dwed, 1)
            make_cat(0, 0)
            turn_agg(0)
            tile(0, 0, first=True)
            with pe.Fori(0, NT // 2 - 1) as h:
                for k in range(2):
                    tile(h * 2 + k + 1, 1 - k)
            tile(NT - 2, 1)
            make_res(NT - 2)
            make_graph(NT - 1)
            pe.wait_ge(res_kept, NT - 1)
            turn_prod(NT - 1)
            make_res(NT - 1)


def add_mapped(nc, X, FT, sumsq):
    with ExitStack() as ctx:
        m = Memory(nc, ctx, "mapped")
        sq, norm, inv, tmp = (m.sb(n, [P, NT]) for n in ("sq", "norm", "inv", "tmp"))
        chain, floored, rooted, known, tanhed = (m.sem(n) for n in ("chain", "floored", "rooted", "known", "tanhed"))
        block = ctx.enter_context(nc.Block())

        @block.vector
        def _(dve):
            c = Chain(dve, chain)
            c.step(dve.tensor_scalar(sq[:, :], sumsq[:, :], MINNORM * MINNORM, None, ALU.max))
            dve.sem_inc(floored, 1)
            dve.wait_ge(rooted, 1)
            c.step(dve.reciprocal(inv[:, :], norm[:, :]))
            refine(c, inv, sq, tmp)
            c.step(dve.tensor_tensor(norm[:, :], sq[:, :], inv[:, :], ALU.mult))
            dve.sem_inc(known, 1)
            dve.wait_ge(tanhed, 1)
            c.step(dve.scalar_tensor_tensor(out=inv[:, :], in0=tmp[:, :], scalar=MAXNORM, in1=inv[:, :],
                                            op0=ALU.min, op1=ALU.mult))
            with dve.Fori(0, NG) as g:
                for n in range(GT):
                    i = g * GT + n
                    dve.scalar_tensor_tensor(out=at(X, i * D, D), in0=at(FT, i * D, D), scalar=at(inv, i, 1),
                                             in1=at(X, i * D, D), op0=ALU.mult, op1=ALU.add)

        @block.scalar
        def _(act):
            act.wait_ge(floored, 1)
            act.activation(norm[:, :], sq[:, :], ACT.Sqrt).then_inc(rooted, 1)
            act.wait_ge(known, 1)
            act.activation(tmp[:, :], norm[:, :], ACT.Tanh).then_inc(tanhed, 1)


def graph_and_kv(nc, const, acc, X, XN, XNT, kv, g_w, g_bias, kv_w, kv_bias):
    with ExitStack() as ctx:
        m = Memory(nc, ctx, "kv")
        gw, kw = m.sb("gw", [P, 4 * D]), m.sb("kw", [P, 4 * D])
        gb, gb2, kb = m.sb("gb", [P, D]), m.sb("gb2", [P, D]), m.sb("kb", [P, 2 * D])
        xs, us = m.sb("xs", [P, D]), m.sb("us", [P, D])
        xuT, key, neg, v = ([m.sb(f"{n}{k}", [P, w]) for k in range(2)]
                            for n, w in (("xuT", 2 * 2 * P), ("key", D), ("neg", D), ("v", 2 * (P + 1))))
        square, sumsq = m.sb("square", [P, D]), m.sb("sumsq", [P, NT])
        inv, tmp, sq = m.sb("inv", [P, NT]), m.sb("tmp", [P, NT]), m.sb("sq", [P, NT])
        p_x = m.ps("p_x", [P, 512])
        p_kv, p_g, p_a = ([m.ps(f"{n}{k}", [P, 512]) for k in range(2)] for n in ("p_kv", "p_g", "p_a"))
        loaded, chain, x_staged, u_staged, turned, kept, kv_made, g_made, cut, exped, k_ready, summed, g_taken, g_ready, squared, root, rooted = (
            m.sem(n) for n in ("loaded", "chain", "x_staged", "u_staged", "turned", "kept", "kv_made", "g_made", "cut",
                               "exped", "k_ready", "summed", "g_taken", "g_ready", "squared", "root", "rooted"))
        block = ctx.enter_context(nc.Block())

        @block.sync
        def _(sp):
            sp.dma_start(gw[:, :], g_w).then_inc(loaded, 16)
            sp.dma_start(kw[:, :], kv_w).then_inc(loaded, 16)
            sp.dma_start(gb[:, :], row(g_bias[0, :])).then_inc(loaded, 16)
            sp.dma_start(gb2[:, :], row(g_bias[1, :])).then_inc(loaded, 16)
            sp.dma_start(kb[:, :], row(kv_bias)).then_inc(loaded, 16)

        @block.vector
        def _(dve):
            c = Chain(dve, chain)
            ts, tt, stt = dve.tensor_scalar, dve.tensor_tensor, dve.scalar_tensor_tensor
            halves = lambda b: b.rearrange("p (c n) -> p c n", c=2)

            def stage(t, n):
                nb = at(acc, n * D, D)
                dve.wait_ge(turned, n)
                t.step(tt(us[:, :], nb, at(XN, n * D, D), ALU.mult))
                tt(us[:, :], us[:, :], nb, ALU.add).then_inc(u_staged, 1)

            def step(t, i, k, first=False, ahead=True, last=False):
                dve.wait_ge(kv_made, i + 1)
                if not first:
                    dve.wait_ge(summed, i - 1)
                t.did(tt(halves(v[k][:, :])[:, :, 0:P], halves(p_kv[k][:, D:2 * D]), halves(kb[:, D:2 * D]), ALU.add))
                t.step(tt(key[k][:, :], p_kv[k][:, 0:D], kb[:, 0:D], ALU.add))
                ts(neg[k][:, :], key[k][:, :], 0.0, None, ALU.min).then_inc(cut, 1)
                if ahead:
                    stage(t, i + 2)
                nb = at(acc, i * D, D)
                dve.wait_ge(g_made, i + 1)
                tt(nb, p_g[k][:, 0:D], gb[:, :], ALU.add).then_inc(g_taken, 1)
                dve.wait_ge(g_taken, i + 1)
                stt(out=nb, in0=nb, scalar=0.2, in1=nb, op0=ALU.mult, op1=ALU.max).then_inc(g_ready, 1)
                dve.wait_ge(exped, i + 1)
                phi = stt(out=key[k][:, :], in0=key[k][:, :], scalar=0.0, in1=neg[k][:, :], op0=ALU.max, op1=ALU.add)
                if last:
                    t.step(phi)
                    phi = ts(key[k][:, :], key[k][:, :], const.valid[:, NT - 1:NT], None, ALU.mult)
                phi.then_inc(k_ready, 1)

            for k in range(2):
                c.did(dve.memset(v[k][:, :], 1.0))
            stage(c, 0)
            dve.wait_ge(loaded, 80)
            c.step(tt(gb[:, :], gb[:, :], gb2[:, :], ALU.add))
            stage(c, 1)
            step(c, 0, 0, first=True)
            base, per = c.n, 3
            with dve.Fori(0, (NT - 3) // 2) as h:
                for k in range(2):
                    t = Chain(dve, chain, (h * 2 + k) * per + base)
                    step(t, h * 2 + k + 1, 1 - k)
                    assert t.n == per, t.n
            c.n = base + (NT - 3) * per
            step(c, NT - 2, 1, ahead=False)
            step(c, NT - 1, 0, ahead=False, last=True)
            dve.wait_ge(squared, NT)
            c.step(ts(sq[:, :], sumsq[:, :], 1e-24, None, ALU.max))
            dve.sem_inc(root, 1)
            dve.wait_ge(summed, NT)
            for k in range(2):
                dve.tensor_copy(kv[:, k * (P + 1):(k + 1) * (P + 1)], p_a[k][:, 0:P + 1])
            dve.wait_ge(rooted, 1)
            c.step(dve.reciprocal(inv[:, :], tmp[:, :]))
            refine(c, inv, sq, tmp)
            with dve.Fori(0, NG) as g:
                for n in range(GT):
                    i = g * GT + n
                    stt(out=at(X, i * D, D), in0=at(acc, i * D, D), scalar=at(inv, i, 1), in1=at(X, i * D, D),
                        op0=ALU.mult, op1=ALU.add)

        @block.scalar
        def _(act):
            def stage(n):
                act.wait_ge(turned, n)
                act.copy(xs[:, :], at(XN, n * D, D)).then_inc(x_staged, 1)

            def keep(n, k, first=False):
                act.wait_ge(turned, n + 1)
                if not first:
                    act.wait_ge(g_made, n - 1)
                act.copy(xuT[k][:, :], p_x[:, :]).then_inc(kept, 1)
                act.copy(XNT[:, :].rearrange("p (c n) -> p c n", c=2)[:, :, bass.ds(n * P, P)],
                         p_x[:, 0:D].rearrange("p (c n) -> p c n", c=2)).then_inc(kept, 1)

            def step(i, k, next_=True, ahead=True):
                if next_:
                    keep(i + 1, 1 - k)
                if ahead:
                    stage(i + 2)
                act.wait_ge(cut, i + 1)
                act.activation(neg[k][:, :], neg[k][:, :], ACT.Exp).then_inc(exped, 1)
                act.wait_ge(g_ready, i + 1)
                act.wait_ge(squared, i)
                act.activation(square[:, :], at(acc, i * D, D), ACT.Square, accum_out=at(sumsq, i, 1)).then_inc(squared, 1)

            stage(0)
            keep(0, 0, first=True)
            stage(1)
            step(0, 0)
            with act.Fori(0, (NT - 3) // 2) as h:
                for k in range(2):
                    step(h * 2 + k + 1, 1 - k)
            step(NT - 2, 1, ahead=False)
            step(NT - 1, 0, next_=False, ahead=False)
            act.wait_ge(root, 1)
            act.activation(tmp[:, :], sq[:, :], ACT.Sqrt).then_inc(rooted, 1)

        @block.tensor
        def _(pe):
            def turn(n):
                pe.wait_ge(x_staged, n + 1)
                pe.wait_ge(u_staged, n + 1)
                pe.wait_ge(kept, n * 2)
                for h in range(4):
                    mm = pe.transpose(p_x[:, h * P:(h + 1) * P], (xs, us)[h // 2][:, (h % 2) * P:(h % 2 + 1) * P],
                                      const.ident[:, :])
                mm.then_inc(turned, 1)

            def make(i, k, first=False):
                pe.wait_ge(kept, (i + 1) * 2)
                if not first:
                    pe.wait_ge(cut, i - 1)
                    pe.wait_ge(g_taken, i - 1)
                for h in range(2):
                    mm = pe.matmul(p_kv[k][:, :], xuT[k][:, h * P:(h + 1) * P], kw[:, h * 2 * D:(h + 1) * 2 * D],
                                   start=(h == 0), stop=(h == 1))
                mm.then_inc(kv_made, 1)
                for h in range(4):
                    mm = pe.matmul(p_g[k][:, 0:D], xuT[k][:, h * P:(h + 1) * P], gw[:, h * D:(h + 1) * D],
                                   start=(h == 0), stop=(h == 3))
                mm.then_inc(g_made, 1)

            def into_kv(i, k, last=False):
                pe.wait_ge(k_ready, i + 1)
                for h in range(2):
                    mm = pe.matmul(p_a[h][:, 0:P + 1], key[k][:, h * P:(h + 1) * P], v[k][:, h * (P + 1):(h + 1) * (P + 1)],
                                   start=False, stop=last)
                mm.then_inc(summed, 1)

            for h in range(2):
                pe.matmul(p_a[h][:, 0:P + 1], const.zero[:, 0:P], const.zero[:, 0:P + 1], start=True, stop=False)
            turn(0)
            pe.wait_ge(loaded, 80)
            turn(1)
            make(0, 0, first=True)
            with pe.Fori(0, (NT - 3) // 2) as h:
                for k in range(2):
                    i = h * 2 + k + 1
                    turn(i + 1)
                    make(i, 1 - k)
                    into_kv(i - 1, k)
            turn(NT - 1)
            make(NT - 2, 1)
            into_kv(NT - 3, 0)
            make(NT - 1, 0)
            into_kv(NT - 2, 1)
            into_kv(NT - 1, 0, last=True)


def attend(nc, const, XN, XNT, kv, q_w, q_bias, o_w, o_bias):
    HW = P + HEADS // 2
    with ExitStack() as ctx:
        m = Memory(nc, ctx, "att")
        qw, ow, ob, qb = m.sb("qw", [P, 2 * D]), m.sb("ow", [P, 2 * D]), m.sb("ob", [P, D]), m.sb("qb", [P, 2])
        heads = m.sb("heads", [P, 2 * HW])
        pos, neg = m.sb("pos", [P, 2 * GN]), m.sb("neg", [P, 2 * GN])
        z, o, oT, res = m.sb("z", [P, HEADS]), m.sb("o", [P, D]), m.sb("oT", [P, D]), m.sb("res", [P, D])
        p_q = [m.ps(f"p_q{k}", [P, 1024]) for k in range(2)]
        p_n, p_t, p_o = (m.ps(n, [P, 512]) for n in ("p_n", "p_t", "p_o"))
        loaded, chain, q_made, cut, exped, q_ready, summed, o_ready, turned, kept, made, taken, headed = (
            m.sem(n) for n in ("loaded", "chain", "q_made", "cut", "exped", "q_ready", "summed", "o_ready", "turned",
                               "kept", "made", "taken", "headed"))
        block = ctx.enter_context(nc.Block())
        halves = lambda b, w: b.rearrange("p (h n) -> p h n", h=2)[:, :, 0:w]

        @block.sync
        def _(sp):
            sp.dma_start(qw[:, :], q_w).then_inc(loaded, 16)
            sp.dma_start(qb[:, :], q_bias).then_inc(loaded, 16)
            sp.dma_start(ow[:, :], o_w).then_inc(loaded, 16)
            sp.dma_start(ob[:, :], row(o_bias)).then_inc(loaded, 16)

        @block.vector
        def _(dve):
            c = Chain(dve, chain)
            ts, tt = dve.tensor_scalar, dve.tensor_tensor
            c.step(dve.memset(heads[:, :], 0.0))
            for h in range(2):
                for b in range(4):
                    r = slice(32 * b, 32 * b + 32)
                    c.did(dve.tensor_copy(heads[r, h * HW + 32 * b:h * HW + 32 * b + 32],
                                          kv[r, h * (P + 1) + 32 * b:h * (P + 1) + 32 * b + 32]))
                    c.did(dve.tensor_copy(heads[r, h * HW + P + b:h * HW + P + b + 1],
                                          kv[r, h * (P + 1) + P:(h + 1) * (P + 1)]))
            c.settle()
            dve.sem_inc(headed, 1)
            dve.wait_ge(loaded, 64)
            base, per = c.n, 5 + GT * 5
            with dve.Fori(0, NG) as g:
                t = Chain(dve, chain, g * per + base)
                dve.wait_ge(summed, g * GT)
                for h in range(2):
                    dve.wait_ge(q_made, g * 2 + h + 1)
                    t.did(ts(halves(pos[:, h * GN:(h + 1) * GN], GH), halves(p_q[h][:, :], GH), qb[:, h:h + 1], 0.0,
                             ALU.add, ALU.max))
                    t.did(ts(halves(neg[:, h * GN:(h + 1) * GN], GH), halves(p_q[h][:, :], GH), qb[:, h:h + 1], 0.0,
                             ALU.add, ALU.min))
                t.settle()
                dve.sem_inc(cut, 1)
                dve.wait_ge(exped, g + 1)
                t.step(tt(pos[:, :], pos[:, :], neg[:, :], ALU.add))
                dve.sem_inc(q_ready, 1)
                for n in range(GT):
                    i = g * GT + n
                    dve.wait_ge(summed, i + 1)
                    t.step(ts(z[:, :].rearrange("p (c h) -> p c h", c=2),
                              p_n[:, 0:2 * HW].rearrange("p (c n) -> p c n", c=2)[:, :, P:HW], 1e-6, None, ALU.add))
                    t.step(dve.reciprocal(z[:, :], z[:, :]))
                    dve.wait_ge(turned, i)
                    for h in range(2):
                        last = tt(o[:, h * P:(h + 1) * P].rearrange("p (h e) -> p h e", e=32),
                                  p_n[:, h * HW:h * HW + P].rearrange("p (h e) -> p h e", e=32),
                                  z[:, 4 * h:4 * h + 4].unsqueeze(2).to_broadcast([P, 4, 32]), ALU.mult)
                        if h == 0:
                            t.did(last)
                    last.then_inc(o_ready, 1)
                    dve.wait_ge(made, i + 1)
                    t.step(tt(res[:, :], p_o[:, 0:D], ob[:, :], ALU.add))
                    dve.sem_inc(taken, 1)
                    t.step(tt(at(XN, i * D, D), at(XN, i * D, D), res[:, :], ALU.add))
                assert t.n == per, t.n

        @block.scalar
        def _(act):
            with act.Fori(0, NG) as g:
                act.wait_ge(cut, g + 1)
                act.activation(neg[:, :], neg[:, :], ACT.Exp).then_inc(exped, 1)
                for n in range(GT):
                    i = g * GT + n
                    act.wait_ge(turned, i + 1)
                    act.wait_ge(made, i)
                    act.copy(oT[:, :], p_t[:, 0:D]).then_inc(kept, 1)

        @block.tensor
        def _(pe):
            pe.wait_ge(loaded, 64)
            pe.wait_ge(headed, 1)
            with pe.Fori(0, NG) as g:
                pe.wait_ge(cut, g)
                for h in range(2):
                    for s in range(2):
                        for c in range(2):
                            mm = pe.matmul(p_q[h][:, s * 512:s * 512 + GH], qw[:, c * D + h * P:c * D + (h + 1) * P],
                                           at(XNT, g * GN + c * NPAD + s * GH, GH), start=(c == 0), stop=(c == 1))
                    mm.then_inc(q_made, 1)
                pe.wait_ge(q_ready, g + 1)
                for n in range(GT):
                    i = g * GT + n
                    pe.wait_ge(o_ready, i)
                    for h in range(2):
                        mm = pe.matmul(p_n[:, h * HW:(h + 1) * HW], pos[:, h * GN + n * P:h * GN + (n + 1) * P],
                                       heads[:, h * HW:(h + 1) * HW], start=True, stop=True)
                    mm.then_inc(summed, 1)
                    pe.wait_ge(o_ready, i + 1)
                    pe.wait_ge(kept, i)
                    for h in range(2):
                        mm = pe.transpose(p_t[:, h * P:(h + 1) * P], o[:, h * P:(h + 1) * P], const.ident[:, :])
                    mm.then_inc(turned, 1)
                    pe.wait_ge(kept, i + 1)
                    pe.wait_ge(taken, i)
                    for h in range(2):
                        mm = pe.matmul(p_o[:, 0:D], oT[:, h * P:(h + 1) * P], ow[:, h * D:(h + 1) * D],
                                       start=(h == 0), stop=(h == 1))
                    mm.then_inc(made, 1)


def feed_forward(nc, const, XN, w1, b1, w2, b2):
    M = FF // P
    with ExitStack() as ctx:
        m = Memory(nc, ctx, "ff")
        w1_, w2_, b1_, b2_ = m.sb("w1", [P, 2 * FF]), m.sb("w2", [P, M * D]), m.sb("b1", [P, M]), m.sb("b2", [P, D])
        rows, xT, hT, res = m.sb("rows", [P, GT * D]), m.sb("xT", [P, 2 * GN]), m.sb("hT", [P, M * GN]), m.sb("res", [P, D])
        p_t, p_y = ([m.ps(f"{n}{k}", [P, 512]) for k in range(2)] for n in ("p_t", "p_y"))
        p_h = [m.ps(f"p_h{k}", [P, 1024]) for k in range(2)]
        loaded, chain, staged, turned, kept, h_made, h_ready, made, taken = (
            m.sem(n) for n in ("loaded", "chain", "staged", "turned", "kept", "h_made", "h_ready", "made", "taken"))
        block = ctx.enter_context(nc.Block())

        @block.sync
        def _(sp):
            sp.dma_start(w1_[:, :], w1).then_inc(loaded, 16)
            sp.dma_start(w2_[:, :], w2).then_inc(loaded, 16)
            sp.dma_start(b1_[:, :], b1).then_inc(loaded, 16)
            sp.dma_start(b2_[:, :], row(b2)).then_inc(loaded, 16)

        @block.vector
        def _(dve):
            dve.wait_ge(loaded, 64)
            with dve.Fori(0, NG) as g:
                dve.wait_ge(turned, g * GT)
                dve.tensor_copy(rows[:, :], at(XN, g * GT * D, GT * D)).then_inc(staged, 1)
                t = Chain(dve, chain, g * 2 * GT)
                for n in range(GT):
                    i = g * GT + n
                    dve.wait_ge(made, i + 1)
                    t.step(dve.tensor_tensor(res[:, :], p_y[n % 2][:, 0:D], b2_[:, :], ALU.add))
                    dve.sem_inc(taken, 1)
                    t.step(dve.tensor_tensor(at(XN, i * D, D), at(XN, i * D, D), res[:, :], ALU.add))

        @block.scalar
        def _(act):
            act.wait_ge(loaded, 64)
            with act.Fori(0, NG) as g:
                act.wait_ge(h_made, g * M)
                for n in range(GT):
                    act.wait_ge(turned, g * GT + n + 1)
                    act.copy(xT[:, :].rearrange("p (c n) -> p c n", c=2)[:, :, n * P:(n + 1) * P],
                             p_t[n % 2][:, 0:D].rearrange("p (c n) -> p c n", c=2)).then_inc(kept, 1)
                act.wait_ge(made, g * GT)
                for q in range(M):
                    act.wait_ge(h_made, g * M + q + 1)
                    act.activation(hT[:, q * GN:(q + 1) * GN].rearrange("p (h n) -> p h n", h=2),
                                   p_h[q % 2][:, :].rearrange("p (h n) -> p h n", h=2)[:, :, 0:GH], ACT.Relu,
                                   bias=b1_[:, q:q + 1]).then_inc(h_ready, 1)

        @block.tensor
        def _(pe):
            pe.wait_ge(loaded, 64)
            with pe.Fori(0, NG) as g:
                pe.wait_ge(staged, g + 1)
                for n in range(GT):
                    pe.wait_ge(kept, g * GT + max(n - 1, 0))
                    for c in range(2):
                        mm = pe.transpose(p_t[n % 2][:, c * P:(c + 1) * P], rows[:, n * D + c * P:n * D + (c + 1) * P],
                                          const.ident[:, :])
                    mm.then_inc(turned, 1)
                pe.wait_ge(kept, (g + 1) * GT)
                for q in range(M):
                    pe.wait_ge(h_ready, g * M + max(q - 1, 0))
                    for s in range(2):
                        for c in range(2):
                            mm = pe.matmul(p_h[q % 2][:, s * 512:s * 512 + GH], w1_[:, c * FF + q * P:c * FF + (q + 1) * P],
                                           xT[:, c * GN + s * GH:c * GN + (s + 1) * GH], start=(c == 0), stop=(c == 1))
                    mm.then_inc(h_made, 1)
                pe.wait_ge(h_ready, (g + 1) * M)
                for n in range(GT):
                    pe.wait_ge(taken, g * GT + max(n - 1, 0))
                    for q in range(M):
                        mm = pe.matmul(p_y[n % 2][:, 0:D], hT[:, q * GN + n * P:q * GN + (n + 1) * P],
                                       w2_[:, q * D:(q + 1) * D], start=(q == 0), stop=(q == M - 1))
                    mm.then_inc(made, 1)


class Routing:

    def __init__(self, nc, ctx, tag, ne):
        m = Memory(nc, ctx, tag)
        self.ne, self.tag = ne, tag
        self.tiles = -(-((2 * N + ne * (P - 1)) // P) // 2) * 2
        self.gate = [m.sb(f"gate{k}", [P, NT]) for k in range(2)]
        self.slot = [m.sb(f"slot{k}", [P, NT], I32) for k in range(2)]
        self.expert = m.sb("expert", [1, self.tiles + 2], I32)

    def route(self, nc, const, XN, w, bias, rows_out, zeroed):
        with ExitStack() as ctx:
            self.build(nc, Memory(nc, ctx, f"{self.tag}r"), ctx, const, XN, w, bias, rows_out, zeroed)

    def build(self, nc, m, ctx, const, XN, w, bias, rows_out, zeroed):
        ne, tj = self.ne, self.tiles
        W = NT * ne
        weight, bias_row = m.sb("weight", [P, 2 * ne]), m.sb("bias_row", [P, ne])
        rows, turned = m.sb("rows", [P, GT * D]), m.sb("turned", [P, GT * D])
        logit, work, cand, pos, ends = (m.sb(n, [P, W]) for n in ("logit", "work", "cand", "pos", "ends"))
        hot = [m.sb(f"hot{k}", [P, W]) for k in range(2)]
        first, second, total, pick, big = (m.sb(n, [P, NT]) for n in ("first", "second", "total", "pick", "big"))
        number, base, size = m.sb("number", [P, ne]), m.sb("base", [P, ne]), m.sb("size", [P, ne])
        size_i = m.sb("size_i", [P, ne], I32)
        scatter_i = [m.sb(f"scatter_i{k}", [P, NT], I32) for k in range(2)]
        place, mine = m.sb("place", [1, tj + 2]), m.sb("mine", [1, tj + 2])
        out_row = m.sb("out_row", [P, 2 * D])
        out_index = m.sb("out_index", [P, 4], I32)
        p_t = m.ps("p_t", [P, 3 * 512])
        p_l, p_before, p_total = (m.ps(n, [P, 512]) for n in ("p_l", "p_before", "p_total"))
        loaded, made_c, staged, turning, kept, made, taken, chain, exped, asked_exp, counted, ranked = (
            m.sem(n) for n in ("loaded", "made_c", "staged", "turning", "kept", "made", "taken", "chain",
                               "exped", "asked_exp", "counted", "ranked"))
        slotted, row_ready, asked, index_put = (m.sem(n) for n in ("slotted", "row_ready", "asked", "index_put"))
        scattered = [m.sem(f"scattered{k}") for k in range(2)]
        block = ctx.enter_context(nc.Block())
        three = lambda b: b[:, :].rearrange("p (i e) -> p i e", e=ne)
        over = lambda b: b[:, :].unsqueeze(2).to_broadcast([P, NT, ne])
        numbers = number[:, :].unsqueeze(1).to_broadcast([P, NT, ne])
        slots = (tj + 2) * P

        @block.sync
        def _(sp):
            sp.dma_start(weight[:, :], w).then_inc(loaded, 16)
            if bias is not None:
                sp.dma_start(bias_row[:, :], row(bias)).then_inc(loaded, 16)

        @block.gpsimd
        def _(pool):
            pool.iota(number[:, :], pattern=[[1, ne]], base=0, channel_multiplier=0,
                      allow_small_or_imprecise_dtypes=True).then_inc(made_c, 1)
            pool.iota(place[:, :], pattern=[[1, tj + 2]], base=0, channel_multiplier=0,
                      allow_small_or_imprecise_dtypes=True).then_inc(made_c, 1)
            pool.wait_ge(zeroed, fills(rows_out) * 16)

            def scatter(i, k):
                pool.wait_ge(row_ready, i + 1)
                pool.sem_inc(asked, 1)
                for s in range(2):
                    pool.indirect_dma_start(
                        out=rows_out, out_offset=bass.IndirectOffsetOnAxis(ap=out_index[:, 2 * k + s:2 * k + s + 1], axis=0),
                        in_=out_row[:, k * D:(k + 1) * D], in_offset=None, bounds_check=slots - 1,
                        oob_is_err=False).then_inc(scattered[k], 16)

            with pool.Fori(0, NT // 2) as h:
                for k in range(2):
                    scatter(h * 2 + k, k)
            scatter(NT - 1, 0)
            pool.wait_ge(scattered[0], (NT // 2 + 1) * 32)
            pool.wait_ge(scattered[1], NT // 2 * 32)

        @block.vector
        def _(dve):
            ts, tt, stt = dve.tensor_scalar, dve.tensor_tensor, dve.scalar_tensor_tensor
            dve.wait_ge(loaded, 16 if bias is None else 32)
            with dve.Fori(0, NG) as g:
                dve.wait_ge(turning, g)
                dve.tensor_copy(rows[:, :], at(XN, g * GT * D, GT * D)).then_inc(staged, 1)
                dve.wait_ge(made, g + 1)
                if bias is None:
                    ins = dve.tensor_copy(at(logit, g * GT * ne, GT * ne), p_l[:, 0:GT * ne])
                else:
                    ins = tt(at(logit, g * GT * ne, GT * ne).rearrange("p (i e) -> p i e", e=ne),
                             p_l[:, 0:GT * ne].rearrange("p (i e) -> p i e", e=ne),
                             bias_row[:, :].unsqueeze(1).to_broadcast([P, GT, ne]), ALU.add)
                ins.then_inc(taken, 1)
            c = Chain(dve, chain)
            dve.wait_ge(taken, NG)
            dve.wait_ge(made_c, 2)
            c.step(dve.tensor_copy(work[:, :], logit[:, :]))
            for k, top in enumerate((first, second)):
                c.step(dve.tensor_reduce(top[:, :], three(work), AX_X, ALU.max))
                c.step(tt(three(cand), three(work), over(top), ALU.is_equal))
                c.step(ts(cand[:, :], cand[:, :], -64.0, 64.0, ALU.mult, ALU.add))
                c.step(tt(three(cand), three(cand), numbers, ALU.add))
                c.step(dve.tensor_reduce(pick[:, :], three(cand), AX_X, ALU.min))
                c.step(tt(three(hot[k]), numbers, over(pick), ALU.is_equal))
                if k == 0:
                    c.step(stt(out=work[:, :], in0=hot[0][:, :], scalar=-1e30, in1=work[:, :], op0=ALU.mult, op1=ALU.add))
            c.step(tt(work[:, :], hot[0][:, :], hot[1][:, :], ALU.add))
            c.step(tt(three(work), three(work), over(const.valid), ALU.mult))
            dve.sem_inc(counted, 1)
            c.step(tt(second[:, :], second[:, :], first[:, :], ALU.subtract))
            c.step(tt(three(cand), three(logit), over(first), ALU.subtract))
            dve.sem_inc(asked_exp, 1)
            dve.wait_ge(exped, 2)
            if bias is None:
                c.step(dve.tensor_reduce(total[:, :], three(cand), AX_X, ALU.add))
                c.step(dve.reciprocal(total[:, :], total[:, :]))
                c.step(tt(second[:, :], second[:, :], total[:, :], ALU.mult))
                c.step(stt(out=first[:, :], in0=total[:, :], scalar=1e-9, in1=second[:, :], op0=ALU.add, op1=ALU.add))
                c.step(dve.reciprocal(first[:, :], first[:, :]))
                c.did(tt(self.gate[0][:, :], total[:, :], first[:, :], ALU.mult))
                c.step(tt(self.gate[1][:, :], second[:, :], first[:, :], ALU.mult))
            else:
                c.step(ts(first[:, :], second[:, :], 1.0, None, ALU.add))
                c.step(dve.reciprocal(self.gate[0][:, :], first[:, :]))
                c.step(tt(self.gate[1][:, :], second[:, :], self.gate[0][:, :], ALU.mult))
            dve.wait_ge(ranked, 2)
            c.did(dve.tensor_copy(pos[:, :], p_before[:, 0:W]))
            c.step(dve.tensor_copy(cand[:, :], p_total[:, 0:W]))
            for e in range(ne):
                c.did(dve.tensor_tensor_scan(three(ends)[:, :, e], const.ones[:, 0:NT], three(cand)[:, :, e], 0.0,
                                             ALU.mult, ALU.add))
            c.settle()
            c.did(ts(size[:, :], three(ends)[:, NT - 1, :], float(P - 1), None, ALU.add))
            c.step(tt(cand[:, :], ends[:, :], cand[:, :], ALU.subtract))
            c.did(tt(pos[:, :], pos[:, :], cand[:, :], ALU.add))
            c.step(dve.tensor_copy(size_i[:, :], size[:, :]))
            c.step(ts(size_i[:, :], size_i[:, :], 7, None, ALU.arith_shift_right))
            c.step(dve.tensor_copy(size[:, :], size_i[:, :]))
            c.step(dve.tensor_tensor_scan(base[:, :], const.ones[:, 0:ne], size[:, :], 0.0, ALU.mult, ALU.add))
            c.step(ts(mine[:, :], place[:, :], base[0:1, 0:1], None, ALU.is_ge))
            for e in range(1, ne - 1):
                c.step(stt(out=mine[:, :], in0=place[:, :], scalar=base[0:1, e:e + 1], in1=mine[:, :],
                           op0=ALU.is_ge, op1=ALU.add))
            c.did(dve.tensor_copy(self.expert[:, :], mine[:, :]))
            c.step(tt(base[:, :], base[:, :], size[:, :], ALU.subtract))
            c.step(ts(base[:, :], base[:, :], float(P), None, ALU.mult))
            c.step(tt(three(pos), three(pos), base[:, :].unsqueeze(1).to_broadcast([P, NT, ne]), ALU.add))
            c.step(ts(big[:, :], const.valid[:, :], -float(slots), float(slots), ALU.mult, ALU.add))
            for k in range(2):
                c.step(tt(cand[:, :], hot[k][:, :], pos[:, :], ALU.mult))
                c.step(dve.tensor_reduce(pick[:, :], three(cand), AX_X, ALU.add))
                c.step(tt(pick[:, :], pick[:, :], const.valid[:, :], ALU.mult))
                c.did(dve.tensor_copy(self.slot[k][:, :], pick[:, :]))
                c.step(tt(total[:, :], pick[:, :], big[:, :], ALU.add))
                c.step(dve.tensor_copy(scatter_i[k][:, :], total[:, :]))
            dve.sem_inc(slotted, 1)

        @block.scalar
        def _(act):
            with act.Fori(0, NG) as g:
                act.wait_ge(made, g)
                act.wait_ge(turning, g + 1)
                act.copy(turned[:, :], p_t[:, 0:GT * D]).then_inc(kept, 1)
            act.wait_ge(asked_exp, 1)
            act.activation(second[:, :], second[:, :], ACT.Exp).then_inc(exped, 1)
            act.activation(cand[:, :], cand[:, :], ACT.Exp).then_inc(exped, 1)
            act.wait_ge(slotted, 1)

            def put(i, k, turn):
                act.wait_ge(scattered[k], turn * 32)
                for s in range(2):
                    act.copy(out_index[:, 2 * k + s:2 * k + s + 1], scatter_i[s][:, bass.ds(i, 1)]).then_inc(index_put, 1)
                act.wait_ge(index_put, 2 * (i + 1))
                act.copy(out_row[:, k * D:(k + 1) * D], at(XN, i * D, D)).then_inc(row_ready, 1)

            with act.Fori(0, NT // 2) as h:
                for k in range(2):
                    put(h * 2 + k, k, h)
            put(NT - 1, 0, NT // 2)

        @block.tensor
        def _(pe):
            pe.wait_ge(loaded, 16 if bias is None else 32)
            with pe.Fori(0, NG) as g:
                pe.wait_ge(staged, g + 1)
                pe.wait_ge(kept, g)
                for q in range(2 * GT):
                    mm = pe.transpose(p_t[:, q * P:(q + 1) * P], rows[:, q * P:(q + 1) * P], const.ident[:, :])
                mm.then_inc(turning, 1)
                pe.wait_ge(kept, g + 1)
                pe.wait_ge(taken, g)
                for n in range(GT):
                    for c in range(2):
                        mm = pe.matmul(p_l[:, n * ne:(n + 1) * ne], turned[:, n * D + c * P:n * D + (c + 1) * P],
                                       weight[:, c * ne:(c + 1) * ne], start=(c == 0), stop=(c == 1))
                mm.then_inc(made, 1)
            pe.wait_ge(counted, 1)
            pe.matmul(p_before[:, 0:W], const.before[:, :], work[:, :], start=True, stop=True).then_inc(ranked, 1)
            pe.matmul(p_total[:, 0:W], const.ones[:, :], work[:, :], start=True, stop=True).then_inc(ranked, 1)


H0 = 682
U0 = H0 // 2
HC = 6
HK = H0 // HC + 1
E0, E1, H1 = 8, 16, 512


def gated_experts(nc, const, routing, rows_in, rows_out, up, up_loaded, w2):
    with ExitStack() as ctx:
        m = Memory(nc, ctx, "ex0")
        down = m.sb("down", [P, E0 * HC * D])
        x, xT, y = (m.sb(n, [P, 2 * D]) for n in ("x", "xT", "y"))
        act_h, h, hT = m.sb("act_h", [P, 2 * U0]), m.sb("h", [P, 2 * HC * HK]), m.sb("hT", [P, 2 * HC * P])
        p_x, p_y = m.ps("p_x", [P, 512]), m.ps("p_y", [P, 512])
        p_h = [m.ps(f"p_h{k}", [P, 1024]) for k in range(2)]
        p_t = m.ps("p_t", [P, 1024])
        loaded, x_turned, x_kept, u_made, silued, h_ready, h_turned, hT_kept, made, kept, padded = (
            m.sem(n) for n in ("loaded", "x_turned", "x_kept", "u_made", "silued", "h_ready", "h_turned", "hT_kept", "made",
                               "kept", "padded"))
        x_loaded = [m.sem(f"x_loaded{k}") for k in range(2)]
        stored = [m.sem(f"stored{k}") for k in range(2)]
        block = ctx.enter_context(nc.Block())
        steps = routing.tiles // 2

        @block.sync
        def _(sp):
            for k in range(2):
                sp.dma_start(x[:, k * D:(k + 1) * D], rows_in[k * P:(k + 1) * P, :]).then_inc(x_loaded[k], 16)
            for e in range(E0):
                sp.dma_start(down[0:HK, e * HC * D:(e + 1) * HC * D], w2[:, e * HC * D:(e + 1) * HC * D]).then_inc(loaded, 16)
            with sp.Fori(0, steps) as r:
                for k in range(2):
                    sp.wait_ge(x_turned, r + 1)
                    sp.dma_start(x[:, k * D:(k + 1) * D], rows_in[bass.ds((r * 2 + 2 + k) * P, P), :]).then_inc(x_loaded[k], 16)
                for k in range(2):
                    sp.wait_ge(kept, r * 2 + k + 1)
                    sp.dma_start(rows_out[bass.ds((r * 2 + k) * P, P), :], y[:, k * D:(k + 1) * D]).then_inc(stored[k], 16)
            for k in range(2):
                sp.wait_ge(stored[k], steps * 16)
                sp.wait_ge(x_loaded[k], (steps + 1) * 16)

        @block.tensor
        def _(pe):
            def turn_x(r):
                for k in range(2):
                    pe.wait_ge(x_loaded[k], r * 16 + 16)
                pe.wait_ge(x_kept, r)
                for q in range(4):
                    mm = pe.transpose(p_x[:, q * P:(q + 1) * P], x[:, q * P:(q + 1) * P], const.ident[:, :])
                mm.then_inc(x_turned, 1)

            turn_x(0)
            pe.wait_ge(up_loaded, E0 * 16)
            pe.wait_ge(padded, 1)
            with pe.Fori(0, steps) as r:
                ex = [pe.value_load(routing.expert[0:1, bass.ds(r * 2 + k, 1)], min_val=0, max_val=E0 - 1) for k in range(2)]

                def hidden(k, u):
                    pe.wait_ge(h_ready, r * 4 + max(2 * k + u - 1, 0))
                    for w in range(2):
                        for c in range(2):
                            mm = pe.matmul(p_h[u][:, w * 512:w * 512 + U0], xT[:, k * D + c * P:k * D + (c + 1) * P],
                                           at(up, ex[k] * (4 * H0) + ((c * 2 + w) * H0 + u * U0), U0),
                                           start=(c == 0), stop=(c == 1))
                    mm.then_inc(u_made, 1)

                def turn_h(k):
                    pe.wait_ge(h_ready, r * 4 + 2 * k + 2)
                    pe.wait_ge(hT_kept, (r * 2 + k) * 2)
                    for q in range(HC):
                        mm = pe.transpose(p_t[0:HK, (q // 3) * 512 + (q % 3) * P:(q // 3) * 512 + (q % 3 + 1) * P],
                                          h[:, (k * HC + q) * HK:(k * HC + q + 1) * HK], const.ident[:, :])
                    mm.then_inc(h_turned, 1)

                def out(k):
                    pe.wait_ge(loaded, E0 * 16)
                    pe.wait_ge(kept, r * 2 + k)
                    for q in range(HC):
                        if q % 3 == 0:
                            pe.wait_ge(hT_kept, (r * 2 + k) * 2 + q // 3 + 1)
                        K = min(HK, H0 - q * HK)
                        mm = pe.matmul(p_y[:, 0:D], hT[0:K, (k * HC + q) * P:(k * HC + q + 1) * P],
                                       down[0:K, bass.ds(ex[k] * (HC * D) + q * D, D)], start=(q == 0), stop=(q == HC - 1))
                    mm.then_inc(made, 1)

                pe.wait_ge(x_kept, r + 1)
                hidden(0, 0)
                hidden(0, 1)
                hidden(1, 0)
                turn_h(0)
                hidden(1, 1)
                turn_x(r + 1)
                out(0)
                turn_h(1)
                out(1)

        @block.scalar
        def _(act):
            def keep_x(r):
                act.wait_ge(x_turned, r + 1)
                act.wait_ge(u_made, r * 4)
                act.copy(xT[:, :], p_x[:, :]).then_inc(x_kept, 1)

            def keep_y(r, k):
                act.wait_ge(made, r * 2 + k + 1)
                act.wait_ge(stored[k], r * 16)
                act.copy(y[:, k * D:(k + 1) * D], p_y[:, 0:D]).then_inc(kept, 1)

            keep_x(0)
            with act.Fori(0, steps) as r:
                for n in range(4):
                    u = n % 2
                    act.wait_ge(u_made, r * 4 + n + 1)
                    act.wait_ge(h_ready, r * 4 + max(n - 1, 0))
                    act.activation(act_h[:, u * U0:(u + 1) * U0], p_h[u][:, 0:U0], ACT.Silu).then_inc(silued, 1)
                keep_x(r + 1)
                keep_y(r, 0)
                keep_y(r, 1)

        @block.vector
        def _(dve):
            dve.memset(h[:, :], 0.0).then_inc(padded, 1)
            dve.wait_ge(padded, 1)
            with dve.Fori(0, steps) as r:
                def gate(k, u):
                    dve.wait_ge(silued, r * 4 + 2 * k + u + 1)
                    dve.wait_ge(h_turned, r * 2)
                    dve.tensor_tensor(h[:, k * HC * HK + u * U0:k * HC * HK + (u + 1) * U0], act_h[:, u * U0:(u + 1) * U0],
                                      p_h[u][:, 512:512 + U0], ALU.mult).then_inc(h_ready, 1)

                def keep_h(k):
                    dve.wait_ge(h_turned, r * 2 + k + 1)
                    dve.wait_ge(made, r * 2 + max(k - 1, 0))
                    for q in range(2):
                        dve.tensor_copy(hT[0:HK, (k * HC + 3 * q) * P:(k * HC + 3 * q + 3) * P],
                                        p_t[0:HK, q * 512:q * 512 + 3 * P]).then_inc(hT_kept, 1)

                gate(0, 0)
                gate(0, 1)
                gate(1, 0)
                keep_h(0)
                gate(1, 1)
                keep_h(1)


def relu_experts(nc, const, routing, rows_in, rows_out, up, up_loaded, b1, w2, b2):
    HQ = H1 // P
    with ExitStack() as ctx:
        m = Memory(nc, ctx, "ex1")
        down = m.sb("down", [P, E1 * HQ * D])
        up_b, down_b = m.sb("up_b", [P, E1 * HQ]), m.sb("down_b", [P, E1 * D])
        x, xT, y = (m.sb(n, [P, 2 * D]) for n in ("x", "xT", "y"))
        h, hT = m.sb("h", [P, 2 * H1]), m.sb("hT", [P, 2 * H1])
        p_x, p_y = m.ps("p_x", [P, 512]), m.ps("p_y", [P, 512])
        p_h, p_t = ([m.ps(f"{n}{k}", [P, 512]) for k in range(2)] for n in ("p_h", "p_t"))
        loaded, down_loaded, x_turned, x_kept, h_made, h_kept, h_turned, h_ready, made, kept = (
            m.sem(n) for n in ("loaded", "down_loaded", "x_turned", "x_kept", "h_made", "h_kept", "h_turned", "h_ready", "made", "kept"))
        x_loaded = [m.sem(f"x_loaded{k}") for k in range(2)]
        stored = [m.sem(f"stored{k}") for k in range(2)]
        block = ctx.enter_context(nc.Block())
        steps = routing.tiles // 2

        @block.sync
        def _(sp):
            for k in range(2):
                sp.dma_start(x[:, k * D:(k + 1) * D], rows_in[k * P:(k + 1) * P, :]).then_inc(x_loaded[k], 16)
            sp.dma_start(up_b[:, :], b1).then_inc(loaded, 16)
            sp.dma_start(down_b[:, :], row(b2)).then_inc(loaded, 16)
            for e in range(0, E1, 4):
                sp.dma_start(down[:, e * HQ * D:(e + 4) * HQ * D], w2[:, e * HQ * D:(e + 4) * HQ * D]).then_inc(down_loaded, 16)
            with sp.Fori(0, steps) as r:
                for k in range(2):
                    sp.wait_ge(x_turned, r + 1)
                    sp.dma_start(x[:, k * D:(k + 1) * D], rows_in[bass.ds((r * 2 + 2 + k) * P, P), :]).then_inc(x_loaded[k], 16)
                for k in range(2):
                    sp.wait_ge(kept, r * 2 + k + 1)
                    sp.dma_start(rows_out[bass.ds((r * 2 + k) * P, P), :], y[:, k * D:(k + 1) * D]).then_inc(stored[k], 16)
            for k in range(2):
                sp.wait_ge(stored[k], steps * 16)
                sp.wait_ge(x_loaded[k], (steps + 1) * 16)

        @block.tensor
        def _(pe):
            def turn_x(r):
                for k in range(2):
                    pe.wait_ge(x_loaded[k], r * 16 + 16)
                pe.wait_ge(x_kept, r)
                for q in range(4):
                    mm = pe.transpose(p_x[:, q * P:(q + 1) * P], x[:, q * P:(q + 1) * P], const.ident[:, :])
                mm.then_inc(x_turned, 1)

            turn_x(0)
            pe.wait_ge(up_loaded, E1 // 4 * 16)
            with pe.Fori(0, steps) as r:
                ex = [pe.value_load(routing.expert[0:1, bass.ds(r * 2 + k, 1)], min_val=0, max_val=E1 - 1) for k in range(2)]

                def hidden(k):
                    pe.wait_ge(h_kept, r * 2)
                    for c in range(2):
                        mm = pe.matmul(p_h[k][:, :], xT[:, k * D + c * P:k * D + (c + 1) * P],
                                       at(up, ex[k] * (2 * H1) + c * H1, H1), start=(c == 0), stop=(c == 1))
                    mm.then_inc(h_made, 1)

                def turn_h(k):
                    pe.wait_ge(h_kept, r * 2 + k + 1)
                    pe.wait_ge(h_ready, r * 2)
                    for q in range(HQ):
                        mm = pe.transpose(p_t[k][:, q * P:(q + 1) * P], h[:, k * H1 + q * P:k * H1 + (q + 1) * P],
                                          const.ident[:, :])
                    mm.then_inc(h_turned, 1)

                def out(k):
                    pe.wait_ge(down_loaded, E1 // 4 * 16)
                    pe.wait_ge(kept, r * 2 + k)
                    pe.wait_ge(h_ready, r * 2 + k + 1)
                    for q in range(HQ):
                        mm = pe.matmul(p_y[:, 0:D], hT[:, k * H1 + q * P:k * H1 + (q + 1) * P],
                                       at(down, ex[k] * (HQ * D) + q * D, D), start=(q == 0), stop=(q == HQ - 1))
                    mm.then_inc(made, 1)

                pe.wait_ge(x_kept, r + 1)
                hidden(0)
                hidden(1)
                turn_h(0)
                turn_x(r + 1)
                turn_h(1)
                out(0)
                out(1)

        @block.scalar
        def _(act):
            def keep_x(r):
                act.wait_ge(x_turned, r + 1)
                act.wait_ge(h_made, r * 2)
                act.copy(xT[:, :], p_x[:, :]).then_inc(x_kept, 1)

            keep_x(0)
            with act.Fori(0, steps) as r:
                for k in range(2):
                    act.wait_ge(h_made, r * 2 + k + 1)
                    act.wait_ge(h_turned, r * 2)
                    act.copy(h[:, k * H1:(k + 1) * H1], p_h[k][:, :]).then_inc(h_kept, 1)
                keep_x(r + 1)

        @block.vector
        def _(dve):
            dve.wait_ge(loaded, 2 * 16)
            with dve.Fori(0, steps) as r:
                ex = [dve.value_load(routing.expert[0:1, bass.ds(r * 2 + k, 1)], min_val=0, max_val=E1 - 1) for k in range(2)]
                for k in range(2):
                    dve.wait_ge(h_turned, r * 2 + k + 1)
                    dve.wait_ge(made, r * 2)
                    for q in range(HQ):
                        ins = dve.tensor_scalar(hT[:, k * H1 + q * P:k * H1 + (q + 1) * P], p_t[k][:, q * P:(q + 1) * P],
                                                at(up_b, ex[k] * HQ + q, 1), 0.0, ALU.add, ALU.max)
                    ins.then_inc(h_ready, 1)
                for k in range(2):
                    dve.wait_ge(made, r * 2 + k + 1)
                    dve.wait_ge(stored[k], r * 16)
                    dve.tensor_tensor(y[:, k * D:(k + 1) * D], p_y[:, 0:D], at(down_b, ex[k] * D, D), ALU.add)\
                        .then_inc(kept, 1)


def combine(nc, routing, rows, to, base=None):
    with ExitStack() as ctx:
        m = Memory(nc, ctx, "comb" if base is None else "comb1")
        index = m.sb("index", [P, 2 * GT], I32)
        got = m.sb("got", [P, 2 * GT * D])
        loaded, chain, asked = m.sem("loaded"), m.sem("chain"), m.sem("asked")
        indexed = m.sem("indexed")
        gathered = [m.sem(f"gathered{k}") for k in range(2 * GT)]
        taken = m.sem("taken")
        block = ctx.enter_context(nc.Block())

        @block.sync
        def _(sp):
            if base is not None:
                sp.dma_start(to[:, :].rearrange("p (i d) -> p i d", d=D), base.rearrange("(i p) d -> p i d", p=P))\
                    .then_inc(loaded, 16)

        @block.scalar
        def _(act):
            with act.Fori(0, NG) as g:
                for n in range(GT):
                    for s in range(2):
                        act.wait_ge(gathered[2 * n + s], g * 16)
                        act.copy(index[:, 2 * n + s:2 * n + s + 1], routing.slot[s][:, bass.ds(g * GT + n, 1)])\
                            .then_inc(indexed, 1)

        @block.gpsimd
        def _(pool):
            with pool.Fori(0, NG) as g:
                for n in range(GT):
                    for s in range(2):
                        k = 2 * n + s
                        pool.wait_ge(indexed, g * 2 * GT + k + 1)
                        pool.wait_ge(taken, g * 2 * GT)
                        pool.sem_inc(asked, 1)
                        pool.indirect_dma_start(out=got[:, k * D:(k + 1) * D], out_offset=None, in_=rows,
                                                in_offset=bass.IndirectOffsetOnAxis(ap=index[:, k:k + 1], axis=0))\
                            .then_inc(gathered[k], 16)

        @block.vector
        def _(dve):
            if base is not None:
                dve.wait_ge(loaded, 16)
            with dve.Fori(0, NG) as g:
                for n in range(GT):
                    for s in range(2):
                        k = 2 * n + s
                        dve.wait_ge(gathered[k], g * 16 + 16)
                        dve.wait_ge(taken, g * 2 * GT + k)
                        y = at(to, (g * GT + n) * D, D)
                        dve.scalar_tensor_tensor(out=y, in0=got[:, k * D:(k + 1) * D],
                                                 scalar=routing.gate[s][:, bass.ds(g * GT + n, 1)], in1=y,
                                                 op0=ALU.mult, op1=ALU.add).then_inc(taken, 1)


def store_nodes(nc, X, out):
    with ExitStack() as ctx:
        m = Memory(nc, ctx, "store")
        stored = m.sem("stored")
        block = ctx.enter_context(nc.Block())
        full = (NT - 1) * P

        @block.sync
        def _(sp):
            sp.dma_start(out[0:full, :].rearrange("(i p) d -> p i d", p=P),
                         X[:, 0:(NT - 1) * D].rearrange("p (i d) -> p i d", d=D)).then_inc(stored, 16)
            sp.dma_start(out[full:N, :], X[0:NTAIL, (NT - 1) * D:NT * D]).then_inc(stored, 16)
            sp.wait_ge(stored, 32)


def build(nc, a, out):
    def scratch(name, rows):
        return nc.dram_tensor(name, [rows, D], F32).ap()

    with ExitStack() as ctx:
        const = Constants(nc, ctx)
        m = Memory(nc, ctx, "main")
        X = m.sb("X", [P, NT * D])
        load_nodes(nc, a["x"], X)
        norm_out, sumsq = m.sb("norm_out", [P, NT]), m.sb("sumsq", [P, NT])
        edges = Edges(nc, ctx, const, a["src"], a["dst"], a["edge_weight"], a["src_rows"],
                      a["dst_rows"], a["weight_rows"], norm_out)
        table0, table1, base1 = scratch("table0", NPAD), scratch("table1", NPAD), scratch("base1", NPAD)
        tiles0, tiles1 = (-(-((2 * N + e * (P - 1)) // P) // 2) * 2 for e in (E0, E1))
        in0, in1 = scratch("in0", (tiles0 + 2) * P), scratch("in1", (tiles1 + 2) * P)
        out0, out1 = scratch("out0", tiles0 * P), scratch("out1", tiles1 * P)
        zeroed = [m.sem(f"zeroed{k}") for k in range(2)]
        start_clearing(nc, const, in0, zeroed[0])
        start_clearing(nc, const, in1, zeroed[1])

        with ExitStack() as part:
            p = Memory(nc, part, "layer0")
            XN = p.sb("XN", [P, NT * D])
            acc = p.sb("acc", [P, (NT + 1) * (D + DE + 1)])
            layer_norm(nc, "ln0", X, XN, table=table0, scale=norm_out, sumsq=sumsq)
            aggregate(nc, "agg0", edges, table0, acc, D + DE + 1, False, a["edge_rows"])
            scale, stats = p.sb("scale", [P, NT]), p.sb("stats", [P, CH0 * NG * 12])
            bn_scale, bn_shift = p.sb("bn_scale", [P, CH0]), p.sb("bn_shift", [P, CH0])
            YT = p.sb("YT", [P, CH0 * NPAD])
            map_scale(nc, sumsq, scale)
            qkv_channels(nc, const, XN, scale, a["m0_qkv"], YT, stats)
            batch_norm(nc, stats, a["m0_gamma"], a["m0_beta"], bn_scale, bn_shift)
            graph_and_mixer(nc, const, acc, X, YT, bn_scale, bn_shift, XN, sumsq, a["g0_w"], a["g0_b"],
                            a["m0_dw"], a["m0_pw"], a["m0_res"], a["m0_res_b"])
            add_mapped(nc, X, XN, sumsq)
        with ExitStack() as part:
            p = Memory(nc, part, "moe0")
            up, up_loaded = p.sb("up", [P, E0 * 4 * H0]), p.sem("up_loaded")
            start_loads(nc, [(up[:, e * 4 * H0:(e + 1) * 4 * H0], a["f0_w13"][:, e * 4 * H0:(e + 1) * 4 * H0])
                             for e in range(E0)], up_loaded)
            routing = Routing(nc, part, "route0", E0)
            with ExitStack() as inner:
                XN = Memory(nc, inner, "moe0x").sb("XN", [P, NT * D])
                layer_norm(nc, "ln1", X, XN)
                routing.route(nc, const, XN, a["f0_router"], None, in0, zeroed[0])
            gated_experts(nc, const, routing, in0, out0, up, up_loaded, a["f0_w2"])
            combine(nc, routing, out0, X)
        with ExitStack() as part:
            p = Memory(nc, part, "layer1")
            XN = p.sb("XN", [P, NT * D])
            acc = p.sb("acc", [P, (NT + 1) * D])
            layer_norm(nc, "ln2", X, XN, table=table1)
            aggregate(nc, "agg1", edges, table1, acc, D, True)
            XNT, kv = p.sb("XNT", [P, 2 * NPAD]), p.sb("kv", [P, 2 * (P + 1)])
            graph_and_kv(nc, const, acc, X, XN, XNT, kv, a["g1_w"], a["g1_b"], a["m1_kv"], a["m1_kv_b"])
            attend(nc, const, XN, XNT, kv, a["m1_q"], a["m1_q_b"], a["m1_o"], a["m1_o_b"])
            layer_norm(nc, "ln3", XN, XN, a["m1_g1"], a["m1_n1"])
            feed_forward(nc, const, XN, a["m1_w1"], a["m1_b1"], a["m1_w2"], a["m1_b2"])
            layer_norm(nc, "ln4", XN, X, a["m1_g2"], a["m1_n2"], add=X)
        with ExitStack() as part:
            p = Memory(nc, part, "moe1")
            up, up_loaded = p.sb("up", [P, E1 * 2 * H1]), p.sem("up_loaded")
            start_loads(nc, [(up[:, e * 2 * H1:(e + 4) * 2 * H1], a["f1_w1"][:, e * 2 * H1:(e + 4) * 2 * H1])
                             for e in range(0, E1, 4)], up_loaded)
            routing = Routing(nc, part, "route1", E1)
            with ExitStack() as inner:
                XN = Memory(nc, inner, "moe1x").sb("XN", [P, NT * D])
                layer_norm(nc, "ln5", X, XN, table=base1)
                routing.route(nc, const, XN, a["f1_router"], a["f1_router_b"], in1, zeroed[1])
            relu_experts(nc, const, routing, in1, out1, up, up_loaded, a["f1_b1"], a["f1_w2"], a["f1_b2"])
            Y = Memory(nc, part, "last").sb("Y", [P, NT * D])
            combine(nc, routing, out1, Y, base1)
            layer_norm(nc, "ln6", Y, X, a["f1_gamma"], a["f1_beta"], add=X)
        store_nodes(nc, X, out)


def chunks(w):
    k, n = w.shape
    return w.reshape(k // P, P, n).transpose(1, 0, 2).reshape(P, -1)


def columns(v):
    return v.reshape(-1, P).T


def kernel(**inputs):
    import numpy as np
    import concourse.bacc as bacc
    from concourse.bass_utils import run_bass_kernel_spmd

    i = {k: np.asarray(v) for k, v in inputs.items()}

    def edge_columns(v, fill):
        return np.concatenate([v, np.full(EPAD - E, fill, v.dtype)]).reshape(ET, P).T

    def edge_tiles(v, fill):
        return np.concatenate([v, np.full(ECH * P * P - E, fill, v.dtype)]).reshape(ECH * P, P)

    spare = NPAD - 1
    a = {
        "x": i["x"],
        "src": edge_columns(i["src"], spare),
        "dst": edge_columns(i["dst"], spare),
        "edge_weight": edge_columns(i["edge_weight"], 0),
        "src_rows": edge_tiles(i["src"], spare),
        "dst_rows": edge_tiles(i["dst"], spare),
        "weight_rows": edge_tiles(i["edge_weight"], 0),
        "edge_rows": np.concatenate([i["edge_attr_64"], np.zeros((EPAD - E, DE), i["edge_attr_64"].dtype)]),
        "g0_w": i["L0_gnn_weight"], "g0_b": i["L0_gnn_bias"],
        "m0_qkv": chunks(i["L0_mix_w_qkv"][:, :, 2].T),
        "m0_gamma": columns(i["L0_mix_bn_gamma"]), "m0_beta": columns(i["L0_mix_bn_beta"]),
        "m0_dw": columns(i["L0_mix_w_dw"][:, 0, 2]),
        "m0_pw": i["L0_mix_w_pw"][:, :, 0].reshape(CH0, 4, 32, 32).transpose(1, 3, 0, 2).reshape(4, 32, -1),
        "m0_res": chunks(i["L0_mix_w_res"][:, :, 0].T), "m0_res_b": i["L0_mix_b_res"],
        "f0_router": chunks(i["L0_ffn_router_w"].T),
        "f0_w13": np.stack([i["L0_ffn_w1"], i["L0_ffn_w3"]]).reshape(2, E0, H0, 2, P).transpose(4, 1, 3, 0, 2).reshape(P, -1),
        "f0_w2": np.concatenate([i["L0_ffn_w2"].transpose(2, 0, 1), np.zeros((HC * HK - H0, E0, D), i["L0_ffn_w2"].dtype)])
                 .reshape(HC, HK, E0, D).transpose(1, 2, 0, 3).reshape(HK, -1),
        "g1_w": chunks(np.concatenate([i["L1_gnn_W1"].T, i["L1_gnn_W2"].T])),
        "g1_b": np.stack([i["L1_gnn_b1"], i["L1_gnn_b2"]]),
        "m1_kv": chunks(np.concatenate([i["L1_mix_Wk"], i["L1_mix_Wv"]], 1)),
        "m1_kv_b": np.concatenate([i["L1_mix_bk"], i["L1_mix_bv"]]),
        "m1_q": chunks(i["L1_mix_Wq"]), "m1_q_b": columns(i["L1_mix_bq"]),
        "m1_o": chunks(i["L1_mix_Wo"]), "m1_o_b": i["L1_mix_bo"],
        "m1_w1": chunks(i["L1_mix_W1"]), "m1_b1": columns(i["L1_mix_b1"]),
        "m1_w2": chunks(i["L1_mix_W2"]), "m1_b2": i["L1_mix_b2"],
        "m1_g1": i["L1_mix_ln1_g"], "m1_n1": i["L1_mix_ln1_b"],
        "m1_g2": i["L1_mix_ln2_g"], "m1_n2": i["L1_mix_ln2_b"],
        "f1_router": chunks(i["L1_ffn_gate_w"]), "f1_router_b": i["L1_ffn_gate_b"],
        "f1_w1": i["L1_ffn_w1"].reshape(E1, 2, P, H1).transpose(2, 0, 1, 3).reshape(P, -1),
        "f1_b1": i["L1_ffn_b1"].reshape(E1, H1 // P, P).transpose(2, 0, 1).reshape(P, -1),
        "f1_w2": i["L1_ffn_w2"].reshape(E1, H1 // P, P, D).transpose(2, 0, 1, 3).reshape(P, -1),
        "f1_b2": i["L1_ffn_b2"].reshape(-1),
        "f1_gamma": i["L1_ffn_gamma"], "f1_beta": i["L1_ffn_beta"],
    }
    a = {k: np.ascontiguousarray(v) for k, v in a.items()}
    nc = bacc.Bacc("TRN2", target_bir_lowering=False, num_devices=1)
    aps = {k: nc.dram_tensor(f"in_{k}", v.shape, mybir.dt.from_np(v.dtype), kind="ExternalInput").ap() for k, v in a.items()}
    out = nc.dram_tensor("out_0", (N, D), F32, kind="ExternalOutput").ap()
    build(nc, aps, out)
    r = run_bass_kernel_spmd(nc, [{f"in_{k}": v for k, v in a.items()}], core_ids=[0])
    return r.results[0]["out_0"]
```

```python
import math
from contextlib import ExitStack

import concourse.bass as bass
from concourse import mybir

F32 = mybir.dt.float32
I32 = mybir.dt.int32
BF16 = mybir.dt.bfloat16
ALU = mybir.AluOpType
ACT = mybir.ActivationFunctionType
AX_X = mybir.AxisListType.X

P = 128
N = 3125
D = 256
DE = 64
E = 50000
NT = -(-N // P)
NTAIL = N - (NT - 1) * P
NPAD = NT * P
ET = -(-E // P)
EPAD = ET * P
ECH = -(-ET // P)
SL = 8
SP = 4
PAIRS = -(-(ET + NT - 1) // SL) * SL
HB = 17
C0 = 768
CH0 = C0 // P
GRP = 16
GT = 5
NG = NT // GT
GN = GT * P
GH = GN // 2
FF = 1024
HEADS = 8
assert ET % HB == 0 and NT % GT == 0 and PAIRS // SL % 2 == 0
MAXNORM = 0.9999899864196777
ATANH_MAXNORM = 0.5 * math.log((1 + MAXNORM) / (1 - MAXNORM))
MINNORM = 1e-15


class Chain:

    def __init__(self, eng, sem, base=0):
        self.eng, self.sem, self.base, self.n = eng, sem, base, 0

    def did(self, ins):
        ins.then_inc(self.sem, 1)
        self.n += 1

    def settle(self):
        self.eng.wait_ge(self.sem, self.base + self.n)

    def step(self, ins):
        self.did(ins)
        self.settle()


class Memory:

    def __init__(self, nc, ctx, tag):
        self.nc, self.ctx, self.tag, self.sems = nc, ctx, tag, []

    def sb(self, name, shape, dt=F32):
        return self.ctx.enter_context(self.nc.sbuf_tensor(f"{self.tag}_{name}", shape, dt))

    def ps(self, name, shape, dt=F32):
        return self.ctx.enter_context(self.nc.psum_tensor(f"{self.tag}_{name}", shape, dt))

    def sem(self, name):
        if not self.sems:
            self.ctx.callback(self.release)
        self.sems.append(self.nc.alloc_semaphore(f"{self.tag}_{name}"))
        return self.sems[-1]

    def release(self):
        self.nc.clear_and_free_semaphores(self.sems)
        self.nc.all_engine_barrier(sem_only=True)


def row(v):
    return v.rearrange("(a n) -> a n", a=1).to_broadcast([P, v.shape[0]])


def at(buf, start, size):
    return buf[:, bass.ds(start, size)]


def refine(c, r, x, tmp):
    dve = c.eng
    c.step(dve.tensor_tensor(tmp[:, :], r[:, :], r[:, :], ALU.mult))
    c.step(dve.tensor_tensor(tmp[:, :], tmp[:, :], x[:, :], ALU.mult))
    c.step(dve.tensor_scalar(tmp[:, :], tmp[:, :], -0.5, 1.5, ALU.mult, ALU.add))
    c.step(dve.tensor_tensor(r[:, :], r[:, :], tmp[:, :], ALU.mult))


class Constants:

    def __init__(self, nc, ctx):
        m = Memory(nc, ctx, "const")
        self.ident = m.sb("ident", [P, P])
        self.before = m.sb("before", [P, P])
        self.ones = m.sb("ones", [P, P])
        self.valid = m.sb("valid", [P, NT])
        self.part = m.sb("part", [P, 1])
        self.zero = m.sb("zero", [P, D])
        built = m.sem("built")
        with nc.Block() as block:

            @block.gpsimd
            def _(pool):
                pool.memset(self.ident[:, :], 0.0).then_inc(built, 1)
                pool.memset(self.before[:, :], 0.0).then_inc(built, 1)
                pool.memset(self.ones[:, :], 1.0).then_inc(built, 1)
                pool.memset(self.valid[:, :], 1.0).then_inc(built, 1)
                pool.iota(self.part[:, :], pattern=[[0, 1]], base=0, channel_multiplier=1,
                          allow_small_or_imprecise_dtypes=True).then_inc(built, 1)
                pool.wait_ge(built, 5)
                pool.affine_select(out=self.ident[:, :], in_=self.ident[:, :], compare_op=ALU.not_equal, fill=1.0,
                                   base=0, pattern=[[-1, P]], channel_multiplier=1).then_inc(built, 1)
                pool.affine_select(out=self.before[:, :], in_=self.before[:, :], compare_op=ALU.is_ge, fill=1.0,
                                   base=0, pattern=[[-1, P]], channel_multiplier=1).then_inc(built, 1)
                pool.affine_select(out=self.valid[:, :], in_=self.valid[:, :], compare_op=ALU.is_ge, fill=0.0,
                                   base=N - 1, pattern=[[-P, NT]], channel_multiplier=-1).then_inc(built, 1)
                pool.memset(self.zero[:, :], 0.0).then_inc(built, 1)
                pool.wait_ge(built, 9)


def start_loads(nc, pieces, loaded):
    with nc.Block() as block:

        @block.scalar
        def _(act):
            for to, of in pieces:
                act.dma_start(to, of).then_inc(loaded, 16)


def fills(slots):
    return -(-slots.shape[0] // (8 * P))


def start_clearing(nc, const, slots, cleared):
    flat = slots.rearrange("(t p) d -> p t d", p=P)
    tiles = slots.shape[0] // P
    start_loads(nc, [(flat[:, t:min(t + 8, tiles), :],
                      const.zero[:, :].unsqueeze(1).to_broadcast([P, min(8, tiles - t), D])) for t in range(0, tiles, 8)],
                cleared)


def start_nodes(nc, x, X, loaded):
    with ExitStack() as ctx:
        m = Memory(nc, ctx, "load")
        cleared = m.sem("cleared")
        block = ctx.enter_context(nc.Block())
        full = (NT - 1) * P

        @block.vector
        def _(dve):
            dve.memset(X[:, (NT - 1) * D:NT * D], 0.0).then_inc(cleared, 1)

        @block.sync
        def _(sp):
            sp.dma_start(X[:, 0:(NT - 1) * D].rearrange("p (i d) -> p i d", d=D),
                         x[0:full, :].rearrange("(i p) d -> p i d", p=P)).then_inc(loaded, 16)
            sp.wait_ge(cleared, 1)
            sp.dma_start(X[0:NTAIL, (NT - 1) * D:NT * D], x[full:N, :]).then_inc(loaded, 16)


def layer_norm(nc, tag, src, dst, gamma=None, beta=None, add=None, table=None, scale=None, sumsq=None, eps=1e-5,
               src_loaded=None, table_stored=None, out=None):
    with ExitStack() as ctx:
        m = Memory(nc, ctx, tag)
        stats = m.sb("stats", [P, NT * 6])
        mean, var, tmp, rstd = (m.sb(n, [P, NT]) for n in ("mean", "var", "tmp", "rstd"))
        if scale is not None:
            row_out = [m.sb(f"row_out{k}", [P, GT * D]) for k in range(2)]
        square = m.sb("square", [P, D])
        chain, var_ready, root_ready = m.sem("chain"), m.sem("var_ready"), m.sem("root_ready")
        tile_ready, rows_ready = m.sem("tile_ready"), m.sem("rows_ready")
        row_stored = [m.sem(f"row_stored{k}") for k in range(2)]
        squared = m.sem("squared")
        if gamma is not None:
            gamma_row, beta_row = m.sb("gamma_row", [P, D]), m.sb("beta_row", [P, D])
            shift = m.sb("shift", [P, NT])
            affine_loaded, shift_ready, normed = m.sem("affine_loaded"), m.sem("shift_ready"), m.sem("normed")
            add_ready, group_ready, stored = m.sem("add_ready"), m.sem("group_ready"), m.sem("stored")
        block = ctx.enter_context(nc.Block())
        st = stats[:, :].rearrange("p (i s) -> p i s", s=6)

        @block.vector
        def _(dve):
            c = Chain(dve, chain)
            if src_loaded is not None:
                dve.wait_ge(src_loaded, 32)
            with dve.Fori(0, NG) as g:
                for n in range(GT):
                    dve.bn_stats(at(stats, (g * GT + n) * 6, 6), at(src, (g * GT + n) * D, D)).then_inc(chain, 1)
            c.n = NT
            c.settle()
            c.did(dve.tensor_tensor(mean[:, :], st[:, :, 1], st[:, :, 4], ALU.add))
            c.did(dve.tensor_tensor(var[:, :], st[:, :, 2], st[:, :, 5], ALU.add))
            c.step(dve.tensor_tensor(tmp[:, :], st[:, :, 1], st[:, :, 4], ALU.subtract))
            c.did(dve.tensor_scalar(mean[:, :], mean[:, :], 0.5, None, ALU.mult))
            c.step(dve.scalar_tensor_tensor(out=tmp[:, :], in0=tmp[:, :], scalar=0.25, in1=tmp[:, :],
                                            op0=ALU.mult, op1=ALU.mult))
            c.step(dve.scalar_tensor_tensor(out=var[:, :], in0=var[:, :], scalar=1.0 / D, in1=tmp[:, :],
                                            op0=ALU.mult, op1=ALU.add))
            dve.tensor_scalar(var[:, :], var[:, :], eps, None, ALU.add).then_inc(var_ready, 1)
            dve.wait_ge(root_ready, 1)
            c.step(dve.reciprocal(rstd[:, :], tmp[:, :]))
            refine(c, rstd, var, tmp)
            if gamma is None:
                with dve.Fori(0, NG) as g:
                    for n in range(GT):
                        i = g * GT + n
                        dve.tensor_scalar(at(dst, i * D, D), at(src, i * D, D), at(mean, i, 1), at(rstd, i, 1),
                                          ALU.subtract, ALU.mult).then_inc(tile_ready, 1)
            else:
                c.step(dve.scalar_tensor_tensor(out=shift[:, :], in0=mean[:, :], scalar=-1.0, in1=rstd[:, :],
                                                op0=ALU.mult, op1=ALU.mult))
                dve.sem_inc(shift_ready, 1)
                dve.wait_ge(affine_loaded, 32)
                base, per = c.n, 1
                group = lambda b, g: at(b, g * GT * D, GT * D).rearrange("p (n d) -> p n d", d=D)
                over = lambda r: r[:, :].unsqueeze(1).to_broadcast([P, GT, D])
                with dve.Fori(0, NG) as g:
                    t = Chain(dve, chain, g * per + base)
                    dve.wait_ge(normed, (g + 1) * GT)
                    y = group(src, g)
                    t.step(dve.tensor_tensor(y, y, over(gamma_row), ALU.mult))
                    if add is None:
                        ins = dve.tensor_tensor(group(dst, g), y, over(beta_row), ALU.add)
                    else:
                        dve.wait_ge(add_ready, g + 1)
                        ins = dve.tensor_tensor(group(dst, g), y, group(add, g), ALU.add)
                    ins.then_inc(group_ready, 1)
                    assert t.n == per

        if add is not None:
            assert add is dst

            @block.gpsimd
            def _(pool):
                pool.wait_ge(affine_loaded, 32)
                for g in range(NG):
                    x = add[:, g * GT * D:(g + 1) * GT * D].rearrange("p (n d) -> p n d", d=D)
                    pool.tensor_tensor(x, x, beta_row[:, :].unsqueeze(1).to_broadcast([P, GT, D]), ALU.add)\
                        .then_inc(add_ready, 1)

        @block.scalar
        def _(act):
            if gamma is not None:
                act.dma_start(gamma_row[:, :], row(gamma)).then_inc(affine_loaded, 16)
                act.dma_start(beta_row[:, :], row(beta)).then_inc(affine_loaded, 16)
            act.wait_ge(var_ready, 1)
            act.activation(tmp[:, :], var[:, :], ACT.Sqrt).then_inc(root_ready, 1)
            if gamma is not None:
                act.wait_ge(shift_ready, 1)
                with act.Fori(0, NG) as g:
                    for n in range(GT):
                        i = g * GT + n
                        x = at(src, i * D, D)
                        act.activation(x, x, ACT.Identity, scale=at(rstd, i, 1), bias=at(shift, i, 1)).then_inc(normed, 1)
            if sumsq is not None:
                with act.Fori(0, NG) as g:
                    for n in range(GT):
                        i = g * GT + n
                        act.wait_ge(tile_ready, i + 1)
                        act.wait_ge(squared, i)
                        act.activation(square[:, :], at(dst, i * D, D), ACT.Square,
                                       accum_out=at(sumsq, i, 1)).then_inc(squared, 1)
            if scale is not None:
                def put(g, k, turn):
                    act.wait_ge(row_stored[k], turn * 16)
                    for n in range(GT):
                        i = g * GT + n
                        act.wait_ge(tile_ready, i + 1)
                        act.activation(row_out[k][:, n * D:(n + 1) * D], at(dst, i * D, D), ACT.Copy,
                                       scale=at(scale, i, 1)).then_inc(rows_ready, 1)

                with act.Fori(0, NG // 2) as h:
                    for k in range(2):
                        put(h * 2 + k, k, h)
                put(NG - 1, 0, NG // 2)

        @block.sync
        def _(sp):
            if out is not None:
                for g in range(NG):
                    sp.wait_ge(group_ready, g + 1)
                    first, last = g * GT, min((g + 1) * GT, NT - 1)
                    sp.dma_start(out[first * P:last * P, :].rearrange("(i p) d -> p i d", p=P),
                                 dst[:, first * D:last * D].rearrange("p (i d) -> p i d", d=D)).then_inc(stored, 16)
                sp.dma_start(out[(NT - 1) * P:N, :], dst[0:NTAIL, (NT - 1) * D:NT * D]).then_inc(stored, 16)
                sp.wait_ge(stored, (NG + 1) * 16)
            if table is not None and scale is None:
                with sp.Fori(0, NG) as g:
                    sp.wait_ge(tile_ready, (g + 1) * GT)
                    sp.dma_start(table[bass.ds(g * GT * P, GT * P), :].rearrange("(n p) d -> p n d", p=P),
                                 at(dst, g * GT * D, GT * D).rearrange("p (n d) -> p n d", d=D))\
                        .then_inc(table_stored or row_stored[0], 16)
                if table_stored is None:
                    sp.wait_ge(row_stored[0], NG * 16)
            if scale is not None:
                def store(g, k):
                    sp.wait_ge(rows_ready, (g + 1) * GT)
                    sp.dma_start(table[bass.ds(g * GT * P, GT * P), :].rearrange("(n p) d -> p n d", p=P),
                                 row_out[k][:, :].rearrange("p (n d) -> p n d", d=D)).then_inc(row_stored[k], 16)

                with sp.Fori(0, NG // 2) as h:
                    for k in range(2):
                        store(h * 2 + k, k)
                store(NG - 1, 0)
                sp.wait_ge(row_stored[0], (NG // 2 + 1) * 16)
                sp.wait_ge(row_stored[1], NG // 2 * 16)


class Edges:

    def __init__(self, nc, ctx, const, src, dst, weight, src_rows, dst_rows, weight_rows, norm_out):
        m = Memory(nc, ctx, "edges")
        self.src = m.sb("src", [P, ET], I32)
        self.dst = m.sb("dst", [P, ET])
        self.weight = m.sb("weight", [P, ET])
        self.tile_of = m.sb("tile_of", [1, PAIRS], I32)
        self.window_of = m.sb("window_of", [1, PAIRS], I32)
        self.pairs = m.sb("pairs", [1, 1], I32)
        self.pair_src = m.sb("pair_src", [P, PAIRS], I32)
        self.pair_dst = m.sb("pair_dst", [P, PAIRS])
        self.pair_weight = m.sb("pair_weight", [P, PAIRS])
        with ExitStack() as inner:
            self.build(nc, Memory(nc, inner, "edgelist"), inner, const, src, dst, weight,
                       src_rows, dst_rows, weight_rows, norm_out)

    def build(self, nc, m, ctx, const, src, dst, weight, src_rows, dst_rows, weight_rows, norm_out):
        dst_i = m.sb("dst_i", [P, ET], I32)
        rows_i = m.sb("rows_i", [P, ECH * P], I32)
        rows_f = m.sb("rows_f", [P, ECH * P])
        rows_src_i, rows_src = m.sb("rows_src_i", [P, ECH * P], I32), m.sb("rows_src", [P, ECH * P])
        rows_weight = m.sb("rows_weight", [P, ECH * P])
        ends = m.sb("ends", [P, 2 * ECH])
        ends_i = m.sb("ends_i", [P, 2 * ECH], I32)
        count, start, stop = (m.sb(n, [P, ECH]) for n in ("count", "start", "stop"))
        picked = m.sb("picked", [P, 3 * ECH * P])
        totals = m.sb("totals", [P, ECH])
        tile_no, has = m.sb("tile_no", [P, ECH]), m.sb("has", [P, ECH])
        place = m.sb("place", [P, PAIRS])
        inside = m.sb("inside", [P, ECH * PAIRS])
        rest = m.sb("rest", [P, PAIRS])
        low_i, high_i = m.sb("low_i", [P, ET], I32), m.sb("high_i", [P, ET], I32)
        low, high = m.sb("low", [P, ET]), m.sb("high", [P, ET])
        node = m.sb("node", [P, P])
        is_low, is_high = ([m.sb(f"{n}{k}", [P, HB * w], BF16) for k in range(2)] for n, w in (("is_low", P), ("is_high", NT)))
        blank = m.sb("blank", [P, P], BF16)
        degree, root_of = m.sb("degree", [P, NT]), m.sb("root_of", [P, NT])
        p_sums = m.ps("p_sums", [P, 512])
        p_start, p_total, p_degree = p_sums[:, 0:ECH], p_sums[:, ECH:2 * ECH], p_sums[:, 128:128 + NT]
        p_list = m.ps("p_list", [P, 6 * 512])
        loaded, made, chain = m.sem("loaded"), m.sem("made"), m.sem("chain")
        counted, placed, chosen, listed = m.sem("counted"), m.sem("placed"), m.sem("chosen"), m.sem("listed")
        hot, summed, root, rooted = m.sem("hot"), m.sem("summed"), m.sem("root"), m.sem("rooted")
        block = ctx.enter_context(nc.Block())

        @block.sync
        def _(sp):
            for to, of in ((self.src, src), (dst_i, dst), (self.weight, weight)):
                sp.dma_start(to[:, :], of).then_inc(loaded, 16)
            for to, of in ((rows_i, dst_rows), (rows_src_i, src_rows), (rows_weight, weight_rows)):
                sp.dma_start(to[:, :].rearrange("p (c e) -> p c e", e=P),
                             of.rearrange("(c p) e -> p c e", p=P)).then_inc(loaded, 16)

        @block.gpsimd
        def _(pool):
            pool.iota(tile_no[:, :], pattern=[[P, ECH]], base=0, channel_multiplier=1,
                      allow_small_or_imprecise_dtypes=True).then_inc(made, 1)
            pool.iota(place[:, :], pattern=[[1, PAIRS]], base=0, channel_multiplier=0,
                      allow_small_or_imprecise_dtypes=True).then_inc(made, 1)
            pool.iota(node[:, :], pattern=[[1, P]], base=0, channel_multiplier=0,
                      allow_small_or_imprecise_dtypes=True).then_inc(made, 1)

        @block.vector
        def _(dve):
            c = Chain(dve, chain)
            dve.wait_ge(loaded, 96)
            dve.wait_ge(made, 3)
            c.did(dve.tensor_copy(rows_src[:, :], rows_src_i[:, :]))
            c.did(dve.tensor_copy(self.dst[:, :], dst_i[:, :]))
            c.did(dve.tensor_copy(rows_f[:, :], rows_i[:, :]))
            c.did(dve.tensor_scalar(low_i[:, :], self.src[:, :], P - 1, None, ALU.bitwise_and))
            c.step(dve.tensor_scalar(high_i[:, :], self.src[:, :], 7, None, ALU.arith_shift_right))
            c.did(dve.tensor_copy(low[:, :], low_i[:, :]))
            c.did(dve.tensor_copy(high[:, :], high_i[:, :]))
            r = rows_f[:, :].rearrange("p (c e) -> p c e", e=P)
            c.did(dve.tensor_reduce(ends[:, 0:ECH], r, AX_X, ALU.min))
            c.step(dve.tensor_reduce(ends[:, ECH:], r, AX_X, ALU.max))
            c.step(dve.tensor_copy(ends_i[:, :], ends[:, :]))
            c.step(dve.tensor_scalar(ends_i[:, :], ends_i[:, :], 7, None, ALU.arith_shift_right))
            c.step(dve.tensor_copy(ends[:, :], ends_i[:, :]))
            c.did(dve.tensor_scalar(has[:, :], tile_no[:, :], float(ET), None, ALU.is_lt))
            c.step(dve.scalar_tensor_tensor(out=count[:, :], in0=ends[:, ECH:], scalar=1.0, in1=ends[:, 0:ECH],
                                            op0=ALU.add, op1=ALU.subtract))
            dve.tensor_tensor(count[:, :], count[:, :], has[:, :], ALU.mult).then_inc(counted, 1)
            dve.wait_ge(placed, 2)
            c.did(dve.tensor_copy(start[:, :], p_start))
            c.step(dve.tensor_copy(totals[:, :], p_total))
            for k in range(1, ECH):
                c.step(dve.tensor_scalar(start[:, k:], start[:, k:], totals[:, k - 1:k], None, ALU.add))
            def wide(q):
                return picked[:, q * ECH * P:(q + 1) * ECH * P].rearrange("p (c m) -> p c m", m=P)

            def narrow(v):
                return v[:, :].unsqueeze(2).to_broadcast([P, ECH, P])

            c.did(dve.tensor_tensor(wide(0), narrow(ends[:, 0:ECH]), narrow(start), ALU.subtract))
            c.did(dve.tensor_copy(wide(1), narrow(tile_no)))
            c.did(dve.memset(picked[:, 2 * ECH * P:], 1.0))
            c.did(dve.tensor_tensor(stop[:, :], start[:, :], count[:, :], ALU.add))
            c.step(dve.tensor_reduce(totals[:, 0:1], totals[:, :], AX_X, ALU.add))
            c.did(dve.tensor_copy(self.pairs[:, :], totals[0:1, 0:1]))
            for k in range(ECH):
                own = inside[:, k * PAIRS:(k + 1) * PAIRS]
                c.step(dve.tensor_scalar(own, place[:, :], start[:, k:k + 1], None, ALU.is_ge))
                c.step(dve.scalar_tensor_tensor(out=own, in0=place[:, :], scalar=stop[:, k:k + 1], in1=own,
                                                op0=ALU.is_lt, op1=ALU.mult))
            dve.sem_inc(chosen, 1)
            dve.memset(blank[:, :], 0.0).then_inc(hot, 1)

            def one_hot(i, k):
                dve.tensor_tensor(is_low[k][:, :].rearrange("p (t n) -> p t n", n=P),
                                  node[:, :].unsqueeze(1).to_broadcast([P, HB, P]),
                                  at(low, i * HB, HB).unsqueeze(2).to_broadcast([P, HB, P]), ALU.is_equal).then_inc(hot, 1)
                dve.tensor_tensor(is_high[k][:, :].rearrange("p (t n) -> p t n", n=NT),
                                  node[:, 0:NT].unsqueeze(1).to_broadcast([P, HB, NT]),
                                  at(high, i * HB, HB).unsqueeze(2).to_broadcast([P, HB, NT]), ALU.is_equal).then_inc(hot, 1)

            for k in range(2):
                one_hot(k, k)
            dve.wait_ge(listed, 6)
            c.did(dve.tensor_copy(self.tile_of[:, :], p_list[0:1, 512:512 + PAIRS]))
            c.did(dve.tensor_copy(self.pair_src[:, :], p_list[:, 1536:1536 + PAIRS]))
            c.did(dve.tensor_copy(self.pair_weight[:, :], p_list[:, 2560:2560 + PAIRS]))
            c.did(dve.tensor_scalar(rest[:, :], p_list[:, 1024:1024 + PAIRS], -float(NT), float(NT), ALU.mult, ALU.add))
            w = place[:, :]
            c.step(dve.tensor_tensor(w, w, p_list[:, 0:PAIRS], ALU.add))
            c.step(dve.tensor_tensor(w, w, p_list[:, 1024:1024 + PAIRS], ALU.mult))
            c.step(dve.tensor_tensor(w, w, rest[:, :], ALU.add))
            c.did(dve.tensor_copy(self.window_of[:, :], place[0:1, :]))
            c.did(dve.scalar_tensor_tensor(out=self.pair_dst[:, :], in0=w, scalar=-float(P),
                                           in1=p_list[:, 2048:2048 + PAIRS], op0=ALU.mult, op1=ALU.add))
            with dve.Fori(1, ET // HB // 2) as h:
                for k in range(2):
                    dve.wait_ge(summed, h * 2 + k - 1)
                    one_hot(h * 2 + k, k)
            dve.wait_ge(summed, ET // HB - 2)
            one_hot(ET // HB - 1, 0)
            dve.wait_ge(summed, ET // HB)
            c.step(dve.tensor_copy(degree[:, :], p_degree))
            dve.tensor_scalar(degree[:, :], degree[:, :], 1.0, None, ALU.max).then_inc(root, 1)
            dve.wait_ge(rooted, 1)
            c.step(dve.reciprocal(norm_out[:, :], root_of[:, :]))
            refine(c, norm_out, degree, root_of)

        @block.scalar
        def _(act):
            act.wait_ge(root, 1)
            act.activation(root_of[:, :], degree[:, :], ACT.Sqrt).then_inc(rooted, 1)

        @block.tensor
        def _(pe):
            pe.wait_ge(counted, 1)
            pe.matmul(p_start, const.before[:, :], count[:, :], start=True, stop=True).then_inc(placed, 1)
            pe.matmul(p_total, const.ones[:, :], count[:, :], start=True, stop=True).then_inc(placed, 1)
            pe.wait_ge(chosen, 1)
            for q in range(6):
                of, o = ((picked, q * ECH * P), (rows_src, 0), (rows_f, 0), (rows_weight, 0))[max(q - 2, 0)]
                for k in range(ECH):
                    mm = pe.matmul(p_list[:, q * 512:q * 512 + PAIRS], of[:, o + k * P:o + (k + 1) * P],
                                   inside[:, k * PAIRS:(k + 1) * PAIRS], start=(k == 0), stop=(k == ECH - 1))
                mm.then_inc(listed, 1)
            pe.wait_ge(hot, 1)
            pe.matmul(p_degree, blank[:, :], blank[:, 0:NT], start=True, stop=False)

            def add_up(i, k, last=False):
                pe.wait_ge(hot, i * 2 + 3)
                for h in range(HB):
                    mm = pe.matmul(p_degree, is_low[k][:, h * P:(h + 1) * P], is_high[k][:, h * NT:(h + 1) * NT],
                                   start=False, stop=(last and h == HB - 1))
                mm.then_inc(summed, 1)

            with pe.Fori(0, ET // HB // 2) as h:
                for k in range(2):
                    add_up(h * 2 + k, k)
            add_up(ET // HB - 1, 0, last=True)


def aggregate(nc, tag, edges, table, acc, width, weighted, edge_rows=None):
    with ExitStack() as ctx:
        m = Memory(nc, ctx, tag)
        columns = m.sb("columns", [P, (NT + 1) * P])
        index = m.sb("index", [P, 2 * SL], I32)
        message = m.sb("message", [P, 2 * SL * width])
        onehot = m.sb("onehot", [P, 2 * SL * P])
        partial = [m.ps(f"partial{k}", [P, width]) for k in range(SP)]
        ready, chain = m.sem("ready"), m.sem("chain")
        indexed, marked = m.sem("indexed"), m.sem("marked")
        gathered, featured = ([m.sem(f"{n}{k}") for k in range(2 * SL)] for n in ("gathered", "featured"))
        used, added = ([m.sem(f"{n}{k}") for k in range(SL)] for n in ("used", "added"))
        weighed = m.sem("weighed")
        all_indexed, all_gathered, all_featured, all_marked, all_used, all_added = (
            m.sem(f"all_{n}") for n in ("indexed", "gathered", "featured", "marked", "used", "added"))
        tile_taken, tile_begun, asked = m.sem("tile_taken"), m.sem("tile_begun"), m.sem("asked")
        block = ctx.enter_context(nc.Block())
        rounds = PAIRS // SL

        def msg(k):
            return message[:, k * width:(k + 1) * width]

        def pair_count(eng):
            return eng.value_load(edges.pairs[0:1, 0:1], min_val=0, max_val=ET * NT)

        def tile_of(eng, j):
            return eng.value_load(edges.tile_of[0:1, bass.ds(j, 1)], min_val=0, max_val=ET - 1)

        def window_of(eng, j):
            return eng.value_load(edges.window_of[0:1, bass.ds(j, 1)], min_val=0, max_val=NT)

        def features(eng, j, t):
            return eng.dma_start(message[:, j * width + D:j * width + D + DE], edge_rows[bass.ds(t * P, P), :])

        def feature_round(eng, h, r, n, free):
            for k in range(n, SL, 2):
                t = tile_of(eng, r * SL + k)
                if free is not None:
                    eng.wait_ge(used[k], free)
                features(eng, h * SL + k, t).then_inc(featured[h * SL + k], 16)

        def gather(pool, k, i, sem):
            pool.sem_inc(asked, 1)
            pool.indirect_dma_start(out=message[:, k * width:k * width + D], out_offset=None, in_=table,
                                    in_offset=bass.IndirectOffsetOnAxis(ap=index[:, i:i + 1], axis=0)).then_inc(sem, 16)

        @block.gpsimd
        def _(pool):
            pool.iota(columns[:, :], pattern=[[1, (NT + 1) * P]], base=0, channel_multiplier=0,
                      allow_small_or_imprecise_dtypes=True).then_inc(ready, 1)
            pool.wait_ge(ready, 2)
            pairs = pair_count(pool)
            with pool.If(pairs <= PAIRS):
                for h in range(2):
                    pool.wait_ge(indexed, h + 1)
                    for k in range(SL):
                        gather(pool, h * SL + k, h * SL + k, gathered[h * SL + k])
                with pool.Fori(1, rounds // 2) as q:
                    for h in range(2):
                        r = q * 2 + h
                        pool.wait_ge(indexed, r + 1)
                        for k in range(SL):
                            pool.wait_ge(used[k], r - 1)
                            gather(pool, h * SL + k, h * SL + k, gathered[h * SL + k])
            with pool.Else():
                with pool.Fori(0, ET) as t:
                    pool.wait_ge(all_indexed, t + 1)
                    gather(pool, 0, 0, all_gathered)

        @block.scalar
        def _(act):
            def pick(h, r):
                return act.copy(index[:, h * SL:(h + 1) * SL], edges.pair_src[:, bass.ds(r * SL, SL)])

            pairs = pair_count(act)
            act.wait_ge(ready, 2)
            with act.If(pairs <= PAIRS):
                def weigh(h, r):
                    act.wait_ge(marked, r + 1)
                    for k in range(SL):
                        hot = onehot[:, (h * SL + k) * P:(h * SL + k + 1) * P]
                        ins = act.activation(hot, hot, ACT.Copy, scale=edges.pair_weight[:, bass.ds(r * SL + k, 1)])
                    ins.then_inc(weighed, 1)

                for h in range(2):
                    pick(h, h).then_inc(indexed, 1)
                for h in range(2):
                    if weighted:
                        weigh(h, h)
                    if edge_rows is not None:
                        feature_round(act, h, h, 1, None)
                with act.Fori(1, rounds // 2) as q:
                    for h in range(2):
                        r = q * 2 + h
                        act.wait_ge(used[SL - 1], r - 1)
                        pick(h, r).then_inc(indexed, 1)
                        if weighted:
                            weigh(h, r)
                        if edge_rows is not None:
                            feature_round(act, h, r, 1, r - 1)
            with act.Else():
                with act.Fori(0, ET) as t:
                    act.wait_ge(tile_taken, t)
                    act.copy(index[:, 0:1], edges.src[:, bass.ds(t, 1)]).then_inc(all_indexed, 1)

        @block.sync
        def _(sp):
            if edge_rows is not None:
                pairs = pair_count(sp)
                sp.wait_ge(ready, 2)
                with sp.If(pairs <= PAIRS):
                    for h in range(2):
                        feature_round(sp, h, h, 0, None)
                    with sp.Fori(1, rounds // 2) as q:
                        for h in range(2):
                            feature_round(sp, h, q * 2 + h, 0, q * 2 + h - 1)
                with sp.Else():
                    with sp.Fori(0, ET) as t:
                        sp.wait_ge(tile_taken, t)
                        features(sp, 0, t).then_inc(all_featured, 16)

        @block.vector
        def _(dve):
            c = Chain(dve, chain)
            c.did(dve.memset(acc[:, :], 0.0))
            c.step(dve.memset(message[:, :], 1.0))
            dve.sem_inc(ready, 1)
            dve.wait_ge(ready, 2)

            def mark_round(h, r):
                dve.tensor_tensor(onehot[:, h * SL * P:(h + 1) * SL * P].rearrange("p (k n) -> p k n", n=P),
                                  columns[:, 0:P].unsqueeze(1).to_broadcast([P, SL, P]),
                                  edges.pair_dst[:, bass.ds(r * SL, SL)].unsqueeze(2).to_broadcast([P, SL, P]),
                                  ALU.is_equal).then_inc(marked, 1)

            def mark(k, t, w):
                hot = onehot[:, k * P:(k + 1) * P]
                col = columns[:, bass.ds(w * P, P)]
                if weighted:
                    return dve.tensor_scalar(hot, col, edges.dst[:, bass.ds(t, 1)], edges.weight[:, bass.ds(t, 1)],
                                             ALU.is_equal, ALU.mult)
                return dve.tensor_scalar(hot, col, edges.dst[:, bass.ds(t, 1)], None, ALU.is_equal)

            def add(k, w):
                to = acc[:, bass.ds(w * width, width)]
                return dve.tensor_tensor(to, to, partial[k % SP][:, :], ALU.add)

            pairs = pair_count(dve)
            with dve.If(pairs <= PAIRS):
                def add_round(r):
                    for k in range(SL):
                        w = window_of(dve, r * SL + k)
                        dve.wait_ge(used[k], r + 1)
                        if k:
                            dve.wait_ge(added[k - 1], r + 1)
                        else:
                            dve.wait_ge(added[SL - 1], r)
                        add(k, w).then_inc(added[k], 1)

                mark_round(0, 0)
                with dve.Fori(0, rounds // 2 - 1) as q:
                    for h in range(2):
                        mark_round(1 - h, q * 2 + h + 1)
                        add_round(q * 2 + h)
                mark_round(1, rounds - 1)
                add_round(rounds - 2)
                add_round(rounds - 1)
            with dve.Else():
                with dve.Fori(0, ET) as t:
                    with dve.Fori(0, NT) as w:
                        j = t * NT + w
                        dve.wait_ge(all_used, j)
                        mark(0, t, w).then_inc(all_marked, 1)
                        dve.wait_ge(all_used, j + 1)
                        dve.wait_ge(all_added, j)
                        add(0, w).then_inc(all_added, 1)

        @block.tensor
        def _(pe):
            def product(k, h=0):
                hot = onehot[:, (h * SL + k) * P:(h * SL + k + 1) * P]
                return pe.matmul(partial[k % SP][:, :], hot, msg(h * SL + k), start=True, stop=True)

            pairs = pair_count(pe)
            with pe.If(pairs <= PAIRS):
                with pe.Fori(0, rounds // 2) as q:
                    for h in range(2):
                        r = q * 2 + h
                        pe.wait_ge(weighed if weighted else marked, r + 1)
                        for k in range(SL):
                            pe.wait_ge(gathered[h * SL + k], (q + 1) * 16)
                            if edge_rows is not None:
                                pe.wait_ge(featured[h * SL + k], (q + 1) * 16)
                            if k < SP:
                                pe.wait_ge(added[k + SL - SP], r)
                            else:
                                pe.wait_ge(added[k - SP], r + 1)
                            product(k, h).then_inc(used[k], 1)
            with pe.Else():
                with pe.Fori(0, ET) as t:
                    pe.wait_ge(all_gathered, (t + 1) * 16)
                    if edge_rows is not None:
                        pe.wait_ge(all_featured, (t + 1) * 16)
                    pe.sem_inc(tile_begun, 1)
                    with pe.Fori(0, NT) as w:
                        j = t * NT + w
                        pe.wait_ge(all_marked, j + 1)
                        pe.wait_ge(all_added, j)
                        product(0).then_inc(all_used, 1)
                    pe.wait_ge(all_used, (t + 1) * NT)
                    pe.sem_inc(tile_taken, 1)


def map_scale(nc, sumsq, scale):
    with ExitStack() as ctx:
        m = Memory(nc, ctx, "map")
        norm, inv, short, sq, poly, up, down, tmp = (
            m.sb(n, [P, NT]) for n in ("norm", "inv", "short", "sq", "poly", "up", "down", "tmp"))
        chain, floored, rooted, argued, logged = (m.sem(n) for n in ("chain", "floored", "rooted", "argued", "logged"))
        block = ctx.enter_context(nc.Block())

        @block.vector
        def _(dve):
            c = Chain(dve, chain)
            ts, tt = dve.tensor_scalar, dve.tensor_tensor
            c.step(ts(sq[:, :], sumsq[:, :], MINNORM * MINNORM, None, ALU.max))
            dve.sem_inc(floored, 1)
            dve.wait_ge(rooted, 1)
            c.step(dve.reciprocal(inv[:, :], norm[:, :]))
            refine(c, inv, sq, tmp)
            c.step(tt(norm[:, :], sq[:, :], inv[:, :], ALU.mult))
            c.step(ts(short[:, :], norm[:, :], MAXNORM, None, ALU.min))
            c.did(ts(up[:, :], short[:, :], 1.0, None, ALU.add))
            c.step(ts(down[:, :], short[:, :], -1.0, 1.0, ALU.mult, ALU.add))
            dve.sem_inc(argued, 1)
            c.step(tt(sq[:, :], short[:, :], short[:, :], ALU.mult))
            c.step(ts(poly[:, :], sq[:, :], 1.0 / 17, 1.0 / 15, ALU.mult, ALU.add))
            for d in (13, 11, 9, 7, 5, 3, 1):
                c.step(tt(poly[:, :], poly[:, :], sq[:, :], ALU.mult))
                c.step(ts(poly[:, :], poly[:, :], 1.0 / d, None, ALU.add))
            c.step(tt(poly[:, :], poly[:, :], short[:, :], ALU.mult))
            dve.wait_ge(logged, 2)
            c.step(tt(up[:, :], up[:, :], down[:, :], ALU.subtract))
            c.step(ts(up[:, :], up[:, :], 0.5, None, ALU.mult))
            c.step(ts(tmp[:, :], short[:, :], 0.3, None, ALU.is_gt))
            c.step(tt(up[:, :], up[:, :], tmp[:, :], ALU.mult))
            c.step(ts(tmp[:, :], tmp[:, :], -1.0, 1.0, ALU.mult, ALU.add))
            c.step(tt(poly[:, :], poly[:, :], tmp[:, :], ALU.mult))
            c.step(tt(poly[:, :], poly[:, :], up[:, :], ALU.add))
            c.step(tt(scale[:, :], poly[:, :], inv[:, :], ALU.mult))

        @block.scalar
        def _(act):
            act.wait_ge(floored, 1)
            act.activation(norm[:, :], sq[:, :], ACT.Sqrt).then_inc(rooted, 1)
            act.wait_ge(argued, 1)
            for x in (up, down):
                act.activation(x[:, :], x[:, :], ACT.Ln).then_inc(logged, 1)


def qkv_channels(nc, const, XN, scale, w, YT, stats):
    with ExitStack() as ctx:
        m = Memory(nc, ctx, "qkv")
        weight = m.sb("weight", [P, 2 * C0])
        rows = m.sb("rows", [P, GT * D])
        turned = m.sb("turned", [P, 2 * GN])
        p_turn = [m.ps(f"p_turn{k}", [P, 512]) for k in range(2)]
        p_out = [m.ps(f"p_out{k}", [P, 1024]) for k in range(2)]
        loaded, scaled, turning, kept, made, stored = (
            m.sem(n) for n in ("loaded", "scaled", "turning", "kept", "made", "stored"))
        block = ctx.enter_context(nc.Block())

        @block.sync
        def _(sp):
            sp.dma_start(weight[:, :], w).then_inc(loaded, 16)

        @block.vector
        def _(dve):
            def stage(g):
                dve.wait_ge(turning, g * GT)
                for t in range(GT):
                    dve.tensor_scalar(rows[:, t * D:(t + 1) * D], at(XN, (g * GT + t) * D, D),
                                      at(scale, g * GT + t, 1), None, ALU.mult).then_inc(scaled, 1)

            def measure(g):
                for q in range(CH0):
                    dve.wait_ge(stored, g * CH0 + q + 1)
                    for h in range(2):
                        dve.bn_stats(at(stats, (q * NG + g) * 12 + h * 6, 6), at(YT, q * NPAD + g * GN + h * GH, GH))

            stage(0)
            with dve.Fori(0, NG - 1) as g:
                stage(g + 1)
                measure(g)
            measure(NG - 1)

        @block.tensor
        def _(pe):
            pe.wait_ge(loaded, 16)
            with pe.Fori(0, NG) as g:
                for t in range(GT):
                    pe.wait_ge(scaled, g * GT + t + 1)
                    pe.wait_ge(kept, g * GT + max(t - 1, 0)) if t else pe.wait_ge(kept, g * GT)
                    for c in range(2):
                        mm = pe.transpose(p_turn[t % 2][:, c * P:(c + 1) * P],
                                          rows[:, t * D + c * P:t * D + (c + 1) * P], const.ident[:, :])
                    mm.then_inc(turning, 1)
                pe.wait_ge(kept, (g + 1) * GT)
                for q in range(CH0):
                    if q < 2:
                        pe.wait_ge(stored, g * CH0)
                    else:
                        pe.wait_ge(stored, g * CH0 + q - 1)
                    for h in range(2):
                        for c in range(2):
                            mm = pe.matmul(p_out[q % 2][:, h * 512:h * 512 + GH],
                                           weight[:, c * C0 + q * P:c * C0 + (q + 1) * P],
                                           turned[:, c * GN + h * GH:c * GN + (h + 1) * GH], start=(c == 0), stop=(c == 1))
                    mm.then_inc(made, 1)

        @block.scalar
        def _(act):
            with act.Fori(0, NG) as g:
                act.wait_ge(made, g * CH0)
                for t in range(GT):
                    act.wait_ge(turning, g * GT + t + 1)
                    act.copy(turned[:, :].rearrange("p (c n) -> p c n", c=2)[:, :, t * P:(t + 1) * P],
                             p_turn[t % 2][:, 0:D].rearrange("p (c n) -> p c n", c=2)).then_inc(kept, 1)
                for q in range(CH0):
                    act.wait_ge(made, g * CH0 + q + 1)
                    act.copy(at(YT, q * NPAD + g * GN, GN).rearrange("p (h n) -> p h n", h=2),
                             p_out[q % 2][:, :].rearrange("p (h n) -> p h n", h=2)[:, :, 0:GH]).then_inc(stored, 1)


def batch_norm(nc, stats, gamma, beta, bn_scale, bn_shift):
    with ExitStack() as ctx:
        m = Memory(nc, ctx, "bn")
        gamma_c, beta_c = m.sb("gamma_c", [P, CH0]), m.sb("beta_c", [P, CH0])
        pair = m.sb("pair", [P, 2 * CH0])
        mean, var, root, tmp = (m.sb(n, [P, CH0]) for n in ("mean", "var", "root", "tmp"))
        loaded, chain, ready, rooted = (m.sem(n) for n in ("loaded", "chain", "ready", "rooted"))
        block = ctx.enter_context(nc.Block())

        @block.sync
        def _(sp):
            sp.dma_start(gamma_c[:, :], gamma).then_inc(loaded, 16)
            sp.dma_start(beta_c[:, :], beta).then_inc(loaded, 16)

        @block.vector
        def _(dve):
            c = Chain(dve, chain)
            for q in range(CH0):
                c.did(dve.bn_aggr(pair[:, 2 * q:2 * q + 2], stats[:, q * NG * 12:(q + 1) * NG * 12]))
            c.settle()
            pv = pair[:, :].rearrange("p (q s) -> p q s", s=2)
            c.did(dve.tensor_scalar(mean[:, :], pv[:, :, 0], NPAD / N, None, ALU.mult))
            c.step(dve.scalar_tensor_tensor(out=tmp[:, :], in0=pv[:, :, 0], scalar=-(NPAD * (NPAD - N)) / (N * N),
                                            in1=pv[:, :, 0], op0=ALU.mult, op1=ALU.mult))
            c.step(dve.scalar_tensor_tensor(out=var[:, :], in0=pv[:, :, 1], scalar=NPAD / N, in1=tmp[:, :],
                                            op0=ALU.mult, op1=ALU.add))
            c.step(dve.tensor_scalar(var[:, :], var[:, :], 1e-5, None, ALU.add))
            dve.sem_inc(ready, 1)
            dve.wait_ge(rooted, 1)
            c.step(dve.reciprocal(bn_scale[:, :], root[:, :]))
            refine(c, bn_scale, var, tmp)
            dve.wait_ge(loaded, 32)
            c.step(dve.tensor_tensor(bn_scale[:, :], bn_scale[:, :], gamma_c[:, :], ALU.mult))
            c.step(dve.tensor_tensor(tmp[:, :], mean[:, :], bn_scale[:, :], ALU.mult))
            c.step(dve.tensor_tensor(bn_shift[:, :], beta_c[:, :], tmp[:, :], ALU.subtract))

        @block.scalar
        def _(act):
            act.wait_ge(ready, 1)
            act.activation(root[:, :], var[:, :], ACT.Sqrt).then_inc(rooted, 1)


def graph_and_mixer(nc, const, acc, X, YT, bn_scale, bn_shift, FT, sumsq, gw, gbias, w_dw, w_pw, w_res, b_res):
    AW = D + DE + 1
    with ExitStack() as ctx:
        m = Memory(nc, ctx, "mix")
        g_w = m.sb("g_w", [P, 3 * D])
        g_b, r_b = m.sb("g_b", [P, D]), m.sb("r_b", [P, D])
        taps = m.sb("taps", [P, CH0])
        blocks = m.sb("blocks", [P, C0])
        r_w = m.sb("r_w", [P, 4 * D])
        norm_in, deg, dtmp = m.sb("norm_in", [P, NT]), m.sb("deg", [P, NT]), m.sb("dtmp", [P, NT])
        rT = m.sb("rT", [P, C0])
        agg = m.sb("agg", [P, D + DE])
        aggT = m.sb("aggT", [P, 3 * P])
        square = m.sb("square", [P, C0])
        sums, norms = m.sb("sums", [P, 4]), m.sb("norms", [P, 4])
        size, least, inv, a, b = (m.sb(n, [P, 1]) for n in ("size", "least", "inv", "a", "b"))
        k_sum = m.sb("k_sum", [P, 2 * GRP])
        kr = m.sb("kr", [P, 2 * 512])
        den, prod, prodT = m.sb("den", [P, 512]), m.sb("prod", [P, 512]), m.sb("prodT", [P, 512])
        g_out = m.sb("g_out", [P, D])
        b3, prod_sums, c_b3 = (m.sb(n, [P, NT]) for n in ("b3", "prod_sums", "c_b3"))
        c_tmp = dtmp
        cat = [m.ps(f"cat{k}", [P, 2 * C0]) for k in range(2)]
        p_graph, p_mix = m.ps("p_graph", [P, 512]), m.ps("p_mix", [P, 512])
        loaded, cleared, chain, dwed = m.sem("loaded"), m.sem("cleared"), m.sem("chain"), m.sem("dwed")
        deg_ready, deg_rooted, act_chain = m.sem("deg_ready"), m.sem("deg_rooted"), m.sem("act_chain")
        relued, rT_staged, catted, cat_free, k_made = (
            m.sem(n) for n in ("relued", "rT_staged", "catted", "cat_free", "k_made"))
        staged, agg_turned, agg_kept, gnn_done, gnn_taken = (
            m.sem(n) for n in ("staged", "agg_turned", "agg_kept", "gnn_done", "gnn_taken"))
        prod_ready, prod_turned, prod_kept, prod_squared, res_done, res_kept = (
            m.sem(n) for n in ("prod_ready", "prod_turned", "prod_kept", "prod_squared", "res_done", "res_kept"))
        sums_ready, prods_rooted, ft_ready = m.sem("sums_ready"), m.sem("prods_rooted"), m.sem("ft_ready")
        block = ctx.enter_context(nc.Block())

        def parts(buf, n):
            return buf[:, :].rearrange("p (g c) -> p g c", c=96)[:, :, 32 * n:32 * n + 32]

        @block.sync
        def _(sp):
            sp.wait_ge(cleared, 2)
            sp.dma_start(g_w[:, 0:2 * D].rearrange("p (k d) -> p k d", d=D),
                         gw[0:2 * P, :].rearrange("(k p) d -> p k d", p=P)).then_inc(loaded, 16)
            sp.dma_start(g_w[0:DE, 2 * D:3 * D], gw[2 * P:, :]).then_inc(loaded, 16)
            sp.dma_start(g_b[:, :], row(gbias)).then_inc(loaded, 16)
            sp.dma_start(r_b[:, :], row(b_res)).then_inc(loaded, 16)
            sp.dma_start(taps[:, :], w_dw).then_inc(loaded, 16)
            sp.dma_start(r_w[:, :], w_res).then_inc(loaded, 16)
            for b_ in range(4):
                sp.dma_start(blocks[32 * b_:32 * b_ + 32, :].rearrange("i (q b o) -> i q b o", b=4, o=32)[:, :, b_, :],
                             w_pw[b_, :, :].rearrange("i (q o) -> i q o", o=32)).then_inc(loaded, 16)

        @block.gpsimd
        def _(pool):
            pool.memset(blocks[:, :], 0.0).then_inc(cleared, 1)
            pool.memset(g_w[:, :], 0.0).then_inc(cleared, 1)

            def stage_rT(n, first=False):
                if not first:
                    pool.wait_ge(catted, n)
                pool.tensor_copy(rT[:, :].rearrange("p (q n) -> p q n", n=P),
                                 YT[:, :].rearrange("p (q n) -> p q n", n=NPAD)[:, :, bass.ds(n * P, P)]).then_inc(rT_staged, 1)

            def stage_agg(n, first=False):
                if not first:
                    pool.wait_ge(agg_turned, n)
                pool.tensor_copy(agg[:, :], at(acc, n * AW, D + DE)).then_inc(staged, 1)

            def weigh(i, k):
                pool.wait_ge(cat_free, i + 1)
                p3 = prod[:, :].rearrange("p (g c) -> p g c", c=32)
                pool.tensor_tensor(p3, p3, k_sum[:, k * GRP:(k + 1) * GRP].unsqueeze(2).to_broadcast([P, GRP, 32]), ALU.mult)\
                    .then_inc(prod_ready, 1)

            pool.wait_ge(relued, 2 * CH0)
            stage_rT(0, first=True)
            stage_agg(0, first=True)
            stage_rT(1)
            with pool.Fori(0, NT // 2 - 1) as h:
                for k in range(2):
                    i = h * 2 + k
                    stage_agg(i + 1)
                    stage_rT(i + 2)
                    weigh(i, k)
            stage_agg(NT - 2)
            stage_rT(NT - 1)
            weigh(NT - 3, 0)
            stage_agg(NT - 1)
            weigh(NT - 2, 1)
            weigh(NT - 1, 0)

        @block.vector
        def _(dve):
            c = Chain(dve, chain)
            ts, tt, stt = dve.tensor_scalar, dve.tensor_tensor, dve.scalar_tensor_tensor
            c.step(ts(deg[:, :], acc[:, :].rearrange("p (i a) -> p i a", a=AW)[:, 0:NT, AW - 1], 1.0, None, ALU.max))
            dve.sem_inc(deg_ready, 1)
            for q in range(CH0 // 2):
                y = YT[:, q * NPAD:(q + 1) * NPAD]
                c.step(ts(y, y, bn_scale[:, q:q + 1], bn_shift[:, q:q + 1], ALU.mult, ALU.add))
                ts(y, y, 0.0, None, ALU.max).then_inc(relued, 2)
            dve.wait_ge(deg_rooted, 1)
            c.step(dve.reciprocal(norm_in[:, :], dtmp[:, :]))
            refine(c, norm_in, deg, dtmp)
            dve.wait_ge(loaded, 160)
            for q in range(CH0):
                c.did(ts(blocks[:, q * P:(q + 1) * P], blocks[:, q * P:(q + 1) * P], taps[:, q:q + 1], None, ALU.mult))
            c.settle()
            dve.sem_inc(dwed, 1)
            third = lambda buf: buf[:, :].rearrange("p (g c) -> p g c", c=32)

            def scales(t, n, k):
                t.step(ts(size[:, :], norms[:, 2 * k:2 * k + 1], MINNORM, None, ALU.max))
                yield
                t.did(ts(least[:, :], size[:, :], ATANH_MAXNORM, None, ALU.min))
                t.step(dve.reciprocal(inv[:, :], size[:, :]))
                yield
                t.step(tt(a[:, :], least[:, :], inv[:, :], ALU.mult))
                yield
                t.step(ts(size[:, :], norms[:, 2 * k + 1:2 * k + 2], a[:, 0:1], MINNORM, ALU.mult, ALU.max))
                t.did(dve.tensor_reduce(k_sum[:, k * GRP:(k + 1) * GRP], kr[:, k * 512:(k + 1) * 512].rearrange("p (g c) -> p g c", c=32),
                                        AX_X, ALU.add))
                t.did(ts(least[:, :], size[:, :], ATANH_MAXNORM, None, ALU.min))
                t.step(dve.reciprocal(inv[:, :], size[:, :]))
                t.step(stt(out=b[:, :], in0=least[:, :], scalar=inv[:, 0:1], in1=a[:, :], op0=ALU.mult, op1=ALU.mult))
                t.did(stt(out=at(b3, n, 1), in0=b[:, :], scalar=b[:, 0:1], in1=b[:, :], op0=ALU.mult, op1=ALU.mult))
                yield

            def tile(t, i, k, last=False):
                following = scales(t, i + 1, 1 - k)
                t.step(ts(third(den), parts(cat[k], 2), b[:, 0:1], 1e-15, ALU.mult, ALU.add))
                t.step(dve.reciprocal(den[:, :], den[:, :]))
                dve.wait_ge(prod_turned, i)
                dve.wait_ge(prod_squared, i)
                t.step(tt(third(prod), parts(cat[k], 2), third(den), ALU.mult))
                stt(out=third(prod), in0=parts(cat[k], 0), scalar=0.0, in1=third(prod), op0=ALU.max, op1=ALU.mult)\
                    .then_inc(cat_free, 1)
                if not last:
                    dve.wait_ge(k_made, i + 2)
                    next(following)
                dve.wait_ge(gnn_done, i + 1)
                stt(out=g_out[:, :], in0=p_graph[:, 0:D], scalar=at(norm_in, i, 1), in1=g_b[:, :],
                    op0=ALU.mult, op1=ALU.add).then_inc(gnn_taken, 1)
                if not last:
                    next(following)
                dve.wait_ge(gnn_taken, i + 1)
                t.did(stt(out=at(X, i * D, D), in0=g_out[:, :], scalar=0.0, in1=at(X, i * D, D), op0=ALU.max, op1=ALU.add))
                if not last:
                    next(following)
                    dve.wait_ge(prod_ready, i)
                    next(following)
                t.settle()

            dve.wait_ge(k_made, 1)
            for _ in scales(c, 0, 0):
                pass
            c.settle()
            base, per = c.n, 14
            with dve.Fori(0, NT // 2) as h:
                for k in range(2):
                    t = Chain(dve, chain, (h * 2 + k) * per + base)
                    tile(t, h * 2 + k, k)
                    assert t.n == per, t.n
            c.n = base + (NT - 1) * per
            tile(c, NT - 1, 0, last=True)
            dve.wait_ge(prods_rooted, 1)
            c.step(tt(c_tmp[:, :], prod_sums[:, :], b3[:, :], ALU.mult))
            c.step(ts(c_tmp[:, :], c_tmp[:, :], MINNORM, None, ALU.max))
            c.did(ts(c_b3[:, :], c_tmp[:, :], ATANH_MAXNORM, None, ALU.min))
            c.step(dve.reciprocal(c_tmp[:, :], c_tmp[:, :]))
            c.step(tt(c_b3[:, :], c_b3[:, :], c_tmp[:, :], ALU.mult))
            c.step(tt(c_b3[:, :], c_b3[:, :], b3[:, :], ALU.mult))
            dve.wait_ge(res_kept, NT)
            with dve.Fori(0, NT) as i:
                stt(out=at(FT, i * D, D), in0=at(FT, i * D, D), scalar=at(c_b3, i, 1), in1=r_b[:, :],
                    op0=ALU.mult, op1=ALU.add).then_inc(ft_ready, 1)

        @block.scalar
        def _(act):
            for q in range(CH0 // 2, CH0):
                y = YT[:, q * NPAD:(q + 1) * NPAD]
                act.activation(y, y, ACT.Relu, scale=bn_scale[:, q:q + 1], bias=bn_shift[:, q:q + 1]).then_inc(relued, 2)
            act.wait_ge(deg_ready, 1)
            act.activation(dtmp[:, :], deg[:, :], ACT.Sqrt).then_inc(deg_rooted, 1)

            def norm(n, k):
                c = Chain(act, act_chain, n * 3)
                act.wait_ge(catted, n + 1)
                c.step(act.activation(square[:, :], cat[k][:, 0:C0], ACT.Square, accum_out=sums[:, 2 * k:2 * k + 1]))
                c.step(act.activation(square[:, :], cat[k][:, C0:], ACT.Square, accum_out=sums[:, 2 * k + 1:2 * k + 2]))
                act.activation(norms[:, 2 * k:2 * k + 1], sums[:, 2 * k:2 * k + 1], ACT.Sqrt)
                c.did(act.activation(norms[:, 2 * k + 1:2 * k + 2], sums[:, 2 * k + 1:2 * k + 2], ACT.Sqrt,
                                     bias=sums[:, 2 * k:2 * k + 1]))
                act.activation(kr[:, k * 512:(k + 1) * 512].rearrange("p (g c) -> p g c", c=32), parts(cat[k], 1),
                               ACT.Relu).then_inc(k_made, 1)

            def keep_agg(n):
                act.wait_ge(agg_turned, n + 1)
                act.copy(aggT[:, 0:2 * P], p_graph[:, 0:2 * P])
                act.copy(aggT[0:DE, 2 * P:], p_graph[0:DE, 2 * P:3 * P]).then_inc(agg_kept, 1)

            def keep_res(i):
                act.wait_ge(res_done, i + 1)
                act.copy(at(FT, i * D, D), p_mix[:, 0:D]).then_inc(res_kept, 1)

            def keep_prod(i):
                act.wait_ge(prod_turned, i + 1)
                act.copy(prodT[:, :], p_mix[:, :]).then_inc(prod_kept, 1)

            def square_prod(i, norms_done):
                act.wait_ge(act_chain, norms_done * 3)
                act.activation(square[:, 0:512], prod[:, :], ACT.Square, accum_out=at(prod_sums, i, 1)).then_inc(prod_squared, 1)
                act.wait_ge(prod_squared, i + 1)

            def tile(i, k, first=False):
                norm(i + 1, 1 - k)
                if not first:
                    keep_res(i - 1)
                keep_prod(i)
                keep_agg(i + 1)
                square_prod(i, i + 2)

            norm(0, 0)
            keep_agg(0)
            tile(0, 0, first=True)
            with act.Fori(0, NT // 2 - 1) as h:
                for k in range(2):
                    tile(h * 2 + k + 1, 1 - k)
            tile(NT - 2, 1)
            keep_res(NT - 2)
            keep_prod(NT - 1)
            square_prod(NT - 1, NT)
            keep_res(NT - 1)
            act.activation(prod_sums[:, :], prod_sums[:, :], ACT.Sqrt).then_inc(prods_rooted, 1)
            with act.Fori(0, NT) as i:
                act.wait_ge(ft_ready, i + 1)
                act.activation(square[:, 0:D], at(FT, i * D, D), ACT.Square, accum_out=at(sumsq, i, 1)).then_inc(sums_ready, 1)
                act.wait_ge(sums_ready, i + 1)

        @block.tensor
        def _(pe):
            def make_cat(n, k):
                pe.wait_ge(rT_staged, n + 1)
                for q in range(CH0):
                    pe.transpose(cat[k][:, q * P:(q + 1) * P], rT[:, q * P:(q + 1) * P], const.ident[:, :])
                for q in range(CH0):
                    mm = pe.matmul(cat[k][:, C0 + q * P:C0 + (q + 1) * P], rT[:, q * P:(q + 1) * P],
                                   blocks[:, q * P:(q + 1) * P], start=True, stop=True)
                mm.then_inc(catted, 1)

            def turn_agg(n):
                pe.wait_ge(staged, n + 1)
                for q in range(3):
                    w = P if q < 2 else DE
                    mm = pe.transpose(p_graph[0:w, q * P:(q + 1) * P], agg[:, q * P:q * P + w], const.ident[:, :])
                mm.then_inc(agg_turned, 1)

            def make_graph(i):
                pe.wait_ge(agg_kept, i + 1)
                for q in range(3):
                    w = P if q < 2 else DE
                    mm = pe.matmul(p_graph[:, 0:D], aggT[0:w, q * P:(q + 1) * P], g_w[0:w, q * D:(q + 1) * D],
                                   start=(q == 0), stop=(q == 2))
                mm.then_inc(gnn_done, 1)

            def turn_prod(i):
                pe.wait_ge(prod_ready, i + 1)
                for q in range(4):
                    mm = pe.transpose(p_mix[:, q * P:(q + 1) * P], prod[:, q * P:(q + 1) * P], const.ident[:, :])
                mm.then_inc(prod_turned, 1)

            def make_res(i):
                pe.wait_ge(prod_kept, i + 1)
                for q in range(4):
                    mm = pe.matmul(p_mix[:, 0:D], prodT[:, q * P:(q + 1) * P], r_w[:, q * D:(q + 1) * D],
                                   start=(q == 0), stop=(q == 3))
                mm.then_inc(res_done, 1)

            def tile(i, k, first=False):
                if not first:
                    pe.wait_ge(cat_free, i)
                make_cat(i + 1, 1 - k)
                if not first:
                    make_res(i - 1)
                make_graph(i)
                if not first:
                    pe.wait_ge(res_kept, i)
                turn_prod(i)
                pe.wait_ge(gnn_taken, i + 1)
                turn_agg(i + 1)

            pe.wait_ge(loaded, 160)
            pe.wait_ge(dwed, 1)
            make_cat(0, 0)
            turn_agg(0)
            tile(0, 0, first=True)
            with pe.Fori(0, NT // 2 - 1) as h:
                for k in range(2):
                    tile(h * 2 + k + 1, 1 - k)
            tile(NT - 2, 1)
            make_res(NT - 2)
            make_graph(NT - 1)
            pe.wait_ge(res_kept, NT - 1)
            turn_prod(NT - 1)
            make_res(NT - 1)


def add_mapped(nc, X, FT, sumsq):
    with ExitStack() as ctx:
        m = Memory(nc, ctx, "mapped")
        sq, norm, inv, tmp = (m.sb(n, [P, NT]) for n in ("sq", "norm", "inv", "tmp"))
        chain, floored, rooted, known, tanhed = (m.sem(n) for n in ("chain", "floored", "rooted", "known", "tanhed"))
        block = ctx.enter_context(nc.Block())

        @block.vector
        def _(dve):
            c = Chain(dve, chain)
            c.step(dve.tensor_scalar(sq[:, :], sumsq[:, :], MINNORM * MINNORM, None, ALU.max))
            dve.sem_inc(floored, 1)
            dve.wait_ge(rooted, 1)
            c.step(dve.reciprocal(inv[:, :], norm[:, :]))
            refine(c, inv, sq, tmp)
            c.step(dve.tensor_tensor(norm[:, :], sq[:, :], inv[:, :], ALU.mult))
            dve.sem_inc(known, 1)
            dve.wait_ge(tanhed, 1)
            c.step(dve.scalar_tensor_tensor(out=inv[:, :], in0=tmp[:, :], scalar=MAXNORM, in1=inv[:, :],
                                            op0=ALU.min, op1=ALU.mult))
            with dve.Fori(0, NG) as g:
                for n in range(GT):
                    i = g * GT + n
                    dve.scalar_tensor_tensor(out=at(X, i * D, D), in0=at(FT, i * D, D), scalar=at(inv, i, 1),
                                             in1=at(X, i * D, D), op0=ALU.mult, op1=ALU.add)

        @block.scalar
        def _(act):
            act.wait_ge(floored, 1)
            act.activation(norm[:, :], sq[:, :], ACT.Sqrt).then_inc(rooted, 1)
            act.wait_ge(known, 1)
            act.activation(tmp[:, :], norm[:, :], ACT.Tanh).then_inc(tanhed, 1)


def graph_and_kv(nc, const, acc, X, XN, XNT, kv, gw, kw, weights_loaded, g_bias, kv_bias):
    with ExitStack() as ctx:
        m = Memory(nc, ctx, "kv")
        gb, gb2, kb = m.sb("gb", [P, D]), m.sb("gb2", [P, D]), m.sb("kb", [P, 2 * D])
        xs, us = m.sb("xs", [P, D]), m.sb("us", [P, D])
        xuT, key, neg, v = ([m.sb(f"{n}{k}", [P, w]) for k in range(2)]
                            for n, w in (("xuT", 2 * 2 * P), ("key", D), ("neg", D), ("v", 2 * (P + 1))))
        square, sumsq = m.sb("square", [P, D]), m.sb("sumsq", [P, NT])
        inv, tmp, sq = m.sb("inv", [P, NT]), m.sb("tmp", [P, NT]), m.sb("sq", [P, NT])
        p_x = m.ps("p_x", [P, 512])
        p_kv, p_g, p_a = ([m.ps(f"{n}{k}", [P, 512]) for k in range(2)] for n in ("p_kv", "p_g", "p_a"))
        loaded, chain, x_staged, u_staged, turned, kept, kv_made, g_made, cut, exped, k_ready, summed, g_taken, g_ready, squared, root, rooted = (
            m.sem(n) for n in ("loaded", "chain", "x_staged", "u_staged", "turned", "kept", "kv_made", "g_made", "cut",
                               "exped", "k_ready", "summed", "g_taken", "g_ready", "squared", "root", "rooted"))
        block = ctx.enter_context(nc.Block())

        @block.sync
        def _(sp):
            sp.dma_start(gb[:, :], row(g_bias[0, :])).then_inc(loaded, 16)
            sp.dma_start(gb2[:, :], row(g_bias[1, :])).then_inc(loaded, 16)
            sp.dma_start(kb[:, :], row(kv_bias)).then_inc(loaded, 16)

        @block.vector
        def _(dve):
            c = Chain(dve, chain)
            ts, tt, stt = dve.tensor_scalar, dve.tensor_tensor, dve.scalar_tensor_tensor
            halves = lambda b: b.rearrange("p (c n) -> p c n", c=2)

            def stage(t, n):
                nb = at(acc, n * D, D)
                dve.wait_ge(turned, n)
                t.step(tt(us[:, :], nb, at(XN, n * D, D), ALU.mult))
                tt(us[:, :], us[:, :], nb, ALU.add).then_inc(u_staged, 1)

            def step(t, i, k, first=False, ahead=True, last=False):
                dve.wait_ge(kv_made, i + 1)
                if not first:
                    dve.wait_ge(summed, i - 1)
                t.did(tt(halves(v[k][:, :])[:, :, 0:P], halves(p_kv[k][:, D:2 * D]), halves(kb[:, D:2 * D]), ALU.add))
                t.step(tt(key[k][:, :], p_kv[k][:, 0:D], kb[:, 0:D], ALU.add))
                ts(neg[k][:, :], key[k][:, :], 0.0, None, ALU.min).then_inc(cut, 1)
                if ahead:
                    stage(t, i + 2)
                nb = at(acc, i * D, D)
                dve.wait_ge(g_made, i + 1)
                tt(nb, p_g[k][:, 0:D], gb[:, :], ALU.add).then_inc(g_taken, 1)
                dve.wait_ge(g_taken, i + 1)
                stt(out=nb, in0=nb, scalar=0.2, in1=nb, op0=ALU.mult, op1=ALU.max).then_inc(g_ready, 1)
                dve.wait_ge(exped, i + 1)
                phi = stt(out=key[k][:, :], in0=key[k][:, :], scalar=0.0, in1=neg[k][:, :], op0=ALU.max, op1=ALU.add)
                if last:
                    t.step(phi)
                    phi = ts(key[k][:, :], key[k][:, :], const.valid[:, NT - 1:NT], None, ALU.mult)
                phi.then_inc(k_ready, 1)

            for k in range(2):
                c.did(dve.memset(v[k][:, :], 1.0))
            stage(c, 0)
            dve.wait_ge(loaded, 48)
            c.step(tt(gb[:, :], gb[:, :], gb2[:, :], ALU.add))
            stage(c, 1)
            step(c, 0, 0, first=True)
            base, per = c.n, 3
            with dve.Fori(0, (NT - 3) // 2) as h:
                for k in range(2):
                    t = Chain(dve, chain, (h * 2 + k) * per + base)
                    step(t, h * 2 + k + 1, 1 - k)
                    assert t.n == per, t.n
            c.n = base + (NT - 3) * per
            step(c, NT - 2, 1, ahead=False)
            step(c, NT - 1, 0, ahead=False, last=True)
            dve.wait_ge(squared, NT)
            c.step(ts(sq[:, :], sumsq[:, :], 1e-24, None, ALU.max))
            dve.sem_inc(root, 1)
            dve.wait_ge(summed, NT)
            for k in range(2):
                dve.tensor_copy(kv[:, k * (P + 1):(k + 1) * (P + 1)], p_a[k][:, 0:P + 1])
            dve.wait_ge(rooted, 1)
            c.step(dve.reciprocal(inv[:, :], tmp[:, :]))
            refine(c, inv, sq, tmp)
            with dve.Fori(0, NG) as g:
                for n in range(GT):
                    i = g * GT + n
                    stt(out=at(X, i * D, D), in0=at(acc, i * D, D), scalar=at(inv, i, 1), in1=at(X, i * D, D),
                        op0=ALU.mult, op1=ALU.add)

        @block.scalar
        def _(act):
            def stage(n):
                act.wait_ge(turned, n)
                act.copy(xs[:, :], at(XN, n * D, D)).then_inc(x_staged, 1)

            def keep(n, k, first=False):
                act.wait_ge(turned, n + 1)
                if not first:
                    act.wait_ge(g_made, n - 1)
                act.copy(xuT[k][:, :], p_x[:, :]).then_inc(kept, 1)
                act.copy(XNT[:, :].rearrange("p (c n) -> p c n", c=2)[:, :, bass.ds(n * P, P)],
                         p_x[:, 0:D].rearrange("p (c n) -> p c n", c=2)).then_inc(kept, 1)

            def step(i, k, next_=True, ahead=True):
                if next_:
                    keep(i + 1, 1 - k)
                if ahead:
                    stage(i + 2)
                act.wait_ge(cut, i + 1)
                act.activation(neg[k][:, :], neg[k][:, :], ACT.Exp).then_inc(exped, 1)
                act.wait_ge(g_ready, i + 1)
                act.wait_ge(squared, i)
                act.activation(square[:, :], at(acc, i * D, D), ACT.Square, accum_out=at(sumsq, i, 1)).then_inc(squared, 1)

            stage(0)
            keep(0, 0, first=True)
            stage(1)
            step(0, 0)
            with act.Fori(0, (NT - 3) // 2) as h:
                for k in range(2):
                    step(h * 2 + k + 1, 1 - k)
            step(NT - 2, 1, ahead=False)
            step(NT - 1, 0, next_=False, ahead=False)
            act.wait_ge(root, 1)
            act.activation(tmp[:, :], sq[:, :], ACT.Sqrt).then_inc(rooted, 1)

        @block.tensor
        def _(pe):
            def turn(n):
                pe.wait_ge(x_staged, n + 1)
                pe.wait_ge(u_staged, n + 1)
                pe.wait_ge(kept, n * 2)
                for h in range(4):
                    mm = pe.transpose(p_x[:, h * P:(h + 1) * P], (xs, us)[h // 2][:, (h % 2) * P:(h % 2 + 1) * P],
                                      const.ident[:, :])
                mm.then_inc(turned, 1)

            def make(i, k, first=False):
                pe.wait_ge(kept, (i + 1) * 2)
                if not first:
                    pe.wait_ge(cut, i - 1)
                    pe.wait_ge(g_taken, i - 1)
                for h in range(2):
                    mm = pe.matmul(p_kv[k][:, :], xuT[k][:, h * P:(h + 1) * P], kw[:, h * 2 * D:(h + 1) * 2 * D],
                                   start=(h == 0), stop=(h == 1))
                mm.then_inc(kv_made, 1)
                for h in range(4):
                    mm = pe.matmul(p_g[k][:, 0:D], xuT[k][:, h * P:(h + 1) * P], gw[:, h * D:(h + 1) * D],
                                   start=(h == 0), stop=(h == 3))
                mm.then_inc(g_made, 1)

            def into_kv(i, k, last=False):
                pe.wait_ge(k_ready, i + 1)
                for h in range(2):
                    mm = pe.matmul(p_a[h][:, 0:P + 1], key[k][:, h * P:(h + 1) * P], v[k][:, h * (P + 1):(h + 1) * (P + 1)],
                                   start=False, stop=last)
                mm.then_inc(summed, 1)

            for h in range(2):
                pe.matmul(p_a[h][:, 0:P + 1], const.zero[:, 0:P], const.zero[:, 0:P + 1], start=True, stop=False)
            turn(0)
            pe.wait_ge(weights_loaded, 64)
            turn(1)
            make(0, 0, first=True)
            with pe.Fori(0, (NT - 3) // 2) as h:
                for k in range(2):
                    i = h * 2 + k + 1
                    turn(i + 1)
                    make(i, 1 - k)
                    into_kv(i - 1, k)
            turn(NT - 1)
            make(NT - 2, 1)
            into_kv(NT - 3, 0)
            make(NT - 1, 0)
            into_kv(NT - 2, 1)
            into_kv(NT - 1, 0, last=True)


def attend(nc, const, XN, XNT, kv, q_w, q_bias, o_w, o_bias):
    HW = P + HEADS // 2
    with ExitStack() as ctx:
        m = Memory(nc, ctx, "att")
        qw, ow, ob, qb = m.sb("qw", [P, 2 * D]), m.sb("ow", [P, 2 * D]), m.sb("ob", [P, D]), m.sb("qb", [P, 2])
        heads = m.sb("heads", [P, 2 * HW])
        pos, neg = ([m.sb(f"{n}{k}", [P, 2 * GN]) for k in range(2)] for n in ("pos", "neg"))
        z, o = ([m.sb(f"{n}{k}", [P, w]) for k in range(2)] for n, w in (("z", HEADS), ("o", D)))
        oT, res = m.sb("oT", [P, D]), m.sb("res", [P, D])
        p_q = [m.ps(f"p_q{k}", [P, 1024]) for k in range(2)]
        p_n = [m.ps(f"p_n{k}", [P, 512]) for k in range(2)]
        p_t, p_o = (m.ps(n, [P, 512]) for n in ("p_t", "p_o"))
        loaded, chain, q_made, cut, exped, q_ready, summed, o_ready, turned, kept, made, taken, headed = (
            m.sem(n) for n in ("loaded", "chain", "q_made", "cut", "exped", "q_ready", "summed", "o_ready", "turned",
                               "kept", "made", "taken", "headed"))
        block = ctx.enter_context(nc.Block())
        halves = lambda b, w: b.rearrange("p (h n) -> p h n", h=2)[:, :, 0:w]

        @block.sync
        def _(sp):
            sp.dma_start(qw[:, :], q_w).then_inc(loaded, 16)
            sp.dma_start(qb[:, :], q_bias).then_inc(loaded, 16)
            sp.dma_start(ow[:, :], o_w).then_inc(loaded, 16)
            sp.dma_start(ob[:, :], row(o_bias)).then_inc(loaded, 16)

        @block.vector
        def _(dve):
            c = Chain(dve, chain)
            ts, tt = dve.tensor_scalar, dve.tensor_tensor
            c.step(dve.memset(heads[:, :], 0.0))
            for h in range(2):
                for b in range(4):
                    r = slice(32 * b, 32 * b + 32)
                    c.did(dve.tensor_copy(heads[r, h * HW + 32 * b:h * HW + 32 * b + 32],
                                          kv[r, h * (P + 1) + 32 * b:h * (P + 1) + 32 * b + 32]))
                    c.did(dve.tensor_copy(heads[r, h * HW + P + b:h * HW + P + b + 1],
                                          kv[r, h * (P + 1) + P:(h + 1) * (P + 1)]))
            c.settle()
            dve.sem_inc(headed, 1)
            dve.wait_ge(loaded, 64)

            def cut_queries(g):
                for h in range(2):
                    dve.wait_ge(q_made, g * 2 + h + 1)
                    for to, op in ((pos, ALU.max), (neg, ALU.min)):
                        c.did(ts(halves(to[g % 2][:, h * GN:(h + 1) * GN], GH), halves(p_q[h][:, :], GH), qb[:, h:h + 1],
                                 0.0, ALU.add, op))
                c.settle()
                dve.sem_inc(cut, 1)

            def finish_queries(g):
                dve.wait_ge(exped, g + 1)
                tt(pos[g % 2][:, :], pos[g % 2][:, :], neg[g % 2][:, :], ALU.add).then_inc(q_ready, 1)

            def quotient(i):
                k = i % 2
                dve.wait_ge(summed, i + 1)
                c.step(ts(z[k][:, :].rearrange("p (c h) -> p c h", c=2),
                          p_n[k][:, 0:2 * HW].rearrange("p (c n) -> p c n", c=2)[:, :, P:HW], 1e-6, None, ALU.add))
                c.step(dve.reciprocal(z[k][:, :], z[k][:, :]))
                if i > 1:
                    dve.wait_ge(turned, i - 1)
                for h in range(2):
                    last = tt(o[k][:, h * P:(h + 1) * P].rearrange("p (h e) -> p h e", e=32),
                              p_n[k][:, h * HW:h * HW + P].rearrange("p (h e) -> p h e", e=32),
                              z[k][:, 4 * h:4 * h + 4].unsqueeze(2).to_broadcast([P, 4, 32]), ALU.mult)
                    if h == 0:
                        c.did(last)
                last.then_inc(o_ready, 1)

            def output(i):
                dve.wait_ge(made, i + 1)
                c.settle()
                tt(res[:, :], p_o[:, 0:D], ob[:, :], ALU.add).then_inc(taken, 1)
                dve.wait_ge(taken, i + 1)
                x = XN[:, i * D:(i + 1) * D]
                c.did(tt(x, x, res[:, :], ALU.add))

            cut_queries(0)
            finish_queries(0)
            for i in range(NT):
                quotient(i)
                if i > 1:
                    output(i - 2)
                if i % GT == 1 and i // GT + 1 < NG:
                    cut_queries(i // GT + 1)
                if i % GT == 2 and i // GT + 1 < NG:
                    finish_queries(i // GT + 1)
            output(NT - 2)
            output(NT - 1)

        @block.scalar
        def _(act):
            def exps(g):
                act.wait_ge(cut, g + 1)
                act.activation(neg[g % 2][:, :], neg[g % 2][:, :], ACT.Exp).then_inc(exped, 1)

            exps(0)
            for i in range(NT):
                if i % GT == 2 and i // GT + 1 < NG:
                    exps(i // GT + 1)
                act.wait_ge(turned, i + 1)
                if i:
                    act.wait_ge(made, i)
                act.copy(oT[:, :], p_t[:, 0:D]).then_inc(kept, 1)

        @block.tensor
        def _(pe):
            def queries(g):
                if g:
                    pe.wait_ge(cut, g)
                for h in range(2):
                    for s in range(2):
                        for c in range(2):
                            x = g * GN + c * NPAD + s * GH
                            mm = pe.matmul(p_q[h][:, s * 512:s * 512 + GH], qw[:, c * D + h * P:c * D + (h + 1) * P],
                                           XNT[:, x:x + GH], start=(c == 0), stop=(c == 1))
                    mm.then_inc(q_made, 1)

            def attended(i):
                g, n = divmod(i, GT)
                pe.wait_ge(q_ready, g + 1)
                if i > 1:
                    pe.wait_ge(o_ready, i - 1)
                for h in range(2):
                    mm = pe.matmul(p_n[i % 2][:, h * HW:(h + 1) * HW], pos[g % 2][:, h * GN + n * P:h * GN + (n + 1) * P],
                                   heads[:, h * HW:(h + 1) * HW], start=True, stop=True)
                mm.then_inc(summed, 1)

            def output(i):
                pe.wait_ge(kept, i + 1)
                if i:
                    pe.wait_ge(taken, i)
                for h in range(2):
                    mm = pe.matmul(p_o[:, 0:D], oT[:, h * P:(h + 1) * P], ow[:, h * D:(h + 1) * D],
                                   start=(h == 0), stop=(h == 1))
                mm.then_inc(made, 1)

            pe.wait_ge(loaded, 64)
            queries(0)
            pe.wait_ge(headed, 1)
            attended(0)
            for i in range(NT):
                if i + 1 < NT:
                    attended(i + 1)
                pe.wait_ge(o_ready, i + 1)
                if i:
                    pe.wait_ge(kept, i)
                for h in range(2):
                    mm = pe.transpose(p_t[:, h * P:(h + 1) * P], o[i % 2][:, h * P:(h + 1) * P], const.ident[:, :])
                mm.then_inc(turned, 1)
                if i:
                    output(i - 1)
                if i % GT == 0 and i // GT + 1 < NG:
                    queries(i // GT + 1)
            output(NT - 1)


def feed_forward(nc, const, XN, w1_, w2_, weights_loaded, b1, b2):
    M = FF // P
    with ExitStack() as ctx:
        m = Memory(nc, ctx, "ff")
        b1_, b2_ = m.sb("b1", [P, M]), m.sb("b2", [P, D])
        rows, xT, hT, res = m.sb("rows", [P, GT * D]), m.sb("xT", [P, 2 * GN]), m.sb("hT", [P, M * GN]), m.sb("res", [P, D])
        p_t, p_y = ([m.ps(f"{n}{k}", [P, 512]) for k in range(2)] for n in ("p_t", "p_y"))
        p_h = [m.ps(f"p_h{k}", [P, 1024]) for k in range(2)]
        loaded, chain, staged, turned, kept, h_made, h_ready, made, taken = (
            m.sem(n) for n in ("loaded", "chain", "staged", "turned", "kept", "h_made", "h_ready", "made", "taken"))
        block = ctx.enter_context(nc.Block())

        @block.sync
        def _(sp):
            sp.dma_start(b1_[:, :], b1).then_inc(loaded, 16)
            sp.dma_start(b2_[:, :], row(b2)).then_inc(loaded, 16)

        @block.vector
        def _(dve):
            def stage(g):
                dve.wait_ge(turned, g * GT)
                dve.tensor_copy(rows[:, :], at(XN, g * GT * D, GT * D)).then_inc(staged, 1)

            def outputs(g):
                t = Chain(dve, chain, g * 2 * GT)
                for n in range(GT):
                    i = g * GT + n
                    dve.wait_ge(made, i + 1)
                    t.step(dve.tensor_tensor(res[:, :], p_y[n % 2][:, 0:D], b2_[:, :], ALU.add))
                    dve.sem_inc(taken, 1)
                    t.step(dve.tensor_tensor(at(XN, i * D, D), at(XN, i * D, D), res[:, :], ALU.add))

            stage(0)
            dve.wait_ge(loaded, 32)
            with dve.Fori(0, NG - 1) as g:
                stage(g + 1)
                outputs(g)
            outputs(NG - 1)

        @block.scalar
        def _(act):
            def keep(g):
                act.wait_ge(h_made, g * M)
                for n in range(GT):
                    act.wait_ge(turned, g * GT + n + 1)
                    act.copy(xT[:, :].rearrange("p (c n) -> p c n", c=2)[:, :, n * P:(n + 1) * P],
                             p_t[n % 2][:, 0:D].rearrange("p (c n) -> p c n", c=2)).then_inc(kept, 1)

            def hidden(g):
                act.wait_ge(made, g * GT)
                for q in range(M):
                    act.wait_ge(h_made, g * M + q + 1)
                    act.activation(hT[:, q * GN:(q + 1) * GN].rearrange("p (h n) -> p h n", h=2),
                                   p_h[q % 2][:, :].rearrange("p (h n) -> p h n", h=2)[:, :, 0:GH], ACT.Relu,
                                   bias=b1_[:, q:q + 1]).then_inc(h_ready, 1)

            keep(0)
            act.wait_ge(loaded, 32)
            with act.Fori(0, NG - 1) as g:
                hidden(g)
                keep(g + 1)
            hidden(NG - 1)

        @block.tensor
        def _(pe):
            def turn(g):
                pe.wait_ge(staged, g + 1)
                for n in range(GT):
                    pe.wait_ge(kept, g * GT + max(n - 1, 0))
                    for c in range(2):
                        mm = pe.transpose(p_t[n % 2][:, c * P:(c + 1) * P], rows[:, n * D + c * P:n * D + (c + 1) * P],
                                          const.ident[:, :])
                    mm.then_inc(turned, 1)

            def hidden(g):
                pe.wait_ge(kept, (g + 1) * GT)
                for q in range(M):
                    pe.wait_ge(h_ready, g * M + max(q - 1, 0))
                    for s in range(2):
                        for c in range(2):
                            mm = pe.matmul(p_h[q % 2][:, s * 512:s * 512 + GH], w1_[:, c * FF + q * P:c * FF + (q + 1) * P],
                                           xT[:, c * GN + s * GH:c * GN + (s + 1) * GH], start=(c == 0), stop=(c == 1))
                    mm.then_inc(h_made, 1)

            def outputs(g):
                pe.wait_ge(h_ready, (g + 1) * M)
                for n in range(GT):
                    pe.wait_ge(taken, g * GT + max(n - 1, 0))
                    for q in range(M):
                        mm = pe.matmul(p_y[n % 2][:, 0:D], hT[:, q * GN + n * P:q * GN + (n + 1) * P],
                                       w2_[:, q * D:(q + 1) * D], start=(q == 0), stop=(q == M - 1))
                    mm.then_inc(made, 1)

            turn(0)
            pe.wait_ge(weights_loaded, 64)
            with pe.Fori(0, NG - 1) as g:
                hidden(g)
                turn(g + 1)
                outputs(g)
            hidden(NG - 1)
            outputs(NG - 1)


class Routing:

    def __init__(self, nc, ctx, tag, ne):
        m = Memory(nc, ctx, tag)
        self.ne, self.tag = ne, tag
        self.tiles = -(-((2 * N + ne * (P - 1)) // P) // 2) * 2
        self.gate = [m.sb(f"gate{k}", [P, NT]) for k in range(2)]
        self.slot = [m.sb(f"slot{k}", [P, NT], I32) for k in range(2)]
        self.expert = m.sb("expert", [1, self.tiles + 2], I32)
        self.weight, self.bias_row = m.sb("weight", [P, 2 * ne]), m.sb("bias_row", [P, ne])
        self.loaded = m.sem("loaded")

    def start_weights(self, nc, w, bias):
        start_loads(nc, [(self.weight[:, :], w)] + ([] if bias is None else [(self.bias_row[:, :], row(bias))]), self.loaded)

    def route(self, nc, const, XN, bias, rows_out, zeroed, stored=None):
        with ExitStack() as ctx:
            self.build(nc, Memory(nc, ctx, f"{self.tag}r"), ctx, const, XN, bias, rows_out, zeroed, stored)

    def build(self, nc, m, ctx, const, XN, bias, rows_out, zeroed, stored):
        ne, tj = self.ne, self.tiles
        W = NT * ne
        weight, bias_row, loaded = self.weight, self.bias_row, self.loaded
        turned = [m.sb(f"turned{k}", [P, GT * D]) for k in range(2)]
        logit, work, cand, pos, ends = (m.sb(n, [P, W]) for n in ("logit", "work", "cand", "pos", "ends"))
        hot = [m.sb(f"hot{k}", [P, W]) for k in range(2)]
        first, second, total, pick, big = (m.sb(n, [P, NT]) for n in ("first", "second", "total", "pick", "big"))
        number, base, size = m.sb("number", [P, ne]), m.sb("base", [P, ne]), m.sb("size", [P, ne])
        size_i = m.sb("size_i", [P, ne], I32)
        scatter_i = [m.sb(f"scatter_i{k}", [P, NT], I32) for k in range(2)]
        place, mine = m.sb("place", [1, tj + 2]), m.sb("mine", [1, tj + 2])
        out_row = turned[0]
        out_index = m.sb("out_index", [P, 2 * GT], I32)
        p_t = [m.ps(f"p_t{k}", [P, 3 * 512]) for k in range(2)]
        p_before, p_total = (m.ps(n, [P, 512]) for n in ("p_before", "p_total"))
        p_l = [p_before, p_total]
        made_c, turning, kept, made, taken, chain, exped, asked_exp, counted, ranked = (
            m.sem(n) for n in ("made_c", "turning", "kept", "made", "taken", "chain",
                               "exped", "asked_exp", "counted", "ranked"))
        slotted, row_ready, asked, index_put = (m.sem(n) for n in ("slotted", "row_ready", "asked", "index_put"))
        scattered = [m.sem(f"scattered{k}") for k in range(GT)]
        block = ctx.enter_context(nc.Block())
        three = lambda b: b[:, :].rearrange("p (i e) -> p i e", e=ne)
        over = lambda b: b[:, :].unsqueeze(2).to_broadcast([P, NT, ne])
        numbers = number[:, :].unsqueeze(1).to_broadcast([P, NT, ne])
        slots = (tj + 2) * P

        @block.gpsimd
        def _(pool):
            pool.iota(number[:, :], pattern=[[1, ne]], base=0, channel_multiplier=0,
                      allow_small_or_imprecise_dtypes=True).then_inc(made_c, 1)
            pool.iota(place[:, :], pattern=[[1, tj + 2]], base=0, channel_multiplier=0,
                      allow_small_or_imprecise_dtypes=True).then_inc(made_c, 1)
            pool.wait_ge(zeroed, fills(rows_out) * 16)

            def scatter(i, k):
                pool.wait_ge(row_ready, i + 1)
                pool.sem_inc(asked, 1)
                for s in range(2):
                    pool.indirect_dma_start(
                        out=rows_out, out_offset=bass.IndirectOffsetOnAxis(ap=out_index[:, 2 * k + s:2 * k + s + 1], axis=0),
                        in_=out_row[:, k * D:(k + 1) * D], in_offset=None, bounds_check=slots - 1,
                        oob_is_err=False).then_inc(scattered[k], 16)

            with pool.Fori(0, NG) as g:
                for k in range(GT):
                    scatter(g * GT + k, k)
            for k in range(GT):
                pool.wait_ge(scattered[k], NG * 32)
            if stored is not None:
                pool.wait_ge(stored, NG * 16)

        @block.vector
        def _(dve):
            ts, tt, stt = dve.tensor_scalar, dve.tensor_tensor, dve.scalar_tensor_tensor
            dve.wait_ge(loaded, 16 if bias is None else 32)

            for g in range(NG):
                dve.wait_ge(made, g + 1)
                to, of = logit[:, g * GT * ne:(g + 1) * GT * ne], p_l[g % 2][:, 0:GT * ne]
                if bias is None:
                    ins = dve.tensor_copy(to, of)
                else:
                    ins = tt(to.rearrange("p (i e) -> p i e", e=ne), of.rearrange("p (i e) -> p i e", e=ne),
                             bias_row[:, :].unsqueeze(1).to_broadcast([P, GT, ne]), ALU.add)
                ins.then_inc(taken, 1)
            c = Chain(dve, chain)
            dve.wait_ge(taken, NG)
            dve.wait_ge(made_c, 2)
            c.step(dve.tensor_copy(work[:, :], logit[:, :]))
            for k, top in enumerate((first, second)):
                c.step(dve.tensor_reduce(top[:, :], three(work), AX_X, ALU.max))
                c.step(tt(three(cand), three(work), over(top), ALU.is_equal))
                c.step(ts(cand[:, :], cand[:, :], -64.0, 64.0, ALU.mult, ALU.add))
                c.step(tt(three(cand), three(cand), numbers, ALU.add))
                c.step(dve.tensor_reduce(pick[:, :], three(cand), AX_X, ALU.min))
                c.step(tt(three(hot[k]), numbers, over(pick), ALU.is_equal))
                if k == 0:
                    c.step(stt(out=work[:, :], in0=hot[0][:, :], scalar=-1e30, in1=work[:, :], op0=ALU.mult, op1=ALU.add))
            c.step(tt(work[:, :], hot[0][:, :], hot[1][:, :], ALU.add))
            c.step(tt(three(work), three(work), over(const.valid), ALU.mult))
            dve.sem_inc(counted, 1)
            c.step(tt(second[:, :], second[:, :], first[:, :], ALU.subtract))
            c.step(tt(three(cand), three(logit), over(first), ALU.subtract))
            dve.sem_inc(asked_exp, 1)
            dve.wait_ge(exped, 2)
            if bias is None:
                c.step(dve.tensor_reduce(total[:, :], three(cand), AX_X, ALU.add))
                c.step(dve.reciprocal(total[:, :], total[:, :]))
                c.step(tt(second[:, :], second[:, :], total[:, :], ALU.mult))
                c.step(stt(out=first[:, :], in0=total[:, :], scalar=1e-9, in1=second[:, :], op0=ALU.add, op1=ALU.add))
                c.step(dve.reciprocal(first[:, :], first[:, :]))
                c.did(tt(self.gate[0][:, :], total[:, :], first[:, :], ALU.mult))
                c.step(tt(self.gate[1][:, :], second[:, :], first[:, :], ALU.mult))
            else:
                c.step(ts(first[:, :], second[:, :], 1.0, None, ALU.add))
                c.step(dve.reciprocal(self.gate[0][:, :], first[:, :]))
                c.step(tt(self.gate[1][:, :], second[:, :], self.gate[0][:, :], ALU.mult))
            dve.wait_ge(ranked, 2)
            c.did(dve.tensor_copy(pos[:, :], p_before[:, 0:W]))
            c.step(dve.tensor_copy(cand[:, :], p_total[:, 0:W]))
            for e in range(ne):
                c.did(dve.tensor_tensor_scan(three(ends)[:, :, e], const.ones[:, 0:NT], three(cand)[:, :, e], 0.0,
                                             ALU.mult, ALU.add))
            c.settle()
            c.did(ts(size[:, :], three(ends)[:, NT - 1, :], float(P - 1), None, ALU.add))
            c.step(tt(cand[:, :], ends[:, :], cand[:, :], ALU.subtract))
            c.did(tt(pos[:, :], pos[:, :], cand[:, :], ALU.add))
            c.step(dve.tensor_copy(size_i[:, :], size[:, :]))
            c.step(ts(size_i[:, :], size_i[:, :], 7, None, ALU.arith_shift_right))
            c.step(dve.tensor_copy(size[:, :], size_i[:, :]))
            c.step(dve.tensor_tensor_scan(base[:, :], const.ones[:, 0:ne], size[:, :], 0.0, ALU.mult, ALU.add))
            c.step(ts(mine[:, :], place[:, :], base[0:1, 0:1], None, ALU.is_ge))
            for e in range(1, ne - 1):
                c.step(stt(out=mine[:, :], in0=place[:, :], scalar=base[0:1, e:e + 1], in1=mine[:, :],
                           op0=ALU.is_ge, op1=ALU.add))
            c.did(dve.tensor_copy(self.expert[:, :], mine[:, :]))
            c.step(tt(base[:, :], base[:, :], size[:, :], ALU.subtract))
            c.step(ts(base[:, :], base[:, :], float(P), None, ALU.mult))
            c.step(tt(three(pos), three(pos), base[:, :].unsqueeze(1).to_broadcast([P, NT, ne]), ALU.add))
            c.step(ts(big[:, :], const.valid[:, :], -float(slots), float(slots), ALU.mult, ALU.add))
            for k in range(2):
                c.step(tt(cand[:, :], hot[k][:, :], pos[:, :], ALU.mult))
                c.step(dve.tensor_reduce(pick[:, :], three(cand), AX_X, ALU.add))
                c.step(tt(pick[:, :], pick[:, :], const.valid[:, :], ALU.mult))
                c.did(dve.tensor_copy(self.slot[k][:, :], pick[:, :]))
                c.step(tt(total[:, :], pick[:, :], big[:, :], ALU.add))
                c.step(dve.tensor_copy(scatter_i[k][:, :], total[:, :]))
            dve.sem_inc(slotted, 1)

        @block.scalar
        def _(act):
            for g in range(NG):
                if g > 1:
                    act.wait_ge(made, g - 1)
                act.wait_ge(turning, g + 1)
                act.copy(turned[g % 2][:, :], p_t[g % 2][:, 0:GT * D]).then_inc(kept, 1)
            act.wait_ge(asked_exp, 1)
            act.activation(second[:, :], second[:, :], ACT.Exp).then_inc(exped, 1)
            act.activation(cand[:, :], cand[:, :], ACT.Exp).then_inc(exped, 1)
            act.wait_ge(slotted, 1)

            def put(i, k, turn):
                act.wait_ge(scattered[k], turn * 32)
                for s in range(2):
                    act.copy(out_index[:, 2 * k + s:2 * k + s + 1], scatter_i[s][:, bass.ds(i, 1)]).then_inc(index_put, 1)
                act.wait_ge(index_put, 2 * (i + 1))
                act.copy(out_row[:, k * D:(k + 1) * D], at(XN, i * D, D)).then_inc(row_ready, 1)

            with act.Fori(0, NG) as g:
                for k in range(GT):
                    put(g * GT + k, k, g)

        @block.tensor
        def _(pe):
            pe.wait_ge(loaded, 16 if bias is None else 32)

            def turn(g):
                if g > 1:
                    pe.wait_ge(kept, g - 1)
                for q in range(2 * GT):
                    x = g * GT * D + q * P
                    mm = pe.transpose(p_t[g % 2][:, q * P:(q + 1) * P], XN[:, x:x + P], const.ident[:, :])
                mm.then_inc(turning, 1)

            turn(0)
            for g in range(NG):
                if g + 1 < NG:
                    turn(g + 1)
                pe.wait_ge(kept, g + 1)
                if g > 1:
                    pe.wait_ge(taken, g - 1)
                for n in range(GT):
                    for c in range(2):
                        mm = pe.matmul(p_l[g % 2][:, n * ne:(n + 1) * ne],
                                       turned[g % 2][:, n * D + c * P:n * D + (c + 1) * P],
                                       weight[:, c * ne:(c + 1) * ne], start=(c == 0), stop=(c == 1))
                mm.then_inc(made, 1)
            pe.wait_ge(counted, 1)
            pe.matmul(p_before[:, 0:W], const.before[:, :], work[:, :], start=True, stop=True).then_inc(ranked, 1)
            pe.matmul(p_total[:, 0:W], const.ones[:, :], work[:, :], start=True, stop=True).then_inc(ranked, 1)


H0 = 682
U0 = H0 // 2
HC = 6
HK = H0 // HC + 1
E0, E1, H1 = 8, 16, 512


def gated_experts(nc, const, routing, rows_in, rows_out, up, up_loaded, w2):
    with ExitStack() as ctx:
        m = Memory(nc, ctx, "ex0")
        down = m.sb("down", [P, E0 * HC * D])
        x, xT, y = (m.sb(n, [P, 2 * D]) for n in ("x", "xT", "y"))
        own_up = m.sb("own_up", [P, 4 * H0])
        gate_h, hT = m.sb("gate_h", [P, HC * P]), m.sb("hT", [P, 2 * HC * P])
        p_x, p_y1 = m.ps("p_x", [P, 512]), m.ps("p_y1", [P, 512])
        p_h = [m.ps(f"p_h{k}", [P, 2 * HC * P]) for k in range(2)]
        p_y = [p_h[0][:, 0:D], p_y1[:, 0:D]]
        loaded, x_turned, x_kept, up_copied, h_made, silued, h_ready, made, kept = (
            m.sem(n) for n in ("loaded", "x_turned", "x_kept", "up_copied", "h_made", "silued", "h_ready", "made", "kept"))
        x_loaded = [m.sem(f"x_loaded{k}") for k in range(2)]
        stored = [m.sem(f"stored{k}") for k in range(2)]
        block = ctx.enter_context(nc.Block())
        steps = routing.tiles // 2

        def expert(eng, r, k):
            return eng.value_load(routing.expert[0:1, bass.ds(r * 2 + k, 1)], min_val=0, max_val=E0 - 1)

        @block.sync
        def _(sp):
            def load(r):
                for k in range(2):
                    sp.wait_ge(x_turned, r + 1)
                    sp.dma_start(x[:, k * D:(k + 1) * D], rows_in[bass.ds((r * 2 + 2 + k) * P, P), :]).then_inc(x_loaded[k], 16)

            def store(r):
                for k in range(2):
                    sp.wait_ge(kept, r * 2 + k + 1)
                    sp.dma_start(rows_out[bass.ds((r * 2 + k) * P, P), :], y[:, k * D:(k + 1) * D]).then_inc(stored[k], 16)

            for k in range(2):
                sp.dma_start(x[:, k * D:(k + 1) * D], rows_in[k * P:(k + 1) * P, :]).then_inc(x_loaded[k], 16)
            for e in range(E0):
                sp.dma_start(down[0:HK, e * HC * D:(e + 1) * HC * D], w2[:, e * HC * D:(e + 1) * HC * D]).then_inc(loaded, 16)
            load(0)
            with sp.Fori(1, steps) as r:
                load(r)
                store(r - 1)
            store(steps - 1)
            for k in range(2):
                sp.wait_ge(stored[k], steps * 16)
                sp.wait_ge(x_loaded[k], (steps + 1) * 16)

        @block.tensor
        def _(pe):
            def turn_x(r):
                for k in range(2):
                    pe.wait_ge(x_loaded[k], r * 16 + 16)
                pe.wait_ge(x_kept, r)
                for q in range(4):
                    mm = pe.transpose(p_x[:, q * P:(q + 1) * P], x[:, q * P:(q + 1) * P], const.ident[:, :])
                mm.then_inc(x_turned, 1)

            turn_x(0)
            with pe.Fori(0, steps) as r:
                ex = []

                def hidden(k):
                    for w in range(2):
                        pe.wait_ge(up_copied, (r * 2 + k) * 2 + w + 1)
                        if w == 0:
                            pe.wait_ge(h_ready, r * 2)
                            if k == 0:
                                pe.wait_ge(kept, r * 2)
                        for q in range(HC):
                            n = min(HK, H0 - q * HK)
                            for c in range(2):
                                o = (w * 2 + c) * H0 + q * HK
                                mm = pe.matmul(p_h[k][0:n, (w * HC + q) * P:(w * HC + q + 1) * P], own_up[:, o:o + n],
                                               xT[:, k * D + c * P:k * D + (c + 1) * P], start=(c == 0), stop=(c == 1))
                        mm.then_inc(h_made, 1)

                def out(k):
                    pe.wait_ge(loaded, E0 * 16)
                    pe.wait_ge(h_ready, r * 2 + k + 1)
                    for q in range(HC):
                        n = min(HK, H0 - q * HK)
                        mm = pe.matmul(p_y[k], hT[0:n, (k * HC + q) * P:(k * HC + q + 1) * P],
                                       down[0:n, bass.ds(ex[k] * (HC * D) + q * D, D)], start=(q == 0), stop=(q == HC - 1))
                    mm.then_inc(made, 1)

                pe.wait_ge(x_kept, r + 1)
                hidden(0)
                ex += [expert(pe, r, k) for k in range(2)]
                hidden(1)
                turn_x(r + 1)
                out(0)
                out(1)

        @block.scalar
        def _(act):
            with act.Fori(0, steps) as r:
                for k in range(2):
                    act.wait_ge(h_made, (r * 2 + k + 1) * 2)
                    act.wait_ge(h_ready, r * 2 + k)
                    for n, a, b in ((HK, 0, HC - 1), (H0 - (HC - 1) * HK, HC - 1, HC)):
                        act.activation(gate_h[0:n, a * P:b * P], p_h[k][0:n, a * P:b * P], ACT.Silu).then_inc(silued, 1)

        @block.vector
        def _(dve):
            def keep_x(r):
                dve.wait_ge(x_turned, r + 1)
                dve.tensor_copy(xT[:, :], p_x[:, :]).then_inc(x_kept, 1)

            def copy_up(w, e):
                dve.tensor_copy(own_up[:, w * 2 * H0:(w + 1) * 2 * H0], at(up, e * (4 * H0) + w * 2 * H0, 2 * H0))\
                    .then_inc(up_copied, 1)

            def keep_y(r, k):
                dve.wait_ge(made, r * 2 + k + 1)
                dve.wait_ge(stored[k], r * 16)
                dve.tensor_copy(y[:, k * D:(k + 1) * D], p_y[k]).then_inc(kept, 1)

            dve.wait_ge(up_loaded, E0 * 16)
            e = expert(dve, 0, 0)
            for w in range(2):
                copy_up(w, e)
            keep_x(0)
            with dve.Fori(0, steps) as r:
                for k in range(2):
                    e = expert(dve, r, k + 1)
                    for w in range(2):
                        dve.wait_ge(h_made, (r * 2 + k) * 2 + w + 1)
                        copy_up(w, e)
                    dve.wait_ge(silued, (r * 2 + k + 1) * 2)
                    dve.wait_ge(made, r * 2)
                    for n, a, b in ((HK, 0, HC - 1), (H0 - (HC - 1) * HK, HC - 1, HC)):
                        ins = dve.tensor_tensor(hT[0:n, (k * HC + a) * P:(k * HC + b) * P], gate_h[0:n, a * P:b * P],
                                                p_h[k][0:n, (HC + a) * P:(HC + b) * P], ALU.mult)
                    ins.then_inc(h_ready, 1)
                keep_x(r + 1)
                for k in range(2):
                    keep_y(r, k)


def relu_experts(nc, const, routing, rows_in, rows_out, up, up_loaded, b1, down, down_loaded, b2):
    HQ = H1 // P
    with ExitStack() as ctx:
        m = Memory(nc, ctx, "ex1")
        up_b, down_b = m.sb("up_b", [P, E1 * HQ]), m.sb("down_b", [P, E1 * D])
        x, xT, y = (m.sb(n, [P, 2 * D]) for n in ("x", "xT", "y"))
        own_up, hT = ([m.sb(f"{n}{k}", [P, w]) for k in range(2)] for n, w in (("own_up", 2 * H1), ("hT", H1)))
        p_x = m.ps("p_x", [P, 512])
        p_h, p_y = ([m.ps(f"{n}{k}", [P, 512]) for k in range(2)] for n in ("p_h", "p_y"))
        loaded, x_turned, x_kept, up_copied, h_made, h_ready, made, kept = (
            m.sem(n) for n in ("loaded", "x_turned", "x_kept", "up_copied", "h_made", "h_ready", "made", "kept"))
        x_loaded = [m.sem(f"x_loaded{k}") for k in range(2)]
        stored = [m.sem(f"stored{k}") for k in range(2)]
        block = ctx.enter_context(nc.Block())
        steps = routing.tiles // 2

        def expert(eng, r, k):
            return eng.value_load(routing.expert[0:1, bass.ds(r * 2 + k, 1)], min_val=0, max_val=E1 - 1)

        @block.sync
        def _(sp):
            def load(r):
                for k in range(2):
                    sp.wait_ge(x_turned, r + 1)
                    sp.dma_start(x[:, k * D:(k + 1) * D], rows_in[bass.ds((r * 2 + 2 + k) * P, P), :]).then_inc(x_loaded[k], 16)

            def store(r):
                for k in range(2):
                    sp.wait_ge(kept, r * 2 + k + 1)
                    sp.dma_start(rows_out[bass.ds((r * 2 + k) * P, P), :], y[:, k * D:(k + 1) * D]).then_inc(stored[k], 16)

            for k in range(2):
                sp.dma_start(x[:, k * D:(k + 1) * D], rows_in[k * P:(k + 1) * P, :]).then_inc(x_loaded[k], 16)
            sp.dma_start(up_b[:, :], b1).then_inc(loaded, 16)
            sp.dma_start(down_b[:, :], row(b2)).then_inc(loaded, 16)
            load(0)
            with sp.Fori(1, steps) as r:
                load(r)
                store(r - 1)
            store(steps - 1)
            for k in range(2):
                sp.wait_ge(stored[k], steps * 16)
                sp.wait_ge(x_loaded[k], (steps + 1) * 16)

        @block.tensor
        def _(pe):
            def turn_x(r):
                for k in range(2):
                    pe.wait_ge(x_loaded[k], r * 16 + 16)
                pe.wait_ge(x_kept, r)
                for q in range(4):
                    mm = pe.transpose(p_x[:, q * P:(q + 1) * P], x[:, q * P:(q + 1) * P], const.ident[:, :])
                mm.then_inc(x_turned, 1)

            turn_x(0)
            with pe.Fori(0, steps) as r:
                ex = [expert(pe, r, k) for k in range(2)]

                def hidden(k):
                    pe.wait_ge(up_copied, r * 2 + k + 1)
                    pe.wait_ge(h_ready, r * 2)
                    for q in range(HQ):
                        for c in range(2):
                            mm = pe.matmul(p_h[k][:, q * P:(q + 1) * P], own_up[k][:, c * H1 + q * P:c * H1 + (q + 1) * P],
                                           xT[:, k * D + c * P:k * D + (c + 1) * P], start=(c == 0), stop=(c == 1))
                    mm.then_inc(h_made, 1)

                def out(k):
                    pe.wait_ge(down_loaded, E1 // 4 * 16)
                    pe.wait_ge(kept, r * 2)
                    pe.wait_ge(h_ready, r * 2 + k + 1)
                    for q in range(HQ):
                        mm = pe.matmul(p_y[k][:, 0:D], hT[k][:, q * P:(q + 1) * P],
                                       at(down, ex[k] * (HQ * D) + q * D, D), start=(q == 0), stop=(q == HQ - 1))
                    mm.then_inc(made, 1)

                pe.wait_ge(x_kept, r + 1)
                hidden(0)
                hidden(1)
                turn_x(r + 1)
                out(0)
                out(1)

        @block.scalar
        def _(act):
            def keep_x(r):
                act.wait_ge(x_turned, r + 1)
                act.copy(xT[:, :], p_x[:, :]).then_inc(x_kept, 1)

            def copy_up(r, k):
                act.copy(own_up[k][:, :], at(up, expert(act, r, k) * (2 * H1), 2 * H1)).then_inc(up_copied, 1)

            act.wait_ge(up_loaded, E1 // 4 * 16)
            for k in range(2):
                copy_up(0, k)
            keep_x(0)
            with act.Fori(0, steps) as r:
                for k in range(2):
                    act.wait_ge(h_made, r * 2 + k + 1)
                    copy_up(r + 1, k)
                keep_x(r + 1)

        @block.vector
        def _(dve):
            dve.wait_ge(loaded, 2 * 16)
            with dve.Fori(0, steps) as r:
                ex = [expert(dve, r, k) for k in range(2)]
                for k in range(2):
                    dve.wait_ge(h_made, r * 2 + k + 1)
                    dve.wait_ge(made, r * 2)
                    for q in range(HQ):
                        ins = dve.tensor_scalar(hT[k][:, q * P:(q + 1) * P], p_h[k][:, q * P:(q + 1) * P],
                                                at(up_b, ex[k] * HQ + q, 1), 0.0, ALU.add, ALU.max)
                    ins.then_inc(h_ready, 1)
                for k in range(2):
                    dve.wait_ge(made, r * 2 + k + 1)
                    dve.wait_ge(stored[k], r * 16)
                    dve.tensor_tensor(y[:, k * D:(k + 1) * D], p_y[k][:, 0:D], at(down_b, ex[k] * D, D), ALU.add)\
                        .then_inc(kept, 1)


def combine(nc, routing, rows, to, base=None):
    with ExitStack() as ctx:
        m = Memory(nc, ctx, "comb" if base is None else "comb1")
        index = m.sb("index", [P, 2 * GT], I32)
        got = m.sb("got", [P, 2 * GT * D])
        loaded, asked = m.sem("loaded"), m.sem("asked")
        indexed = m.sem("indexed")
        gathered = [m.sem(f"gathered{k}") for k in range(2 * GT)]
        taken = m.sem("taken")
        block = ctx.enter_context(nc.Block())

        @block.sync
        def _(sp):
            if base is not None:
                sp.dma_start(to[:, :].rearrange("p (i d) -> p i d", d=D), base.rearrange("(i p) d -> p i d", p=P))\
                    .then_inc(loaded, 16)

        @block.scalar
        def _(act):
            with act.Fori(0, NG) as g:
                for n in range(GT):
                    for s in range(2):
                        act.wait_ge(gathered[2 * n + s], g * 16)
                        act.copy(index[:, 2 * n + s:2 * n + s + 1], routing.slot[s][:, bass.ds(g * GT + n, 1)])\
                            .then_inc(indexed, 1)

        @block.gpsimd
        def _(pool):
            def gather(g, first=False):
                for n in range(GT):
                    for s in range(2):
                        k = 2 * n + s
                        pool.wait_ge(indexed, g * 2 * GT + k + 1)
                        if not first:
                            pool.wait_ge(taken, (g - 1) * 2 * GT + k + 1)
                        pool.sem_inc(asked, 1)
                        pool.indirect_dma_start(out=got[:, k * D:(k + 1) * D], out_offset=None, in_=rows,
                                                in_offset=bass.IndirectOffsetOnAxis(ap=index[:, k:k + 1], axis=0))\
                            .then_inc(gathered[k], 16)

            gather(0, first=True)
            with pool.Fori(1, NG) as g:
                gather(g)

        @block.vector
        def _(dve):
            if base is not None:
                dve.wait_ge(loaded, 16)
            with dve.Fori(0, NG) as g:
                for n in range(GT):
                    for s in range(2):
                        k = 2 * n + s
                        dve.wait_ge(gathered[k], g * 16 + 16)
                        dve.wait_ge(taken, g * 2 * GT + k)
                        y = at(to, (g * GT + n) * D, D)
                        dve.scalar_tensor_tensor(out=y, in0=got[:, k * D:(k + 1) * D],
                                                 scalar=routing.gate[s][:, bass.ds(g * GT + n, 1)], in1=y,
                                                 op0=ALU.mult, op1=ALU.add).then_inc(taken, 1)


def build(nc, a, out):
    def scratch(name, rows):
        return nc.dram_tensor(name, [rows, D], F32).ap()

    with ExitStack() as ctx:
        const = Constants(nc, ctx)
        m = Memory(nc, ctx, "main")
        X = m.sb("X", [P, NT * D])
        x_loaded = m.sem("x_loaded")
        start_nodes(nc, a["x"], X, x_loaded)
        norm_out, sumsq = m.sb("norm_out", [P, NT]), m.sb("sumsq", [P, NT])
        graph = ctx.enter_context(ExitStack())
        edges = Edges(nc, graph, const, a["src"], a["dst"], a["edge_weight"], a["src_rows"],
                      a["dst_rows"], a["weight_rows"], norm_out)
        table0, table1, base1 = scratch("table0", NPAD), scratch("table1", NPAD), scratch("base1", NPAD)
        tiles0, tiles1 = (-(-((2 * N + e * (P - 1)) // P) // 2) * 2 for e in (E0, E1))
        in0, in1 = scratch("in0", (tiles0 + 2) * P), scratch("in1", (tiles1 + 2) * P)
        out0, out1 = scratch("out0", tiles0 * P), scratch("out1", tiles1 * P)
        zeroed = [m.sem(f"zeroed{k}") for k in range(2)]
        start_clearing(nc, const, in0, zeroed[0])
        start_clearing(nc, const, in1, zeroed[1])

        with ExitStack() as part:
            p = Memory(nc, part, "layer0")
            XN = p.sb("XN", [P, NT * D])
            acc = p.sb("acc", [P, (NT + 1) * (D + DE + 1)])
            layer_norm(nc, "ln0", X, XN, table=table0, scale=norm_out, sumsq=sumsq, src_loaded=x_loaded)
            aggregate(nc, "agg0", edges, table0, acc, D + DE + 1, False, a["edge_rows"])
            scale, stats = p.sb("scale", [P, NT]), p.sb("stats", [P, CH0 * NG * 12])
            bn_scale, bn_shift = p.sb("bn_scale", [P, CH0]), p.sb("bn_shift", [P, CH0])
            YT = p.sb("YT", [P, CH0 * NPAD])
            map_scale(nc, sumsq, scale)
            qkv_channels(nc, const, XN, scale, a["m0_qkv"], YT, stats)
            batch_norm(nc, stats, a["m0_gamma"], a["m0_beta"], bn_scale, bn_shift)
            graph_and_mixer(nc, const, acc, X, YT, bn_scale, bn_shift, XN, sumsq, a["g0_w"], a["g0_b"],
                            a["m0_dw"], a["m0_pw"], a["m0_res"], a["m0_res_b"])
            add_mapped(nc, X, XN, sumsq)
        with ExitStack() as part:
            routing = Routing(nc, part, "route0", E0)
            routing.start_weights(nc, a["f0_router"], None)
            p = Memory(nc, part, "moe0")
            up, up_loaded = p.sb("up", [P, E0 * 4 * H0]), p.sem("up_loaded")
            start_loads(nc, [(up[:, e * 4 * H0:(e + 1) * 4 * H0], a["f0_w13"][:, e * 4 * H0:(e + 1) * 4 * H0])
                             for e in range(E0)], up_loaded)
            with ExitStack() as inner:
                XN = Memory(nc, inner, "moe0x").sb("XN", [P, NT * D])
                layer_norm(nc, "ln1", X, XN)
                routing.route(nc, const, XN, None, in0, zeroed[0])
            gated_experts(nc, const, routing, in0, out0, up, up_loaded, a["f0_w2"])
            combine(nc, routing, out0, X)
        with ExitStack() as part:
            p = Memory(nc, part, "layer1")
            XN = p.sb("XN", [P, NT * D])
            acc = p.sb("acc", [P, (NT + 1) * D])
            gw, kw = p.sb("gw", [P, 4 * D]), p.sb("kw", [P, 4 * D])
            w1, w2, weights_loaded = p.sb("w1", [P, 2 * FF]), p.sb("w2", [P, FF // P * D]), p.sem("weights_loaded")
            start_loads(nc, [(gw[:, :], a["g1_w"]), (kw[:, :], a["m1_kv"]), (w1[:, :], a["m1_w1"]), (w2[:, :], a["m1_w2"])],
                        weights_loaded)
            layer_norm(nc, "ln2", X, XN, table=table1)
            aggregate(nc, "agg1", edges, table1, acc, D, True)
            XNT, kv = p.sb("XNT", [P, 2 * NPAD]), p.sb("kv", [P, 2 * (P + 1)])
            graph_and_kv(nc, const, acc, X, XN, XNT, kv, gw, kw, weights_loaded, a["g1_b"], a["m1_kv_b"])
            attend(nc, const, XN, XNT, kv, a["m1_q"], a["m1_q_b"], a["m1_o"], a["m1_o_b"])
            layer_norm(nc, "ln3", XN, XN, a["m1_g1"], a["m1_n1"])
            feed_forward(nc, const, XN, w1, w2, weights_loaded, a["m1_b1"], a["m1_b2"])
            layer_norm(nc, "ln4", XN, X, a["m1_g2"], a["m1_n2"], add=X)
        graph.close()
        with ExitStack() as part:
            routing = Routing(nc, part, "route1", E1)
            routing.start_weights(nc, a["f1_router"], a["f1_router_b"])
            p = Memory(nc, part, "moe1")
            up, up_loaded = p.sb("up", [P, E1 * 2 * H1]), p.sem("up_loaded")
            start_loads(nc, [(up[:, e * 2 * H1:(e + 4) * 2 * H1], a["f1_w1"][:, e * 2 * H1:(e + 4) * 2 * H1])
                             for e in range(0, E1, 4)], up_loaded)
            down, down_loaded = p.sb("down", [P, E1 * 2 * H1]), p.sem("down_loaded")
            start_loads(nc, [(down[:, e * 2 * H1:(e + 4) * 2 * H1], a["f1_w2"][:, e * 2 * H1:(e + 4) * 2 * H1])
                             for e in range(0, E1, 4)], down_loaded)
            with ExitStack() as inner:
                XN = Memory(nc, inner, "moe1x").sb("XN", [P, NT * D])
                base_stored = p.sem("base_stored")
                layer_norm(nc, "ln5", X, XN, table=base1, table_stored=base_stored)
                routing.route(nc, const, XN, a["f1_router_b"], in1, zeroed[1], base_stored)
            relu_experts(nc, const, routing, in1, out1, up, up_loaded, a["f1_b1"], down, down_loaded, a["f1_b2"])
            Y = Memory(nc, part, "last").sb("Y", [P, NT * D])
            combine(nc, routing, out1, Y, base1)
            layer_norm(nc, "ln6", Y, X, a["f1_gamma"], a["f1_beta"], add=X, out=out)


def chunks(w):
    k, n = w.shape
    return w.reshape(k // P, P, n).transpose(1, 0, 2).reshape(P, -1)


def columns(v):
    return v.reshape(-1, P).T


def kernel(**inputs):
    import numpy as np
    import concourse.bacc as bacc
    from concourse.bass_utils import run_bass_kernel_spmd

    i = {k: np.asarray(v) for k, v in inputs.items()}

    def edge_columns(v, fill):
        return np.concatenate([v, np.full(EPAD - E, fill, v.dtype)]).reshape(ET, P).T

    def edge_tiles(v, fill):
        return np.concatenate([v, np.full(ECH * P * P - E, fill, v.dtype)]).reshape(ECH * P, P)

    spare = NPAD - 1
    a = {
        "x": i["x"],
        "src": edge_columns(i["src"], spare),
        "dst": edge_columns(i["dst"], spare),
        "edge_weight": edge_columns(i["edge_weight"], 0),
        "src_rows": edge_tiles(i["src"], spare),
        "dst_rows": edge_tiles(i["dst"], spare),
        "weight_rows": edge_tiles(i["edge_weight"], 0),
        "edge_rows": np.concatenate([i["edge_attr_64"], np.zeros((EPAD - E, DE), i["edge_attr_64"].dtype)]),
        "g0_w": i["L0_gnn_weight"], "g0_b": i["L0_gnn_bias"],
        "m0_qkv": chunks(i["L0_mix_w_qkv"][:, :, 2].T),
        "m0_gamma": columns(i["L0_mix_bn_gamma"]), "m0_beta": columns(i["L0_mix_bn_beta"]),
        "m0_dw": columns(i["L0_mix_w_dw"][:, 0, 2]),
        "m0_pw": i["L0_mix_w_pw"][:, :, 0].reshape(CH0, 4, 32, 32).transpose(1, 3, 0, 2).reshape(4, 32, -1),
        "m0_res": chunks(i["L0_mix_w_res"][:, :, 0].T), "m0_res_b": i["L0_mix_b_res"],
        "f0_router": chunks(i["L0_ffn_router_w"].T),
        "f0_w13": np.stack([i["L0_ffn_w1"], i["L0_ffn_w3"]]).reshape(2, E0, H0, 2, P).transpose(4, 1, 0, 3, 2).reshape(P, -1),
        "f0_w2": np.concatenate([i["L0_ffn_w2"].transpose(2, 0, 1), np.zeros((HC * HK - H0, E0, D), i["L0_ffn_w2"].dtype)])
                 .reshape(HC, HK, E0, D).transpose(1, 2, 0, 3).reshape(HK, -1),
        "g1_w": chunks(np.concatenate([i["L1_gnn_W1"].T, i["L1_gnn_W2"].T])),
        "g1_b": np.stack([i["L1_gnn_b1"], i["L1_gnn_b2"]]),
        "m1_kv": chunks(np.concatenate([i["L1_mix_Wk"], i["L1_mix_Wv"]], 1)),
        "m1_kv_b": np.concatenate([i["L1_mix_bk"], i["L1_mix_bv"]]),
        "m1_q": chunks(i["L1_mix_Wq"]), "m1_q_b": columns(i["L1_mix_bq"]),
        "m1_o": chunks(i["L1_mix_Wo"]), "m1_o_b": i["L1_mix_bo"],
        "m1_w1": chunks(i["L1_mix_W1"]), "m1_b1": columns(i["L1_mix_b1"]),
        "m1_w2": chunks(i["L1_mix_W2"]), "m1_b2": i["L1_mix_b2"],
        "m1_g1": i["L1_mix_ln1_g"], "m1_n1": i["L1_mix_ln1_b"],
        "m1_g2": i["L1_mix_ln2_g"], "m1_n2": i["L1_mix_ln2_b"],
        "f1_router": chunks(i["L1_ffn_gate_w"]), "f1_router_b": i["L1_ffn_gate_b"],
        "f1_w1": i["L1_ffn_w1"].reshape(E1, 2, P, H1).transpose(2, 0, 1, 3).reshape(P, -1),
        "f1_b1": i["L1_ffn_b1"].reshape(E1, H1 // P, P).transpose(2, 0, 1).reshape(P, -1),
        "f1_w2": i["L1_ffn_w2"].reshape(E1, H1 // P, P, D).transpose(2, 0, 1, 3).reshape(P, -1),
        "f1_b2": i["L1_ffn_b2"].reshape(-1),
        "f1_gamma": i["L1_ffn_gamma"], "f1_beta": i["L1_ffn_beta"],
    }
    a = {k: np.ascontiguousarray(v) for k, v in a.items()}
    nc = bacc.Bacc("TRN2", target_bir_lowering=False, num_devices=1)
    aps = {k: nc.dram_tensor(f"in_{k}", v.shape, mybir.dt.from_np(v.dtype), kind="ExternalInput").ap() for k, v in a.items()}
    out = nc.dram_tensor("out_0", (N, D), F32, kind="ExternalOutput").ap()
    build(nc, aps, out)
    r = run_bass_kernel_spmd(nc, [{f"in_{k}": v for k, v in a.items()}], core_ids=[0])
    return r.results[0]["out_0"]
```
